# Optimizing a Trainium2 kernel written in Bass

```python
import numpy as np
import jax
import jax.numpy as jnp

def _softmax(x, axis=-1):
    return jax.nn.softmax(x, axis=axis)
def _gelu(x):
    return jax.nn.gelu(x, approximate=True)
def _silu(x):
    return jax.nn.silu(x)
def _sigmoid(x):
    return jax.nn.sigmoid(x)
def _layernorm(x, axis=-1, eps=1e-5):
    m = jnp.mean(x, axis=axis, keepdims=True)
    v = jnp.var(x, axis=axis, keepdims=True)
    return (x - m) / jnp.sqrt(v + eps)
def _scatter_add(tgt, idx, src, axis=0):
    return tgt.at[idx].add(src)
def _segment_sum(src, seg, n):
    return jax.ops.segment_sum(src, seg, n)

kernel_name = 'mk_conv_attn_hybrid_d2_conv_nhwc128_0824fc'

def setup_inputs(seed: int = 0):
    np.random.seed(seed)
    _w = jnp.asarray
    def _rec_inputs():
        import jax
        import jax.numpy as jnp
        _gk = jax.random.key(seed)
        x = -0.0009896 + 1 * jax.random.normal(jax.random.fold_in(_gk, 1), (4, 56, 56, 128), jnp.float32)
        return x
    x = _rec_inputs()
    def _L0_conv_setup():
        import jax, jax.numpy as jnp
        import numpy as np
        DIM = 128
        NH = 4
        K = 7
        PAD = K // 2
        MLP_HID = 4 * DIM
        EPS = 1e-05

        def _layernorm(x, w, b):
            m = jnp.mean(x, axis=-1, keepdims=True)
            v = jnp.mean((x - m) ** 2, axis=-1, keepdims=True)
            return (x - m) / jnp.sqrt(v + EPS) * w + b

        def _windows(xp, H, W):
            return jnp.stack([xp[:, :, i:i + H, j:j + W, :] for i in range(K) for j in range(K)], axis=-1)

        def _nat_block(x, ln1_w, ln1_b, w_qkv, b_qkv, rpb, w_proj, b_proj, ln2_w, ln2_b, w_fc1, b_fc1, w_fc2, b_fc2):
            B, H, W, C = x.shape
            hd = C // NH
            scale = hd ** (-0.5)
            xn = _layernorm(x, ln1_w, ln1_b)
            qkv = xn @ w_qkv + b_qkv
            qkv = qkv.reshape(B, H, W, 3, NH, hd)
            qkv = jnp.transpose(qkv, (3, 0, 4, 1, 2, 5))
            q, k, v = (qkv[0] * scale, qkv[1], qkv[2])
            pad = ((0, 0), (0, 0), (PAD, PAD), (PAD, PAD), (0, 0))
            kp = jnp.pad(k, pad)
            vp = jnp.pad(v, pad)
            kw = _windows(kp, H, W)
            vw = _windows(vp, H, W)
            attn = jnp.einsum('bnhwd,bnhwdk->bnhwk', q, kw)
            attn = attn + rpb[None, :, None, None, :]
            attn = jax.nn.softmax(attn, axis=-1)
            out = jnp.einsum('bnhwk,bnhwdk->bnhwd', attn, vw)
            out = jnp.transpose(out, (0, 2, 3, 1, 4)).reshape(B, H, W, C)
            x = x + (out @ w_proj + b_proj)
            xn2 = _layernorm(x, ln2_w, ln2_b)
            h = jax.nn.gelu(xn2 @ w_fc1 + b_fc1, approximate=False)
            x = x + (h @ w_fc2 + b_fc2)
            return x
        key = jax.random.key(seed)
        ks = jax.random.split(key, 10)
        s = 0.02
        inp = {'x': jax.random.normal(ks[0], (4, 56, 56, DIM), dtype=jnp.float32), 'ln1_w': jnp.ones((DIM,), jnp.float32), 'ln1_b': jnp.zeros((DIM,), jnp.float32), 'w_qkv': jax.random.normal(ks[1], (DIM, 3 * DIM), jnp.float32) * s, 'b_qkv': jnp.zeros((3 * DIM,), jnp.float32), 'rpb': jax.random.normal(ks[2], (NH, K * K), jnp.float32) * s, 'w_proj': jax.random.normal(ks[3], (DIM, DIM), jnp.float32) * s, 'b_proj': jnp.zeros((DIM,), jnp.float32), 'ln2_w': jnp.ones((DIM,), jnp.float32), 'ln2_b': jnp.zeros((DIM,), jnp.float32), 'w_fc1': jax.random.normal(ks[4], (DIM, MLP_HID), jnp.float32) * s, 'b_fc1': jnp.zeros((MLP_HID,), jnp.float32), 'w_fc2': jax.random.normal(ks[5], (MLP_HID, DIM), jnp.float32) * s, 'b_fc2': jnp.zeros((DIM,), jnp.float32)}
        return inp
    _L0_conv_all = _L0_conv_setup()
    _L0_conv_in = {k: v for k, v in _L0_conv_all.items() if k in ('ln1_w', 'ln1_b', 'w_qkv', 'b_qkv', 'rpb', 'w_proj', 'b_proj', 'ln2_w', 'ln2_b', 'w_fc1', 'b_fc1', 'w_fc2', 'b_fc2', )}
    del _L0_conv_all

    def _L1_attn_setup():
        import jax, jax.numpy as jnp
        import numpy as np
        B, N, D = (4, 1024, 128)
        key = jax.random.key(seed)
        ks = jax.random.split(key, 4)
        scale = 1.0 / np.sqrt(D)
        return {'inputs': jax.random.normal(ks[0], (B, N, D), dtype=jnp.float32), 'Wq': jax.random.normal(ks[1], (D, D), dtype=jnp.float32) * scale, 'bq': jnp.zeros((D,), dtype=jnp.float32), 'Wk': jax.random.normal(ks[2], (D, D), dtype=jnp.float32) * scale, 'bk': jnp.zeros((D,), dtype=jnp.float32), 'Wv': jax.random.normal(ks[3], (D, D), dtype=jnp.float32) * scale, 'bv': jnp.zeros((D,), dtype=jnp.float32)}
    _L1_attn_all = _L1_attn_setup()
    _L1_attn_in = {k: v for k, v in _L1_attn_all.items() if k in ('Wq', 'bq', 'Wk', 'bk', 'Wv', 'bv', )}
    del _L1_attn_all

    def _L1_ffn_setup():
        import jax, jax.numpy as jnp
        import numpy as np
        PADDED_SL = 8192
        TEMPERATURE = 1.0
        SIGMA_POW = 0.25

        def _stu_conv(phi, u, n):
            b, sl, d = u.shape
            sgn = jnp.where(jnp.arange(sl) % 2 == 0, 1.0, -1.0).astype(u.dtype)
            sgn3 = sgn[None, :, None]
            Vf = jnp.fft.rfft(phi, n=n, axis=0)
            Uf_p = jnp.fft.rfft(u, n=n, axis=1)
            Uf_m = jnp.fft.rfft(u * sgn3, n=n, axis=1)
            U_plus = jnp.fft.irfft(Vf[None, :, :, None] * Uf_p[:, :, None, :], n=n, axis=1)[:, :sl]
            U_minus = jnp.fft.irfft(Vf[None, :, :, None] * Uf_m[:, :, None, :], n=n, axis=1)[:, :sl]
            U_minus = U_minus * sgn[None, :, None, None]
            return (U_plus, U_minus)

        def _compute_spectral(u, sigma, phi, Mpp, Mpm):
            U_plus, U_minus = _stu_conv(phi, u, PADDED_SL)
            s = sigma ** SIGMA_POW
            out = jnp.einsum('btkd,k,kde->bte', U_plus, s, Mpp)
            out = out + jnp.einsum('btkd,k,kde->bte', U_minus, s, Mpm)
            return out

        def _compute_ar_u(Mu, u):
            sl = u.shape[1]
            out = jnp.zeros(u.shape[:2] + (Mu.shape[-1],), dtype=u.dtype)
            for i in range(Mu.shape[0]):
                ui = jnp.pad(u, ((0, 0), (i, 0), (0, 0)))[:, :sl]
                out = out + jnp.einsum('btd,de->bte', ui, Mu[i])
            return out

        def _stu(u, sigma, phi, Mu, Mpp, Mpm):
            return _compute_spectral(u, sigma, phi, Mpp, Mpm) + _compute_ar_u(Mu, u)
        key = jax.random.key(seed)
        ks = jax.random.split(key, 8)
        b, sl, d, K, k_u = (2, 4096, 128, 16, 3)
        x = jax.random.normal(ks[0], (b, sl, d), dtype=jnp.float32)
        sigma = jax.random.uniform(ks[1], (K,), dtype=jnp.float32, minval=0.001, maxval=1.0)
        phi = jax.random.normal(ks[2], (sl, K), dtype=jnp.float32) / np.sqrt(sl)
        M_u = jax.random.normal(ks[3], (4, k_u, d, d), dtype=jnp.float32) * 0.02
        M_phi_plus = jax.random.normal(ks[4], (4, K, d, d), dtype=jnp.float32) * 0.02
        M_phi_minus = jax.random.normal(ks[5], (4, K, d, d), dtype=jnp.float32) * 0.02
        log_weights = jnp.ones((4,), dtype=jnp.float32)
        u01 = jax.random.uniform(ks[6], (4,), dtype=jnp.float32, minval=1e-06, maxval=1.0 - 1e-06)
        gumbel = -jnp.log(-jnp.log(u01))
        return {'x': x, 'sigma': sigma, 'phi': phi, 'M_u': M_u, 'M_phi_plus': M_phi_plus, 'M_phi_minus': M_phi_minus, 'log_weights': log_weights, 'gumbel': gumbel}
    _L1_ffn_all = _L1_ffn_setup()
    _L1_ffn_in = {k: v for k, v in _L1_ffn_all.items() if k in ('sigma', 'phi', 'M_u', 'M_phi_plus', 'M_phi_minus', 'log_weights', 'gumbel', )}
    del _L1_ffn_all

    return {
        "x": x,
        "L0_conv_ln1_w": _L0_conv_in["ln1_w"],
        "L0_conv_ln1_b": _L0_conv_in["ln1_b"],
        "L0_conv_w_qkv": _L0_conv_in["w_qkv"],
        "L0_conv_b_qkv": _L0_conv_in["b_qkv"],
        "L0_conv_rpb": _L0_conv_in["rpb"],
        "L0_conv_w_proj": _L0_conv_in["w_proj"],
        "L0_conv_b_proj": _L0_conv_in["b_proj"],
        "L0_conv_ln2_w": _L0_conv_in["ln2_w"],
        "L0_conv_ln2_b": _L0_conv_in["ln2_b"],
        "L0_conv_w_fc1": _L0_conv_in["w_fc1"],
        "L0_conv_b_fc1": _L0_conv_in["b_fc1"],
        "L0_conv_w_fc2": _L0_conv_in["w_fc2"],
        "L0_conv_b_fc2": _L0_conv_in["b_fc2"],
        "L1_attn_Wq": _L1_attn_in["Wq"],
        "L1_attn_bq": _L1_attn_in["bq"],
        "L1_attn_Wk": _L1_attn_in["Wk"],
        "L1_attn_bk": _L1_attn_in["bk"],
        "L1_attn_Wv": _L1_attn_in["Wv"],
        "L1_attn_bv": _L1_attn_in["bv"],
        "L1_ffn_sigma": _L1_ffn_in["sigma"],
        "L1_ffn_phi": _L1_ffn_in["phi"],
        "L1_ffn_M_u": _L1_ffn_in["M_u"],
        "L1_ffn_M_phi_plus": _L1_ffn_in["M_phi_plus"],
        "L1_ffn_M_phi_minus": _L1_ffn_in["M_phi_minus"],
        "L1_ffn_log_weights": _L1_ffn_in["log_weights"],
        "L1_ffn_gumbel": _L1_ffn_in["gumbel"],
    }

def reference(x, L0_conv_ln1_w, L0_conv_ln1_b, L0_conv_w_qkv, L0_conv_b_qkv, L0_conv_rpb, L0_conv_w_proj, L0_conv_b_proj, L0_conv_ln2_w, L0_conv_ln2_b, L0_conv_w_fc1, L0_conv_b_fc1, L0_conv_w_fc2, L0_conv_b_fc2, L1_attn_Wq, L1_attn_bq, L1_attn_Wk, L1_attn_bk, L1_attn_Wv, L1_attn_bv, L1_ffn_sigma, L1_ffn_phi, L1_ffn_M_u, L1_ffn_M_phi_plus, L1_ffn_M_phi_minus, L1_ffn_log_weights, L1_ffn_gumbel):
    import jax
    import jax.numpy as jnp
    def _L0_conv_ref(x, ln1_w, ln1_b, w_qkv, b_qkv, rpb, w_proj, b_proj, ln2_w, ln2_b, w_fc1, b_fc1, w_fc2, b_fc2):
        import jax, jax.numpy as jnp
        import numpy as np
        DIM = 128
        NH = 4
        K = 7
        PAD = K // 2
        MLP_HID = 4 * DIM
        EPS = 1e-05

        def _layernorm(x, w, b):
            m = jnp.mean(x, axis=-1, keepdims=True)
            v = jnp.mean((x - m) ** 2, axis=-1, keepdims=True)
            return (x - m) / jnp.sqrt(v + EPS) * w + b

        def _windows(xp, H, W):
            return jnp.stack([xp[:, :, i:i + H, j:j + W, :] for i in range(K) for j in range(K)], axis=-1)

        def _nat_block(x, ln1_w, ln1_b, w_qkv, b_qkv, rpb, w_proj, b_proj, ln2_w, ln2_b, w_fc1, b_fc1, w_fc2, b_fc2):
            B, H, W, C = x.shape
            hd = C // NH
            scale = hd ** (-0.5)
            xn = _layernorm(x, ln1_w, ln1_b)
            qkv = xn @ w_qkv + b_qkv
            qkv = qkv.reshape(B, H, W, 3, NH, hd)
            qkv = jnp.transpose(qkv, (3, 0, 4, 1, 2, 5))
            q, k, v = (qkv[0] * scale, qkv[1], qkv[2])
            pad = ((0, 0), (0, 0), (PAD, PAD), (PAD, PAD), (0, 0))
            kp = jnp.pad(k, pad)
            vp = jnp.pad(v, pad)
            kw = _windows(kp, H, W)
            vw = _windows(vp, H, W)
            attn = jnp.einsum('bnhwd,bnhwdk->bnhwk', q, kw)
            attn = attn + rpb[None, :, None, None, :]
            attn = jax.nn.softmax(attn, axis=-1)
            out = jnp.einsum('bnhwk,bnhwdk->bnhwd', attn, vw)
            out = jnp.transpose(out, (0, 2, 3, 1, 4)).reshape(B, H, W, C)
            x = x + (out @ w_proj + b_proj)
            xn2 = _layernorm(x, ln2_w, ln2_b)
            h = jax.nn.gelu(xn2 @ w_fc1 + b_fc1, approximate=False)
            x = x + (h @ w_fc2 + b_fc2)
            return x
        return _nat_block(x, ln1_w, ln1_b, w_qkv, b_qkv, rpb, w_proj, b_proj, ln2_w, ln2_b, w_fc1, b_fc1, w_fc2, b_fc2)

    def _L1_attn_ref(inputs, Wq, bq, Wk, bk, Wv, bv):
        import jax, jax.numpy as jnp
        import numpy as np
        B, N, D = (4, 1024, 128)
        q = inputs @ Wq + bq
        k = inputs @ Wk + bk
        v = inputs @ Wv + bv
        kv = jnp.sum(k * v, axis=1, keepdims=True)
        return q * kv

    def _L1_ffn_ref(x, sigma, phi, M_u, M_phi_plus, M_phi_minus, log_weights, gumbel):
        import jax, jax.numpy as jnp
        import numpy as np
        PADDED_SL = 8192
        TEMPERATURE = 1.0
        SIGMA_POW = 0.25

        def _stu_conv(phi, u, n):
            b, sl, d = u.shape
            sgn = jnp.where(jnp.arange(sl) % 2 == 0, 1.0, -1.0).astype(u.dtype)
            sgn3 = sgn[None, :, None]
            Vf = jnp.fft.rfft(phi, n=n, axis=0)
            Uf_p = jnp.fft.rfft(u, n=n, axis=1)
            Uf_m = jnp.fft.rfft(u * sgn3, n=n, axis=1)
            U_plus = jnp.fft.irfft(Vf[None, :, :, None] * Uf_p[:, :, None, :], n=n, axis=1)[:, :sl]
            U_minus = jnp.fft.irfft(Vf[None, :, :, None] * Uf_m[:, :, None, :], n=n, axis=1)[:, :sl]
            U_minus = U_minus * sgn[None, :, None, None]
            return (U_plus, U_minus)

        def _compute_spectral(u, sigma, phi, Mpp, Mpm):
            U_plus, U_minus = _stu_conv(phi, u, PADDED_SL)
            s = sigma ** SIGMA_POW
            out = jnp.einsum('btkd,k,kde->bte', U_plus, s, Mpp)
            out = out + jnp.einsum('btkd,k,kde->bte', U_minus, s, Mpm)
            return out

        def _compute_ar_u(Mu, u):
            sl = u.shape[1]
            out = jnp.zeros(u.shape[:2] + (Mu.shape[-1],), dtype=u.dtype)
            for i in range(Mu.shape[0]):
                ui = jnp.pad(u, ((0, 0), (i, 0), (0, 0)))[:, :sl]
                out = out + jnp.einsum('btd,de->bte', ui, Mu[i])
            return out

        def _stu(u, sigma, phi, Mu, Mpp, Mpm):
            return _compute_spectral(u, sigma, phi, Mpp, Mpm) + _compute_ar_u(Mu, u)
        T = x.shape[1]
        outs = []
        for i, frac in enumerate((1, 2, 4, 8)):
            xi = x[:, :T // frac]
            si = _stu(xi, sigma, phi, M_u[i], M_phi_plus[i], M_phi_minus[i])
            si = jnp.pad(si, ((0, 0), (0, T - si.shape[1]), (0, 0)))
            outs.append(si)
        y_soft = jax.nn.softmax((log_weights + gumbel) / TEMPERATURE)
        y_hard = jax.nn.one_hot(jnp.argmax(y_soft), 4, dtype=y_soft.dtype)
        weights = y_hard - jax.lax.stop_gradient(y_soft) + y_soft
        stacked = jnp.stack(outs, axis=-1)
        return jnp.sum(stacked * weights, axis=-1)

    def _gn(v, G=32, eps=1e-5):
        B_, H_, W_, C_ = v.shape
        g = v.reshape(B_, H_, W_, G, C_ // G)
        m = jnp.mean(g, axis=(1, 2, 4), keepdims=True)
        s = jnp.var(g, axis=(1, 2, 4), keepdims=True)
        return ((g - m) / jnp.sqrt(s + eps)).reshape(v.shape)

    def _ln_c(v, eps=1e-6):
        m = jnp.mean(v, axis=-1, keepdims=True)
        s = jnp.var(v, axis=-1, keepdims=True)
        return (v - m) / jnp.sqrt(s + eps)

    def _ln_t(v, eps=1e-5):
        m = jnp.mean(v, axis=-1, keepdims=True)
        s = jnp.var(v, axis=-1, keepdims=True)
        return (v - m) / jnp.sqrt(s + eps)

    def _to_tokens(v):
        B_, H_, W_, C_ = v.shape
        return v.reshape(B_, H_ * W_, C_)
    def _from_tokens(t, like):
        return t.reshape(like.shape)

    x = _L0_conv_ref(x, L0_conv_ln1_w, L0_conv_ln1_b, L0_conv_w_qkv, L0_conv_b_qkv, L0_conv_rpb, L0_conv_w_proj, L0_conv_b_proj, L0_conv_ln2_w, L0_conv_ln2_b, L0_conv_w_fc1, L0_conv_b_fc1, L0_conv_w_fc2, L0_conv_b_fc2)
    t = _to_tokens(x)
    t = t + _L1_attn_ref(_ln_t(t), L1_attn_Wq, L1_attn_bq, L1_attn_Wk, L1_attn_bk, L1_attn_Wv, L1_attn_bv)
    t = t + _L1_ffn_ref(_ln_t(t), L1_ffn_sigma, L1_ffn_phi, L1_ffn_M_u, L1_ffn_M_phi_plus, L1_ffn_M_phi_minus, L1_ffn_log_weights, L1_ffn_gumbel)
    x = _from_tokens(t, x)
    return x


_drawn_inputs = setup_inputs


def setup_inputs(seed=0):
    import zlib

    import numpy as np

    out = dict(_drawn_inputs(seed))
    spreads = {'L0_conv_ln1_w': (1.0, 0.6),
     'L0_conv_ln1_b': (0.0, 0.679),
     'L0_conv_b_qkv': (0.0, 0.1),
     'L0_conv_b_proj': (0.0, 0.1),
     'L0_conv_ln2_w': (1.0, 0.6),
     'L0_conv_ln2_b': (0.0, 0.57),
     'L0_conv_b_fc1': (0.0, 0.1),
     'L0_conv_b_fc2': (0.0, 0.1),
     'L1_attn_bq': (0.0, 0.1),
     'L1_attn_bk': (0.0, 0.1),
     'L1_attn_bv': (0.0, 0.1),
     'L1_ffn_log_weights': (1.0, 0.2)}
    factors = {'L0_conv_w_qkv': 3.679,
     'L0_conv_rpb': 36.163,
     'L1_ffn_sigma': 8.0,
     'L1_ffn_phi': 8.0,
     'L1_ffn_M_u': 43.466,
     'L1_ffn_M_phi_plus': 8.0,
     'L1_ffn_M_phi_minus': 8.0,
     'L1_ffn_gumbel': 8.0}
    for name, (base, spread) in spreads.items():
        noise = np.random.default_rng([zlib.crc32(name.encode()), seed]).standard_normal(out[name].shape)
        drawn = base * np.exp(spread * noise) if base else spread * noise
        out[name] = jnp.asarray(drawn.astype(out[name].dtype))
    for name, factor in factors.items():
        out[name] = (out[name] * factor).astype(out[name].dtype)
    return out
```

```python
import concourse.bass as bass
from concourse import mybir
from concourse.alu_op_type import AluOpType as ALU
from contextlib import ExitStack
import numpy as np

F32 = mybir.dt.float32
BF16 = mybir.dt.bfloat16
I32 = mybir.dt.int32
ACT = mybir.ActivationFunctionType
NB, T, C, NH, HD = 4, 3136, 128, 4, 32
G = 98
NJ = 8
PW = 62
EPS = 1e-5
SC = HD ** -0.5
BIG = 1.0e30
L, FC, NCH, SLOTS = 4, 28, 28, 784
TERMS = [(0, 0), (0, 1), (1, 0), (0, 2), (1, 1), (2, 0), (1, 2)]
KT = 16 * len(TERMS) + 6


class Queue:

    def __init__(self, eng):
        self.eng, self.seen, self.sem, self.n = eng, {}, None, 0

    def on(self, sem):
        self.sem, self.n = sem, 0

    def wait(self, *tokens):
        for t in tokens:
            if t is not None and self.seen.get(t[2], 0) < t[1]:
                self.seen[t[2]] = t[1]
                self.eng.wait_ge(t[0], t[1])

    def __call__(self, fn, *after, tick=True):
        self.wait(*after)
        ins = fn(self.eng)
        if tick:
            self.n += 1
            ins.then_inc(self.sem, 1)
            return (self.sem, self.n, self.sem.num)
        return None

    def last(self):
        return (self.sem, self.n, self.sem.num)

    def dma(self, line, fn, *after):
        self.wait(*after)
        line.n += 16
        fn(self.eng).then_inc(line.sem, 16)
        return (line.sem, line.n, line.sem.num)


class Line:

    def __init__(self, sem):
        self.sem, self.n = sem, 0

    def all(self):
        return (self.sem, self.n, self.sem.num)


class Ring:

    def __init__(self, bufs):
        self.bufs, self.free, self.i = bufs, [None] * len(bufs), -1

    def take(self):
        self.i = (self.i + 1) % len(self.bufs)
        free, self.free[self.i] = self.free[self.i], "in use"
        assert free != "in use", self.i
        return self.i, self.bufs[self.i], free


def program(nc, x, ln1_w, ln1_b, w_qkv, b_qkv, rpb, w_proj, b_proj, ln2_w, ln2_b, w_fc1, b_fc1, w_fc2, b_fc2,
            Wq, bq, Wk, bk, Wv, bv, sigma, phi, M_u, M_pp, M_pm, log_w, gumbel,
            c_id, c_fwd, c_vdft, c_tw, c_inv, c_ar, c_msk, c_rev, out):
    with ExitStack() as ctx:
        nsem = [0]

        def sem(tag="s"):
            nsem[0] += 1
            return ctx.enter_context(nc.semaphore(f"{tag}{nsem[0]}"))

        def line(tag="l"):
            return Line(sem(tag))

        pe, act, dve, pool, sp = (Queue(e) for e in (nc.tensor, nc.scalar, nc.vector, nc.gpsimd, nc.sync))
        for q, n in ((pe, "pe"), (act, "act"), (dve, "dve"), (pool, "pool")):
            q.on(sem(n))

        dr = lambda name, shape, dt=F32: nc.dram_tensor(name, shape, dt, kind="Internal").ap()
        Vd = dr("Vd", [NB, PW, PW, C])
        biasD = dr("biasD", [NH, 64, 196])
        T2 = dr("T2", [NB, SLOTS, 512])
        Un = dr("Un", [NB, SLOTS, 512])
        Ud = dr("Ud", [128, SLOTS * 32])
        Yd = dr("Yd", [SLOTS, 32, 256])
        Mbf = dr("Mbf", [2, 3, 16, 16384], BF16)
        MUd = dr("MUd", [3, 3, 16384], BF16)

        VbD = dr("VbD", [2, KT, NCH, 112], BF16)
        banks = ctx.enter_context(nc.psum_tensor("banks", [128, 8 * 512], F32))
        psum = [banks[:, 512 * i:512 * i + 512] for i in range(8)]
        wsel = ctx.enter_context(nc.sbuf_tensor("wsel", [128, 24], F32))

        def settle(*lines):
            ends = [q.last() for q in (pe, act, dve, pool)] + [ln.all() for ln in lines]
            for q in (pe, act, dve, pool, sp):
                q.wait(*ends)

        P = dict(nc=nc, ctx=ctx, line=line, pe=pe, act=act, dve=dve, pool=pool, sp=sp, banks=banks, psum=psum,
                 wsel=wsel, Vd=Vd, biasD=biasD, T2=T2, Un=Un, Ud=Ud, Yd=Yd, Mbf=Mbf, MUd=MUd, VbD=VbD,
                 x=x, ln1_w=ln1_w, ln1_b=ln1_b, w_qkv=w_qkv, b_qkv=b_qkv, rpb=rpb, w_proj=w_proj, b_proj=b_proj,
                 ln2_w=ln2_w, ln2_b=ln2_b, w_fc1=w_fc1, b_fc1=b_fc1, w_fc2=w_fc2, b_fc2=b_fc2,
                 Wq=Wq, bq=bq, Wk=Wk, bk=bk, Wv=Wv, bv=bv, sigma=sigma, phi=phi, M_u=M_u, M_pp=M_pp, M_pm=M_pm,
                 log_w=log_w, gumbel=gumbel, c_id=c_id, c_fwd=c_fwd, c_vdft=c_vdft, c_tw=c_tw, c_inv=c_inv,
                 c_ar=c_ar, c_msk=c_msk, c_rev=c_rev, out=out)
        phase_ab(P)
        settle(*P["ends_ab"])
        phase_prep(P)
        settle(*P["ends_prep"])
        phase_fwd(P)
        settle(*P["ends_fwd"])
        phase_freq(P)
        settle(*P["ends_freq"])
        phase_inv(P)


def phase_ab(P):
    nc, line = P["nc"], P["line"]
    pe, act, dve, pool, sp, psum = P["pe"], P["act"], P["dve"], P["pool"], P["sp"], P["psum"]
    Vd, biasD, T2, Un = P["Vd"], P["biasD"], P["T2"], P["Un"]
    with ExitStack() as c2:
        sb = lambda name, shape, dt=F32: c2.enter_context(nc.sbuf_tensor(name, shape, dt))
        XR = sb("XR", [G, NB * NJ, 512])
        qT = [sb(f"qT{i}", [128, T]) for i in range(2)]
        kP = [sb(f"kP{i}", [128, PW, PW]) for i in range(2)]
        oT = sb("oT", [128, T])
        Qs = [sb(f"Qs{i}", [128, 7, NH, 64]) for i in range(2)]
        XN = Ring([sb(f"XN{i}", [G, 4, 132]) for i in range(3)])
        XT = Ring([sb(f"XT{i}", [128, 392]) for i in range(2)])
        VS = Ring([sb(f"VS{i}", [G, 512]) for i in range(2)])
        hT = sb("hT", [128, 4, 392])
        VC = Ring([sb(f"VC{i}", [G, 2, 128]) for i in range(5)])
        SB = Ring([sb(f"SB{i}", [128, 2, 196]) for i in range(2)])
        PB = Ring([sb(f"PB{i}", [128, 2, 196]) for i in range(2)])
        PN = Ring([sb(f"PN{i}", [128, 2, 196]) for i in range(3)])
        PT = Ring([sb(f"PT{i}", [G, 512]) for i in range(2)])
        mx = Ring([sb(f"mx{i}", [128, 6]) for i in range(4)])
        st = Ring([sb(f"st{i}", [G, 4, 6]) for i in range(2)])
        mv = sb("mv", [G, NB * NJ, 4, 2])
        rs = sb("rs", [G, 4, NB * NJ, 4])
        nw = Ring([sb(f"nw{i}", [G, 4, 4]) for i in range(2)])
        ident = sb("ident", [128, 128])
        wqkv = sb("wqkv", [128, 384])
        wpr = sb("wpr", [128, 128])
        wf1 = sb("wf1", [128, 512])
        wf2 = sb("wf2", [128, 4, 128])
        wl1 = sb("wl1", [128, 3, 128])
        biasN = sb("biasN", [128, 2, 196])
        col = sb("col", [128, 16])
        rowb = sb("rowb", [128, 6, 128])
        kv = sb("kv", [128, 5, 128])
        zero = SB.bufs[0]

        ld, ldx = line("ld"), [line("ldx") for _ in range(NB)]
        cw = lambda a: a.rearrange("(p o) -> p o", o=1)
        for b in range(NB):
            sp.dma(ldx[b], lambda e, b=b: e.dma_start(XR[:, NJ * b:NJ * b + NJ, :], P["x"][b].rearrange(
                "(J r) w c -> (J r w c)", r=7).rearrange("(J j x) -> j J x", J=NJ, j=G)))
            if b == 0:
                sp.dma(ld, lambda e: e.dma_start(ident[:, :], P["c_id"]))
                for i, a in enumerate((P["ln1_w"], P["ln1_b"], P["b_qkv"][0:128], P["b_qkv"][128:256],
                                       P["ln2_w"], P["ln2_b"])):
                    sp.dma(ld, lambda e, i=i, a=a: e.dma_start(col[:, i:i + 1], cw(a)))
                for i in range(4):
                    sp.dma(ld, lambda e, i=i: e.dma_start(col[:, 6 + i:7 + i], cw(P["b_fc1"][128 * i:128 * i + 128])))
                sp.dma(ld, lambda e: e.dma_start(wqkv[:, :], P["w_qkv"]))
                for i, a in enumerate((P["b_qkv"][256:384], P["b_proj"], P["b_fc2"], P["bq"], P["bk"], P["bv"])):
                    sp.dma(ld, lambda e, i=i, a=a: e.dma_start(
                        rowb[:, i, :], a.rearrange("(o p) -> o p", o=1).broadcast_to([128, 128])))
                sp.dma(ld, lambda e: e.dma_start(wpr[:, :], P["w_proj"]))
                sp.dma(ld, lambda e: e.dma_start(wf1[:, :], P["w_fc1"]))
                sp.dma(ld, lambda e: e.dma_start(wf2[:, :, :], P["w_fc2"].rearrange("(i p) c -> p i c", p=128)))
                for i, a in enumerate((P["Wq"], P["Wk"], P["Wv"])):
                    sp.dma(ld, lambda e, i=i, a=a: e.dma_start(wl1[:, i, :], a))
        t_ld = ld.all()
        t_x = [l.all() for l in ldx]
        t_z = pool(lambda e: e.memset(biasN[:, :, :], BIG))
        t_z0 = pool(lambda e: e.memset(zero[:, :, :], 0.0))
        lb = line("lb")
        sp.dma(lb, lambda e: e.dma_start(biasD.rearrange("(a h) q k -> (h q) a k", a=2), biasN[:, :, :]), t_z)
        lz = line("lz")
        for b in range(NB):
            for rr in ((0, 3), (PW - 3, 3)):
                sp.dma(lz, lambda e, b=b, rr=rr: e.dma_start(
                    Vd[b, rr[0]:rr[0] + 3].rearrange("r w c -> (r w c)").rearrange("(p n) -> p n", p=93),
                    zero.rearrange("p a b -> p (a b)")[0:93, 0:256]), t_z0)
            for cc in (0, PW - 3):
                sp.dma(lz, lambda e, b=b, cc=cc: e.dma_start(
                    Vd[b, 3:PW - 3, cc:cc + 3, :].rearrange("r w c -> r (w c)"),
                    zero.rearrange("p a b -> p (a b)")[0:56, 0:384]), t_z0)
        lr = line("lr")
        t_b0 = lb.all()
        for h in range(NH):
            for qi in range(8):
                def f(e, h=h, qi=qi):
                    dst = bass.AP(biasD.tensor, h * 12544 + qi * 1582, [[197, 8], [14, 7], [1, 7]])
                    src = bass.AP(P["rpb"].tensor, h * 49, [[0, 8], [7, 7], [1, 7]])
                    return e.dma_start(dst, src)
                sp.dma(lr, f, t_b0)
        t_raw = sp.dma(lb, lambda e: e.dma_start(
            biasN[:, :, :], biasD.rearrange("(a h) q k -> (h q) a k", a=2)), lr.all())
        t_q0 = [pool(lambda e, i=i: e.memset(Qs[i][:, :, :, :], 0.0)) for i in range(2)]
        t_k0 = [pool(lambda e, i=i: e.memset(kP[i][:, :, :], 0.0)) for i in range(2)]
        t_o0 = None
        for i in range(3):
            t_o0 = pool(lambda e, i=i: e.memset(XN.bufs[i][:, :, 128:129], 1.0))
        ones = sb("ones", [128, 128])
        t_one = pool(lambda e: e.memset(ones[:, :], 1.0))
        t_m = pool(lambda e: e.tensor_scalar(PB.bufs[0][:, :, :], biasN[:, :, :], 0.5 * BIG, None, ALU.is_lt), t_raw)
        t_m = pool(lambda e: e.tensor_scalar(PB.bufs[0][:, :, :], PB.bufs[0][:, :, :], -2.0, 1.0, ALU.mult, ALU.add), t_m)
        t_bias = pool(lambda e: e.tensor_tensor(biasN[:, :, :], biasN[:, :, :], PB.bufs[0][:, :, :], ALU.mult), t_m)
        PB.free[0] = t_bias
        SB.free[0] = lz.all()
        t_c = pool(lambda e: e.tensor_scalar(col[:, 10:11], col[:, 2:3], -SC, None, ALU.mult), t_ld)
        gen = Ring(psum[0:2])
        psS, psT = Ring(psum[2:4]), Ring(psum[4:6])
        po, pC = psum[6], psum[7]

        def rstd(k, g, t_mv):
            i, w, fr = nw.take()
            v, y = w[:, 0, :], rs[:, k, g, :]
            t = pool(lambda e: e.tensor_scalar(v, mv[:, g, :, 1], EPS, None, ALU.add), t_mv, fr)
            t = dve(lambda e: e.tensor_scalar(w[:, 1, :].bitcast(I32), v.bitcast(I32), 1, None,
                                              ALU.arith_shift_right), t)
            t = dve(lambda e: e.tensor_scalar(y.bitcast(I32), w[:, 1, :].bitcast(I32), -1, 0x5f3759df,
                                              ALU.mult, ALU.add), t)
            for _ in range(4):
                t = pool(lambda e: e.tensor_tensor(w[:, 2, :], y, y, ALU.mult), t)
                t = pool(lambda e: e.tensor_tensor(w[:, 2, :], w[:, 2, :], v, ALU.mult), t)
                t = pool(lambda e: e.tensor_scalar(w[:, 2, :], w[:, 2, :], -0.5, 1.5, ALU.mult, ALU.add), t)
                t = pool(lambda e: e.tensor_tensor(y, y, w[:, 2, :], ALU.mult), t)
            nw.free[i] = t
            return t

        def stats(g, t_src):
            i, s, fr = st.take()
            for m in range(4):
                t = dve(lambda e, m=m: e.bn_stats(s[:, m, :], XR[:, g, 128 * m:128 * m + 128]), t_src, fr, tick=m == 3)
            for m in range(4):
                t2 = dve(lambda e, m=m: e.bn_aggr(mv[:, g, m, :], s[:, m, :]), t, mv_free[g], tick=m == 3)
            st.free[i] = t2
            return t2

        mv_free = [None] * (NB * NJ)

        def norm(k, g, t_r):
            i, n, fr = XN.take()
            for m in range(4):
                t = pool(lambda e, m=m: e.tensor_scalar(n[:, m, 0:128], XR[:, g, 128 * m:128 * m + 128],
                                                        mv[:, g, m, 0:1], rs[:, k, g, m:m + 1],
                                                        ALU.subtract, ALU.mult), t_r, fr, t_o0)
            mv_free[g] = t
            return i, n, t

        def transposed(n, t_n):
            i, p, fr = gen.take()
            for m in range(4):
                t = pe(lambda e, m=m: e.transpose(p[:, G * m:G * m + G], n[:, m, 0:128], ident[0:G, 0:G]),
                       t_n, fr, t_ld, tick=m == 3)
            return i, p, t

        q_free, k_free = [None, None], [None, None]
        q_done = {}
        v_done = {}
        lv = [line("lv") for _ in range(2)]
        t_x_cur = {}

        def qkv(b):
            for J in range(NJ):
                g = NJ * b + J
                t = stats(g, t_x[b])
                t = rstd(0, g, t)
                xi, n, t = norm(0, g, t)
                i, p, t = transposed(n, t)
                XN.free[xi] = t
                a, xt, fr = XT.take()
                t = act(lambda e: e.activation(xt.rearrange("c (j m) -> c m j", m=4),
                                               p[:, 0:392].rearrange("c (m j) -> c m j", m=4),
                                               ACT.Identity, bias=col[:, 1:2], scale=col[:, 0:1]), t, fr, t_ld)
                gen.free[i] = t
                yield
                i, p, fr = gen.take()
                t1 = pe(lambda e: e.matmul(p[:, 0:392], wqkv[:, 0:128], xt[:, :], start=True, stop=True), t, fr)
                t2 = act(lambda e: e.activation(qT[b % 2][:, 392 * J:392 * J + 392], p[:, 0:392], ACT.Identity,
                                                bias=col[:, 10:11], scale=-SC), t1, t_c, q_free[b % 2])
                gen.free[i] = t2
                i, p2, fr = gen.take()
                t1 = pe(lambda e: e.matmul(p2[:, 0:392], wqkv[:, 128:256], xt[:, :], start=True, stop=True), fr)
                t3 = dve(lambda e: e.tensor_scalar(kP[b % 2][:, 3 + 7 * J:10 + 7 * J, 3:59],
                                                   p2[:, 0:392].rearrange("c (r w) -> c r w", w=56),
                                                   col[:, 3:4], None, ALU.add), t1, t_k0[b % 2], k_free[b % 2])
                gen.free[i] = t3
                q_done[b, J] = (t2, t3)
                yield
                i, p3, fr = gen.take()
                xm = xt.rearrange("c (j m) -> c m j", m=4)
                for m in range(4):
                    t1 = pe(lambda e, m=m: e.matmul(p3[0:G, 128 * m:128 * m + 128], xm[:, m, :], wqkv[:, 256:384],
                                                    start=True, stop=True), fr, tick=m == 3)
                XT.free[a] = t1
                vi, vs, vf = VS.take()
                t4 = dve(lambda e: e.tensor_tensor(vs.rearrange("j (m c) -> j m c", m=4),
                                                   p3[0:G, :].rearrange("j (m c) -> j m c", m=4),
                                                   rowb[0:G, 0:1, :].broadcast_to([G, 4, 128]), ALU.add), t1, vf)
                gen.free[i] = t4
                ln = lv[vi]
                t5 = sp.dma(ln, lambda e: e.dma_start(
                    bass.AP(Vd.tensor, ((b * PW + 3 + 7 * J) * PW + 3) * C, [[PW * C, 7], [512, 14], [1, 512]]),
                    vs[:, :]), t4)
                VS.free[vi] = t5
                v_done[b, J] = t5
                yield

        lvc = [line("lvc") for _ in range(5)]
        o_free = [None] * NJ
        x2 = {}
        qs_free = [None, None]
        o_done = {}

        def nat(b, back):
            tiles = [(i, j) for i in range(7) for j in range(7)]
            hold, state = {}, {}

            def vload(n):
                if n >= len(tiles):
                    return
                i, jx = tiles[n]
                vi, vc, fr = VC.take()
                need = [v_done[b, J] for J in range(NJ)] if n == 0 else []
                for c in range(2):
                    t = sp.dma(lvc[vi], lambda e, c=c: e.dma_start(
                        vc[:, c, :], Vd[b, 8 * i + 7 * c:8 * i + 7 * c + 7, 8 * jx:8 * jx + 14, :]),
                        fr, lz.all(), *need)
                hold[n] = (vi, vc, t)

            for n in range(2):
                vload(n)
            for n in range(len(tiles) + 3):
                if n < len(tiles):
                    i, jx = tiles[n]
                    if jx == 0:
                        s = i % 2
                        src = qT[b % 2].rearrange("c (r w) -> c r w", w=56)[:, 8 * i:8 * i + 8, :].rearrange(
                            "c r (x w) -> c x r w", w=8)
                        for h in range(NH):
                            hs = slice(32 * h, 32 * h + 32)
                            t = pool(lambda e, h=h, hs=hs: e.tensor_copy(
                                Qs[s][hs, :, h, :].rearrange("c x (r w) -> c x r w", w=8), src[hs]),
                                pool.last(), t_q0[s], qs_free[s], *[q_done[b, min(7, (8 * i + d) // 7)][0] for d in (0, 7)])
                        pool.wait(t)
                        state["qs"] = t
                        if i == 6:
                            q_free[b % 2] = t
                    s = i % 2
                    si, S, fr = psS.take()
                    kr = [q_done[b, J][1] for J in range(NJ)] if n == 0 else []
                    for pr in range(2):
                        t = pe(lambda e, pr=pr: e.matmul(
                            S[:, 196 * pr:196 * pr + 196], Qs[s][:, jx, 2 * pr:2 * pr + 2, :],
                            kP[b % 2][:, 8 * i:8 * i + 14, 8 * jx:8 * jx + 14], start=True, stop=True),
                            fr, state["qs"], *kr, tick=pr == 1)
                    if jx == 6:
                        qs_free[s] = t
                    if n == len(tiles) - 1:
                        k_free[b % 2] = t
                    bi, sbf, f1 = SB.take()
                    mi, m_, f2 = mx.take()
                    for pr in range(2):
                        td = dve(lambda e, pr=pr: e.tensor_tensor_reduce(
                            out=sbf[:, pr, :], in0=S[:, 196 * pr:196 * pr + 196], in1=biasN[:, pr, :], scale=1.0,
                            scalar=3.0e38, op0=ALU.add, op1=ALU.min, accum_out=m_[:, pr:pr + 1]),
                            t, f1, f2, t_bias)
                    psS.free[si] = td
                    pi, pb, f3 = PB.take()
                    for pr in range(2):
                        ta = act(lambda e, pr=pr: e.activation(
                            pb[:, pr, :], sbf[:, pr, :], ACT.Exp, bias=m_[:, pr:pr + 1], scale=-1.0,
                            accum_out=m_[:, 2 + pr:3 + pr]), td, f3)
                    SB.free[bi] = ta
                    tr = dve(lambda e: e.reciprocal(m_[:, 4:6], m_[:, 2:4]), ta)
                    ni, pn, f4 = PN.take()
                    for pr in range(2):
                        tp = pool(lambda e, pr=pr: e.tensor_scalar(
                            pn[:, pr, :], pb[:, pr, :], m_[:, 4 + pr:5 + pr], None, ALU.mult), tr, f4)
                    PB.free[pi] = tp
                    mx.free[mi] = tp
                    hold[n] = hold[n] + (ni, pn, tp)
                if 0 <= n - 2 < len(tiles):
                    vi, vc, tv, ni, pn, tp = hold[n - 2]
                    ti, pt, fr = psT.take()
                    for c in range(2):
                        for pr in range(2):
                            t = pe(lambda e, c=c, pr=pr: e.transpose(
                                pt[0:G, 256 * c + 128 * pr:256 * c + 128 * pr + 128],
                                pn[:, pr, G * c:G * c + G], ident[:, :]), tp, fr, tick=(c, pr) == (1, 1))
                    PN.free[ni] = t
                    oi, ob, fo = PT.take()
                    if n % 2:
                        t = act(lambda e: e.activation(ob[:, :], pt[0:G, :], ACT.Copy), t, fo)
                    else:
                        t = dve(lambda e: e.tensor_copy(ob[:, :], pt[0:G, :]), t, fo)
                    psT.free[ti] = t
                    hold[n - 2] = (vi, vc, tv, oi, ob, t)
                if 0 <= n - 3 < len(tiles):
                    i, jx = tiles[n - 3]
                    vi, vc, tv, oi, ob, t = hold.pop(n - 3)
                    for h in range(NH):
                        for c in range(2):
                            t1 = pe(lambda e, h=h, c=c: e.matmul(
                                po[32 * h:32 * h + 32, 64 * jx:64 * jx + 64], vc[:, c, 32 * h:32 * h + 32],
                                ob[:, 256 * c + 64 * h:256 * c + 64 * h + 64], start=c == 0, stop=c == 1,
                                tile_position=(0, 32 * h)),
                                t, tv, state.get("po"), tick=(h, c) == (3, 1))
                    PT.free[oi] = t1
                    VC.free[vi] = t1
                    if jx == 6:
                        fr = [o_free[J] for J in range(NJ) if 7 * J < 8 * i + 8 and 7 * J + 7 > 8 * i]
                        t = act(lambda e, i=i: e.activation(
                            oT.rearrange("c (r w) -> c r w", w=56)[:, 8 * i:8 * i + 8, :].rearrange(
                                "c r (x w) -> c x r w", w=8),
                            po[:, 0:448].rearrange("c (x r w) -> c x r w", r=8, w=8), ACT.Copy), t1, *fr)
                        state["po"] = t
                        o_done[b, i] = t
                        for J in [i] if i < 6 else [6, 7]:
                            back.append(mlp(b, J))
                        if i == 6:
                            back.append(attn(b))
                vload(n + 2)
                for _ in range(2):
                    step(back)

        def step(back):
            while back:
                try:
                    next(back[0])
                    return True
                except StopIteration:
                    back.pop(0)
            return False

        h_free = [None] * 4

        def add_rows(k, g, after):
            return pool(lambda e: e.tensor_tensor(
                XR[:, g, :].rearrange("j (m c) -> j m c", m=4), XR[:, g, :].rearrange("j (m c) -> j m c", m=4),
                rowb[0:G, k:k + 1, :].broadcast_to([G, 4, 128]), ALU.add), *after)

        def mlp(b, J):
            g = NJ * b + J
            ta = add_rows(1, g, [t_x[b], t_ld])
            i, p, fr = gen.take()
            om = oT[:, 392 * J:392 * J + 392].rearrange("c (j m) -> c m j", m=4)
            for m in range(4):
                t = pe(lambda e, m=m: e.matmul(p[0:G, 128 * m:128 * m + 128], om[:, m, :], wpr[:, :],
                                               start=True, stop=True), fr, o_done[b, min(J, 6)], tick=m == 3)
            o_free[J] = t
            t = dve(lambda e: e.tensor_tensor(XR[:, g, :], XR[:, g, :], p[0:G, :], ALU.add), t, ta)
            gen.free[i] = t
            t = stats(g, t)
            t = rstd(1, g, t)
            xi, n, t = norm(1, g, t)
            ta = add_rows(2, g, [t])
            yield
            i, p, t = transposed(n, t)
            XN.free[xi] = t
            a, xt, fr = XT.take()
            t = act(lambda e: e.activation(xt[:, :], p[:, 0:392], ACT.Identity, bias=col[:, 5:6],
                                           scale=col[:, 4:5]), t, fr, t_ld)
            gen.free[i] = t
            yield
            th = []
            for f in range(4):
                i, p, fr = gen.take()
                t1 = pe(lambda e, f=f, p=p: e.matmul(p[:, 0:392], wf1[:, 128 * f:128 * f + 128], xt[:, :],
                                                     start=True, stop=True), t, fr)
                t2 = act(lambda e, f=f, p=p: e.activation(hT[:, f, :], p[:, 0:392], ACT.Gelu,
                                                          bias=col[:, 6 + f:7 + f]), t1, h_free[f])
                gen.free[i] = t2
                th.append(t2)
            XT.free[a] = t1
            yield
            i, p, fr = gen.take()
            for m in range(4):
                for f in range(4):
                    t = pe(lambda e, m=m, f=f: e.matmul(p[0:G, 128 * m:128 * m + 128], hT[:, f, G * m:G * m + G],
                                                        wf2[:, f, :], start=f == 0, stop=f == 3),
                           fr, th[f], tick=(m, f) == (3, 3))
            for f in range(4):
                h_free[f] = t
            t = dve(lambda e: e.tensor_tensor(XR[:, g, :], XR[:, g, :], p[0:G, :], ALU.add), t, ta)
            gen.free[i] = t
            yield
            t = stats(g, t)
            t = rstd(2, g, t)
            xi, n, t = norm(2, g, t)
            yield
            for m in range(4):
                t = pe(lambda e, m=m: e.matmul(pC[:, 0:129], n[:, m, 0:128], n[:, m, 0:129],
                                               start=(J, m) == (0, 0), stop=(J, m) == (NJ - 1, 3)),
                       t, c_free[0], tick=m == 3)
            XN.free[xi] = t
            x2[g] = t
            yield

        c_free = [None]
        kv_free = [None]
        lst = [line("lst") for _ in range(3)]

        def attn(b):
            tc = x2[NJ * b + NJ - 1]
            Cs, S1 = kv[:, 0, :], kv[:, 4, 0:1]
            t = act(lambda e: e.activation(Cs, pC[:, 0:128], ACT.Copy), tc, kv_free[0])
            t = act(lambda e: e.activation(S1, pC[:, 128:129], ACT.Copy), tc, kv_free[0])
            c_free[0] = t
            ts = pool(lambda e: e.tensor_scalar(kv[:, 1, :], ones[:, :], S1, None, ALU.mult), t, t_one)
            i, p, fr = gen.take()
            t1 = pe(lambda e: e.matmul(p[:, 0:128], Cs, wl1[:, 2, :], start=True, stop=True), t, fr)
            t1 = pe(lambda e: e.matmul(p[:, 128:256], kv[:, 1, :], wl1[:, 2, :], start=True, stop=True), ts)
            t2 = dve(lambda e: e.scalar_tensor_tensor(kv[:, 2, :], rowb[:, 5, :], S1, p[:, 0:128],
                                                      ALU.mult, ALU.add), t1, kv_free[0])
            t2 = dve(lambda e: e.tensor_tensor(kv[:, 2, :], kv[:, 2, :], wl1[:, 1, :], ALU.mult), t2)
            t3 = dve(lambda e: e.scalar_tensor_tensor(kv[:, 3, :], rowb[:, 5, :], float(T), p[:, 128:256],
                                                      ALU.mult, ALU.add), t1)
            t3 = dve(lambda e: e.tensor_tensor(kv[:, 3, :], kv[:, 3, :], rowb[:, 4, :], ALU.mult), t3)
            gen.free[i] = t3
            yield
            i, p, fr = gen.take()
            t = pe(lambda e: e.matmul(p[:, 0:128], ones[:, :], kv[:, 2, :], start=True, stop=True), t2, fr)
            t = dve(lambda e: e.tensor_tensor(kv[:, 3, :], kv[:, 3, :], p[:, 0:128], ALU.add), t, t3)
            gen.free[i] = t
            tw = dve(lambda e: e.tensor_tensor(kv[:, 2, :], kv[:, 3, :], wl1[:, 0, :], ALU.mult), t)
            tb = dve(lambda e: e.tensor_tensor(kv[:, 4, :], kv[:, 3, :], rowb[:, 3, :], ALU.mult), t)
            yield
            for J in range(NJ):
                g = NJ * b + J
                xi, n, t = norm(2, g, x2[g])
                ta = pool(lambda e: e.tensor_tensor(
                    XR[:, g, :].rearrange("j (m c) -> j m c", m=4), XR[:, g, :].rearrange("j (m c) -> j m c", m=4),
                    kv[0:G, 4:5, :].broadcast_to([G, 4, 128]), ALU.add), t, tb)
                i, p, t = transposed(n, t)
                XN.free[xi] = t
                a, xt, fr = XT.take()
                t = act(lambda e: e.activation(xt[:, :], p[:, 0:392], ACT.Copy), t, fr)
                gen.free[i] = t
                yield
                i, p, fr = gen.take()
                for m in range(4):
                    t = pe(lambda e, m=m: e.matmul(p[0:G, 128 * m:128 * m + 128], xt[:, G * m:G * m + G], kv[:, 2, :],
                                                   start=True, stop=True), fr, t, tw, tick=m == 3)
                XT.free[a] = t
                kv_free[0] = t
                t = dve(lambda e: e.tensor_tensor(XR[:, g, :], XR[:, g, :], p[0:G, :], ALU.add), t, ta)
                gen.free[i] = t
                sp.dma(P["lt2"], lambda e: e.dma_start(T2[b, G * J:G * J + G, :], XR[:, g, :]), t)
                t = stats(g, t)
                t = rstd(3, g, t)
                xi, n, t = norm(3, g, t)
                t = sp.dma(lst[xi], lambda e: e.dma_start(
                    Un[b, G * J:G * J + G, :].rearrange("j (m c) -> j m c", m=4), n[:, :, 0:128]), t)
                XN.free[xi] = t
                yield

        P["lt2"] = line("lt2")
        for _ in qkv(0):
            pass
        back = []
        for b in range(NB):
            if b + 1 < NB:
                back.append(qkv(b + 1))
            nat(b, back)
            while b + 1 < NB and (b + 1, NJ - 1) not in v_done:
                step(back)
        while step(back):
            pass
        P["ends_ab"] = [P["lt2"]] + lst + lv
        P["t_ab"] = [P["lt2"].all()] + [l.all() for l in lst] + [l.all() for l in lv]


def phase_prep(P):
    nc, line = P["nc"], P["line"]
    pe, act, dve, pool, sp, psum = P["pe"], P["act"], P["dve"], P["pool"], P["sp"], P["psum"]
    w = P["wsel"]
    with ExitStack() as c2:
        sb = lambda name, shape, dt=F32: c2.enter_context(nc.sbuf_tensor(name, shape, dt))
        lg = sb("lg", [128, 8])
        mk = sb("mk", [128, 4, 8])
        tm = sb("tm", [128, 24])
        ph = sb("ph", [G, 8, 4, 32])
        vd = sb("vd", [G, 8, 1568])
        vf = sb("vf", [128, 1568])
        vp = [sb(f"vp{i}", [128, 1568], BF16) for i in range(3)]
        sg = sb("sg", [128, 4])
        ML = Ring([sb(f"ML{i}", [128, 2048]) for i in range(3)])
        mp, mm = sb("mp", [128, 2048]), sb("mm", [128, 2048])
        mo = Ring([sb(f"mo{i}", [128, 2048], BF16) for i in range(3)])
        la, lp, lst = line("la"), line("lp"), line("lst")
        bc = lambda a: a.rearrange("(o p) -> o p", o=1).broadcast_to([128, 4])
        sp.dma(la, lambda e: e.dma_start(lg[:, 0:4], bc(P["log_w"])))
        sp.dma(la, lambda e: e.dma_start(lg[:, 4:8], bc(P["gumbel"])))
        t = sp.dma(la, lambda e: e.dma_start(mk[:, :, :], P["c_msk"].rearrange("(o i) j -> o i j", o=1)
                                             .broadcast_to([128, 4, 8])))
        t_s1 = pool(lambda e: e.memset(sg[:, :], 1.0))
        t_p0 = pool(lambda e: e.memset(ph[:, :, :, :], 0.0))
        for q in range(4):
            sp.dma(lp, lambda e, q=q: e.dma_start(sg[32 * q:32 * q + 16, 0:1],
                                                  P["sigma"].rearrange("(p o) -> p o", o=1)), t_s1)
        phv = P["phi"][0:3136].rearrange("(a j m) k -> j a m k", j=G, m=4)
        for a in range(8):
            sp.dma(lp, lambda e, a=a: e.dma_start(ph[:, a, :, 0:16], phv[:, a]), t_p0)
        sp.dma(lp, lambda e: e.dma_start(vd[:, :, :], P["c_vdft"]))
        t_ph = lp.all()
        z, y, eq, h = tm[:, 0:4], tm[:, 4:8], tm[:, 8:12], tm[:, 12:16]
        t = dve(lambda e: e.tensor_tensor(z, lg[:, 0:4], lg[:, 4:8], ALU.add), t)
        t = dve(lambda e: e.reduce_max(tm[:, 16:17], z, mybir.AxisListType.X), t)
        t = dve(lambda e: e.tensor_scalar(z, z, tm[:, 16:17], None, ALU.subtract), t)
        t = act(lambda e: e.activation(y, z, ACT.Exp, accum_out=tm[:, 17:18]), t)
        t = dve(lambda e: e.reciprocal(tm[:, 18:19], tm[:, 17:18]), t)
        t = dve(lambda e: e.tensor_scalar(y, y, tm[:, 18:19], None, ALU.mult), t)
        t = dve(lambda e: e.reduce_max(tm[:, 16:17], y, mybir.AxisListType.X), t)
        t = dve(lambda e: e.tensor_scalar(eq, y, tm[:, 16:17], None, ALU.is_ge), t)
        t = dve(lambda e: e.memset(tm[:, 20:21], 1.0), t)
        for i in range(4):
            t = dve(lambda e, i=i: e.tensor_tensor(h[:, i:i + 1], eq[:, i:i + 1], tm[:, 20:21], ALU.mult), t)
            t = dve(lambda e, i=i: e.tensor_tensor(tm[:, 20:21], tm[:, 20:21], h[:, i:i + 1], ALU.subtract), t)
        t = dve(lambda e: e.tensor_tensor(w[:, 0:4], h, y, ALU.subtract), t)
        t_w = dve(lambda e: e.tensor_tensor(w[:, 0:4], w[:, 0:4], y, ALU.add), t)
        t = dve(lambda e: e.tensor_scalar(w[:, 8:16], mk[:, 0, :], h[:, 0:1], None, ALU.mult), t_w)
        for i in range(1, 4):
            t = dve(lambda e, i=i: e.scalar_tensor_tensor(w[:, 8:16], mk[:, i, :], h[:, i:i + 1], w[:, 8:16],
                                                          ALU.mult, ALU.add), t)
        for i in range(2):
            s, r = sg[:, i:i + 1], sg[:, i + 1:i + 2]
            t = act(lambda e: e.activation(r, s, ACT.Sqrt), t_ph, dve.last())
            t = dve(lambda e: e.tensor_scalar(sg[:, 3:4], r, 1e-30, None, ALU.max), t)
            t = dve(lambda e: e.reciprocal(sg[:, 3:4], sg[:, 3:4]), t)
            t = dve(lambda e: e.tensor_tensor(sg[:, 3:4], sg[:, 3:4], s, ALU.mult), t)
            t = dve(lambda e: e.tensor_tensor(r, r, sg[:, 3:4], ALU.add), t)
            t = dve(lambda e: e.tensor_scalar(r, r, 0.5, None, ALU.mult), t)
        for i in range(4):
            for a in range(8):
                t1 = pe(lambda e, a=a: e.matmul(psum[i][:, 0:392], ph[:, a, :, :], vd[:, a, 392 * i:392 * i + 392],
                                                start=a == 0, stop=a == 7), t_ph, tick=a == 7)
            tv = act(lambda e: e.activation(vf[:, 392 * i:392 * i + 392], psum[i][:, 0:392], ACT.Copy,
                                            scale=sg[:, 2:3]), t1, t)
        tv = dve(lambda e: e.tensor_copy(vp[0][:, :], vf[:, :]), tv)
        for i in (1, 2):
            tv = dve(lambda e: e.tensor_tensor(vf[:, :], vf[:, :], vp[i - 1][:, :], ALU.subtract), tv)
            tv = dve(lambda e: e.tensor_copy(vp[i][:, :], vf[:, :]), tv)
        for k, (_, v) in enumerate(TERMS):
            for q in range(4):
                sp.dma(lst, lambda e, k=k, v=v, q=q: e.dma_start(
                    P["VbD"][q % 2, 16 * k:16 * k + 16, :, 56 * (q // 2):56 * (q // 2) + 56],
                    vp[v][32 * q:32 * q + 16, :].rearrange("k (c x) -> k c x", c=NCH)), tv)
        lc = line("lc")
        for p in range(2):
            pool.dma(lc, lambda e, p=p: e.dma_start(P["VbD"][p, 112:118], P["c_ar"][p]))

        lm = [line("lm") for _ in range(3)]
        lo = [line("lo") for _ in range(3)]
        free = [None, None]

        def split(src, n, t, dst):
            for i in range(3):
                oi, o, fr = mo.take()
                t1 = act(lambda e: e.activation(o[:, 0:n], src[:, 0:n], ACT.Copy), t, fr)
                mo.free[oi] = sp.dma(lo[oi], lambda e, i=i: e.dma_start(dst(i), o[:, 0:n]), t1)
                t = dve(lambda e: e.tensor_tensor(src[:, 0:n], src[:, 0:n], o[:, 0:n], ALU.subtract), t1) if i < 2 else t1
            return t

        def mixed(dst, n, view, t_free):
            for i in range(4):
                li, m, fr = ML.take()
                t = sp.dma(lm[li], lambda e, i=i: e.dma_start(m[:, 0:n], view(i)), fr)
                if i == 0:
                    t = dve(lambda e: e.tensor_scalar(dst[:, 0:n], m[:, 0:n], w[:, 0:1], None, ALU.mult), t, t_w, t_free)
                else:
                    t = dve(lambda e, i=i: e.scalar_tensor_tensor(dst[:, 0:n], m[:, 0:n], w[:, i:i + 1], dst[:, 0:n],
                                                                  ALU.mult, ALU.add), t, dve.last())
                ML.free[li] = t
            return t

        big = lambda a: (lambda i: a[i].rearrange("k d e -> (k d e)").rearrange("(p x) -> p x", p=128))
        mixed(mp, 2048, big(P["M_pp"]), None)
        t = mixed(mm, 2048, big(P["M_pm"]), None)
        dif = sb("dif", [128, 2048])
        t1 = dve(lambda e: e.tensor_tensor(dif[:, :], mp[:, :], mm[:, :], ALU.subtract), t)
        t2 = dve(lambda e: e.tensor_tensor(mp[:, :], mp[:, :], mm[:, :], ALU.add), t1)
        for par, (s, t) in enumerate(((mp, t2), (dif, t1))):
            split(s, 2048, t, lambda i, par=par: P["Mbf"][par, i].rearrange("k x -> (k x)").rearrange(
                "(p x) -> p x", p=128))
        t = mixed(mm, 384, lambda i: P["M_u"][i].rearrange("k d e -> (k d e)").rearrange("(p x) -> p x", p=128), t2)
        split(mm, 384, t, lambda i: P["MUd"][i].rearrange("k x -> (k x)").rearrange("(p x) -> p x", p=128))
        P["ends_prep"] = [lst, lc] + lo


def phase_fwd(P):
    nc, line = P["nc"], P["line"]
    pe, act, dve, pool, sp, psum = P["pe"], P["act"], P["dve"], P["pool"], P["sp"], P["psum"]
    Un = P["Un"]
    with ExitStack() as c2:
        sb = lambda name, shape, dt=F32: c2.enter_context(nc.sbuf_tensor(name, shape, dt))
        U = sb("U", [128, SLOTS, 4, 2, 4])
        F = sb("F", [G, 2, 4, 784])
        UA = Ring([sb(f"UA{i}", [G, 4, 512]) for i in range(2)])
        UR = Ring([sb(f"UR{i}", [G, 4, 512]) for i in range(2)])
        EO = [Ring([sb(f"E{c}{i}", [G, 4, 512]) for i in range(2)]) for c in range(2)]
        lf, lu = line("lf"), [line("lu") for _ in range(2)]
        rev = sb("rev", [G, G])
        sp.dma(lf, lambda e: e.dma_start(rev[:, :], P["c_rev"]))
        tf = sp.dma(lf, lambda e: e.dma_start(F[:, :, :, :], P["c_fwd"]))
        bank = Ring(psum)
        n = 0
        for b in range(NB):
            i, ua, fr = UA.take()
            i, ur, fr2 = UR.take()
            sp.dma(lu[i], lambda e: e.dma_start(ua[:, :, :], Un[b, 0:392].rearrange("(a p) x -> p a x", p=G)), fr, fr2)
            t = sp.dma(lu[i], lambda e: e.dma_start(ur[:, :, :], Un[b, 392:784].rearrange(
                "(a p) x -> p a x", p=G)))
            ei, ev, fr = EO[0].take()
            oi, od, fr2 = EO[1].take()
            for a in range(4):
                pi, p, fp = bank.take()
                tp = pe(lambda e: e.matmul(p[0:G, :], rev[:, :], ur[:, 3 - a, :], start=True, stop=True), t, fp, tf)
                t0 = dve(lambda e: e.tensor_tensor(ev[:, a, :], ua[:, a, :], p[0:G, :], ALU.add), tp, t, fr)
                t1 = dve(lambda e: e.tensor_tensor(od[:, a, :], ua[:, a, :], p[0:G, :], ALU.subtract), fr2)
                bank.free[pi] = t1
            UA.free[i], UR.free[i] = t1, tp
            for m in range(4):
                for c, (src, ts) in enumerate(((ev, t0), (od, t1))):
                    for half in range(2):
                        pi, p, fr = bank.take()
                        for a in range(4):
                            tp = pe(lambda e, a=a: e.matmul(p[:, 0:392], src[:, a, 128 * m:128 * m + 128],
                                                            F[:, c, a, 392 * half:392 * half + 392],
                                                            start=a == 0, stop=a == 3), ts, fr, tf, tick=a == 3)
                        lo = 392 * (c ^ half)
                        dst = U[:, lo:lo + 392, m, half, b]
                        n += 1
                        if n % 2:
                            bank.free[pi] = act(lambda e: e.activation(dst, p[:, 0:392], ACT.Copy), tp)
                        else:
                            bank.free[pi] = dve(lambda e: e.tensor_copy(dst, p[:, 0:392]), tp)
            EO[0].free[ei], EO[1].free[oi] = tp, tp
        lo_ = line("lou")
        sp.wait(act.last(), dve.last())
        for k in range(4):
            sl = slice(196 * 32 * k, 196 * 32 * k + 196 * 32)
            sp.dma(lo_, lambda e: e.dma_start(P["Ud"][:, sl], U.rearrange("d s m r b -> d (s m r b)")[:, sl]))
        P["ends_fwd"] = [lo_]


def phase_freq(P):
    nc, line = P["nc"], P["line"]
    pe, act, dve, pool, sp = P["pe"], P["act"], P["dve"], P["pool"], P["sp"]
    banks, psum, Yd = P["banks"], P["psum"], P["Yd"]
    with ExitStack() as c2:
        sb = lambda name, shape, dt=F32: c2.enter_context(nc.sbuf_tensor(name, shape, dt))
        M = sb("M", [KT, 2, 16384], BF16)
        Gm = sb("Gm", [128, 2, 112, 128])
        VS = Ring([sb(f"V{i}", [KT, 2, 112], BF16) for i in range(2)])
        TW = Ring([sb(f"TW{i}", [128, 3, FC]) for i in range(2)])
        UL = Ring([sb(f"UL{i}", [128, FC, 32]) for i in range(1)])
        U7 = Ring([sb(f"U7{i}", [128, FC, 56]) for i in range(2)])
        tmp = sb("tmp", [128, FC, 3, 4])
        YS = Ring([sb(f"YS{i}", [128, 7, 256]) for i in range(1)])
        lm = line("lm2")
        for par in range(2):
            for k, (m, _) in enumerate(TERMS):
                sp.dma(lm, lambda e: e.dma_start(M[16 * k:16 * k + 16, par, :], P["Mbf"][par, m]))
            for r, tap in ((112, par), (115, 2)):
                sp.dma(lm, lambda e: e.dma_start(M[r:r + 3, par, :], P["MUd"][:, tap, :]))
        t_m = lm.all()
        lv, lw, ll = [line("lvq") for _ in range(2)], [line("ltw") for _ in range(2)], line("lul")
        ly = line("ly")
        tiles = Ring([banks[:, 1024 * i:1024 * i + 1024] for i in range(3)])
        yb = Ring(psum[6:8])
        ready = {}

        def load(ch):
            vi, v, fv = VS.take()
            tv = sp.dma(lv[vi], lambda e: e.dma_start(v[:, :, :], P["VbD"][:, :, ch, :].rearrange("a k x -> k a x")), fv)
            wi, w, fw = TW.take()
            tw = sp.dma(lw[wi], lambda e: e.dma_start(
                w[:, :, :], P["c_tw"][:, FC * ch:FC * ch + FC].rearrange("(o a) s -> o a s", o=1).broadcast_to([128, 3, FC])), fw)
            li, u, fl = UL.take()
            tu = sp.dma(ll, lambda e: e.dma_start(u.rearrange("d s x -> d (s x)"),
                                                  P["Ud"][:, FC * 32 * ch:FC * 32 * ch + FC * 32]), fl)
            ui, u7, fu = U7.take()
            a = u7.rearrange("d s (m r b) -> d s m r b", m=7, r=2)
            s4 = u.rearrange("d s (m r b) -> d s m r b", m=4, r=2)
            t = pool(lambda e: e.tensor_copy(u7[:, :, 24:56], u[:, :, :]), tu, fu)
            cc = [w[:, k, :].rearrange("d (s o) -> d s o", o=1).broadcast_to([128, FC, 4]) for k in range(3)]
            for m in range(3):
                R, I = s4[:, :, m + 1, 0, :], s4[:, :, m + 1, 1, :]
                x = tmp[:, :, m, :]
                t = pool(lambda e: e.tensor_tensor(x, I, cc[1], ALU.mult), tw, pool.last())
                t = pool(lambda e: e.tensor_tensor(a[:, :, m, 0, :], R, cc[0], ALU.mult))
                t = pool(lambda e: e.tensor_tensor(a[:, :, m, 0, :], a[:, :, m, 0, :], x, ALU.add), t)
                t = pool(lambda e: e.tensor_tensor(x, R, cc[1], ALU.mult), t)
                t = pool(lambda e: e.tensor_tensor(a[:, :, m, 1, :], I, cc[2], ALU.mult))
                t = pool(lambda e: e.tensor_tensor(a[:, :, m, 1, :], a[:, :, m, 1, :], x, ALU.subtract), t)
            UL.free[li], TW.free[wi] = t, t
            ready[ch] = (vi, v, tv, ui, u7, t)

        load(0)
        t_y, n = None, 0
        for ch in range(NCH):
            vi, v, tv, ui, u7, tu = ready.pop(ch)
            ends = [None, None]
            for eg in range(16):
                for par in range(2):
                    ti, pt, fr = tiles.take()
                    for k in range(8):
                        ec = 8 * eg + k
                        tp = pe(lambda e: e.matmul(pt[:, 128 * k:128 * k + 112],
                                                   M.rearrange("r a (d e) -> r a e d", e=128)[:, par, ec, :],
                                                   v[:, par, :], start=True, stop=True), fr, t_m, tv, tick=k == 7)
                    src = pt.rearrange("d (e x) -> d x e", x=128)[:, 0:112, :]
                    dst = Gm[:, par, :, 8 * eg:8 * eg + 8]
                    n += 1
                    if n % 2:
                        t = act(lambda e: e.activation(dst, src, ACT.Copy), tp, t_y)
                    else:
                        t = dve(lambda e: e.tensor_copy(dst, src), tp, t_y)
                    ends[n % 2] = t
                    tiles.free[ti] = t
            VS.free[vi] = tp
            if ch + 1 < NCH:
                load(ch + 1)
            yi, ys, fy = YS.take()
            for gp in range(7):
                if gp % 2 == 0:
                    bi, pb, fr = yb.take()
                for q in range(4):
                    for s in range(4):
                        sl = 4 * gp + s
                        r = ((q // 2) * FC + sl) * 2
                        tp = pe(lambda e: e.matmul(pb[32 * s:32 * s + 32, 256 * (gp % 2):256 * (gp % 2) + 256],
                                                   u7[:, sl, 8 * (3 - q):8 * (3 - q) + 32],
                                                   Gm[:, q % 2, r:r + 2, :], start=q == 0, stop=q == 3,
                                                   tile_position=(0, 32 * s)),
                                fr, tu, *ends, tick=(q, s) == (3, 3))
                if gp % 2 or gp == 6:
                    g0 = gp - gp % 2
                    wd = 256 * (gp - g0 + 1)
                    f = (lambda e: e.tensor_copy(ys[:, g0:gp + 1, :], pb[:, 0:wd].rearrange("p (a x) -> p a x", x=256)))
                    te = dve(f, tp, fy)
                    yb.free[bi] = te
            U7.free[ui] = tp
            t_y = tp
            for s in range(4):
                dst = Yd[FC * ch:FC * ch + FC].rearrange("(g s) r x -> s r g x", s=4)[s]
                t = sp.dma(ly, lambda e: e.dma_start(dst, ys[32 * s:32 * s + 32, :, :]), te)
            YS.free[yi] = t
        P["ends_freq"] = [ly]


def phase_inv(P):
    nc, line = P["nc"], P["line"]
    pe, act, dve, pool, sp, psum = P["pe"], P["act"], P["dve"], P["pool"], P["sp"], P["psum"]
    Yd, T2, w = P["Yd"], P["T2"], P["wsel"]
    out = P["out"].rearrange("b h w c -> b (h w c)").rearrange("b (j x) -> b j x", x=512)
    with ExitStack() as c2:
        sb = lambda name, shape, dt=F32: c2.enter_context(nc.sbuf_tensor(name, shape, dt))
        IV = sb("IV", [G, 2, 8, 392])
        YL = Ring([sb(f"YL{i}", [G, 8, 2, 2, 256]) for i in range(2)])
        YC = Ring([sb(f"YC{i}", [G, 2, 8, 2, 128]) for i in range(2)])
        RN = Ring([sb(f"RN{i}", [G, 2, 4, 256]) for i in range(2)])
        S2 = Ring([sb(f"S2{i}", [G, 256]) for i in range(2)])
        TT = Ring([sb(f"TT{i}", [G, 2, 256]) for i in range(2)])
        lf = line("lf3")
        rev = sb("rev3", [G, G])
        sp.dma(lf, lambda e: e.dma_start(rev[:, :], P["c_rev"]))
        tf = sp.dma(lf, lambda e: e.dma_start(IV[:, :, :, :], P["c_inv"]))
        ll, lr, lo = [line("ll") for _ in range(2)], [line("lr") for _ in range(2)], [line("lo3") for _ in range(2)]
        bank = Ring(psum)
        work = [(b, pp) for b in range(NB) for pp in range(2)]
        got = {}
        rows = lambda b, k, pp, A: A[b, 392 * k:392 * k + 392, 256 * pp:256 * pp + 256].rearrange("(a p) x -> p a x", p=G)

        def load(n):
            if n >= len(work):
                return
            b, pp = work[n]
            i, yl, fr = YL.take()
            for a in range(8):
                src = Yd[G * a:G * a + G].rearrange("s (p r b) x -> s b p r x", r=2, b=4)[:, b, 2 * pp:2 * pp + 2]
                t = sp.dma(ll[i], lambda e: e.dma_start(yl[:, a], src), fr)
            j, rn, fr = RN.take()
            for k in range(2):
                t2 = sp.dma(lr[j], lambda e: e.dma_start(rn[:, k], rows(b, k, pp, T2)), fr)
            got[n] = (i, yl, t, j, rn, t2)

        load(0)
        for n, (b, pp) in enumerate(work):
            load(n + 1)
            i, yl, t, j, rn, t2 = got.pop(n)
            ci, yc, fr = YC.take()
            ta = dve(lambda e: e.tensor_tensor(yc[:, 0], yl[:, :, :, 0, 0:128], yl[:, :, :, 1, 128:256], ALU.subtract), t, fr)
            tb = pool(lambda e: e.tensor_tensor(yc[:, 1], yl[:, :, :, 0, 128:256], yl[:, :, :, 1, 0:128], ALU.add), t, fr)
            ta = dve(lambda e: e.tensor_copy(yc[0:1, 0, 0], yl[0:1, 0, :, 0, 0:128]), ta, tb)
            tb = dve(lambda e: e.tensor_copy(yc[0:1, 1, 0], yl[0:1, 0, :, 1, 128:256]), tb)
            YL.free[i] = tb
            for jt in range(4):
                pi, p, fr = bank.take()
                for c in range(2):
                    for a in range(8):
                        k = (a >= 4) ^ c
                        tp = pe(lambda e: e.matmul(p[0:G, 256 * c:256 * c + 256], IV[:, c, a, G * jt:G * jt + G],
                                                   yc[:, int(k), a], start=a == 0, stop=a == 7),
                                fr, ta, tb, tf, tick=a == 7)
                si, s2, fr = S2.take()
                t = act(lambda e: e.activation(s2[:, :], p[0:G, 256:512], ACT.Copy), tp, fr)
                xi, tt, fr = TT.take()
                t1 = dve(lambda e: e.tensor_tensor(tt[:, 0], p[0:G, 0:256], s2[:, :], ALU.add), t, fr)
                t3 = dve(lambda e: e.tensor_tensor(tt[:, 1], p[0:G, 0:256], s2[:, :], ALU.subtract), t)
                bank.free[pi], S2.free[si] = t3, t3
                dve(lambda e: e.scalar_tensor_tensor(rn[:, 0, jt], tt[:, 0], w[0:G, 8 + jt:9 + jt], rn[:, 0, jt],
                                                     ALU.mult, ALU.add), t1, t2)
                pi, p, fr = bank.take()
                t = pe(lambda e: e.matmul(p[0:G, 0:256], rev[:, :], tt[:, 1], start=True, stop=True), t3, fr)
                TT.free[xi] = t
                t = dve(lambda e: e.scalar_tensor_tensor(rn[:, 1, 3 - jt], p[0:G, 0:256], w[0:G, 15 - jt:16 - jt],
                                                         rn[:, 1, 3 - jt], ALU.mult, ALU.add), t)
                bank.free[pi] = t
            YC.free[ci] = tp
            for k in range(2):
                to = sp.dma(lo[j], lambda e: e.dma_start(rows(b, k, pp, out), rn[:, k]), t)
            RN.free[j] = to
        sp.wait(*[l.all() for l in lo])


def tables():
    NP_, J = 1568, 784
    even = np.arange(0, 784, 2)
    odd = np.arange(1, 784, 2)
    slots = np.concatenate([even, odd])
    j = np.arange(392)[:, None] + 0.5
    th = lambda a, f: 2 * np.pi * a * f / NP_
    fe, fo = even[None, :].astype(float), odd[None, :].astype(float)
    fi = fe.copy()
    fi[0, 0] = 784.0
    Fe = np.concatenate([np.cos(th(j, fe)), -np.sin(th(j, fo))], 1)
    Fo = np.concatenate([np.cos(th(j, fo)), -np.sin(th(j, fi))], 1)
    fwd = np.stack([Fe, Fo], 0).reshape(2, 4, 98, 784).transpose(2, 0, 1, 3)
    jj = np.arange(784)[:, None].astype(float)
    fs = slots[None, :].astype(float)
    V = np.empty((784, 784, 2))
    V[:, :, 0] = np.cos(th(jj, fs))
    V[:, :, 1] = -np.sin(th(jj, fs))
    V[:, 0, 1] = np.cos(th(jj[:, 0], 784.0))
    vdft = V.reshape(8, 98, 1568).transpose(1, 0, 2)
    tc, ts = np.cos(th(1.0, slots)), np.sin(th(1.0, slots))
    tci = tc.copy()
    tci[0] = -1.0
    tw = np.stack([tc, ts, tci])
    w = np.full(784, 2.0)
    w[0] = 1.0
    jr = np.arange(392)[None, :] + 0.5
    ev, od = slots[:392, None].astype(float), slots[392:, None].astype(float)
    wc = w[:392, None] / NP_
    evi = ev.copy()
    evi[0, 0] = 784.0
    C1 = np.concatenate([wc * np.cos(th(jr, ev)), -2.0 / NP_ * np.sin(th(jr, od))])
    C2 = np.concatenate([-wc * np.sin(th(jr, evi)), 2.0 / NP_ * np.cos(th(jr, od))])
    inv = np.stack([C1, C2], 0).reshape(2, 8, 98, 392).transpose(2, 0, 1, 3)
    f = lambda a: np.ascontiguousarray(a, dtype=np.float32)
    return f(fwd), f(vdft), f(tw), f(inv)


def shape_constants():
    fwd, vdft, tw, inv = tables()
    ar = np.zeros((2, 6, NCH, 2, FC, 2), np.float32)
    ar[:, 0:3, :, 0, :, 0] = 1
    ar[:, 0:3, 0, 0, 0, 1] = 1
    ar[0, 3:6, :, 1, :, 0] = 1
    ar[0, 3:6, 0, 1, 0, 1] = 1
    msk = np.array([[1.0 if J < 8 >> i else 0.0 for J in range(8)] for i in range(4)], np.float32)
    return {"c_id": np.eye(128, dtype=np.float32), "c_fwd": fwd, "c_vdft": vdft, "c_tw": tw, "c_inv": inv,
            "c_ar": ar.reshape(2, 6, NCH, 112), "c_msk": msk, "c_rev": np.eye(G, dtype=np.float32)[::-1]}


_INS = ['x', 'L0_conv_ln1_w', 'L0_conv_ln1_b', 'L0_conv_w_qkv', 'L0_conv_b_qkv', 'L0_conv_rpb', 'L0_conv_w_proj', 'L0_conv_b_proj', 'L0_conv_ln2_w', 'L0_conv_ln2_b', 'L0_conv_w_fc1', 'L0_conv_b_fc1', 'L0_conv_w_fc2', 'L0_conv_b_fc2', 'L1_attn_Wq', 'L1_attn_bq', 'L1_attn_Wk', 'L1_attn_bk', 'L1_attn_Wv', 'L1_attn_bv', 'L1_ffn_sigma', 'L1_ffn_phi', 'L1_ffn_M_u', 'L1_ffn_M_phi_plus', 'L1_ffn_M_phi_minus', 'L1_ffn_log_weights', 'L1_ffn_gumbel']


def kernel(**inputs):
    import numpy as _np
    import concourse.bacc as _bacc
    from concourse import mybir as _mybir
    from concourse.bass_utils import run_bass_kernel_spmd as _run

    nc = _bacc.Bacc("TRN2", target_bir_lowering=False, num_devices=1)
    arrays, args = {}, []
    consts = shape_constants()
    for name, a in [(n, inputs[n]) for n in _INS] + list(consts.items()):
        a = _np.ascontiguousarray(a)
        arrays[f"in_{name}_dram"] = a
        args.append(nc.dram_tensor(f"in_{name}_dram", a.shape, _mybir.dt.from_np(a.dtype), kind="ExternalInput").ap())
    args.append(nc.dram_tensor("out_0_dram", (4, 56, 56, 128), _mybir.dt.float32, kind="ExternalOutput").ap())
    program(nc, *args)
    r = _run(nc, [arrays], core_ids=[0])
    return r.results[0]["out_0_dram"]
```

```python
import concourse.bass as bass
from concourse import mybir
from concourse.alu_op_type import AluOpType as ALU
from contextlib import ExitStack
import numpy as np

F32 = mybir.dt.float32
BF16 = mybir.dt.bfloat16
I32 = mybir.dt.int32
ACT = mybir.ActivationFunctionType
NB, T, C, NH, HD = 4, 3136, 128, 4, 32
G = 98
NJ = 8
PW = 62
EPS = 1e-5
SC = HD ** -0.5
BIG = 1.0e30
L, FC, NCH, SLOTS = 4, 28, 28, 784
TERMS = [(0, 0), (0, 1), (1, 0), (0, 2), (1, 1), (2, 0), (1, 2)]
KT = 16 * len(TERMS) + 6


class Queue:

    def __init__(self, eng):
        self.eng, self.seen, self.sem, self.n = eng, {}, None, 0

    def on(self, sem):
        self.sem, self.n = sem, 0

    def wait(self, *tokens):
        for t in tokens:
            if t is not None and self.seen.get(t[2], 0) < t[1]:
                self.seen[t[2]] = t[1]
                self.eng.wait_ge(t[0], t[1])

    def __call__(self, fn, *after, tick=True):
        self.wait(*after)
        ins = fn(self.eng)
        if tick:
            self.n += 1
            ins.then_inc(self.sem, 1)
            return (self.sem, self.n, self.sem.num)
        return None

    def last(self):
        return (self.sem, self.n, self.sem.num)

    def dma(self, line, fn, *after):
        self.wait(*after)
        line.n += 16
        fn(self.eng).then_inc(line.sem, 16)
        return (line.sem, line.n, line.sem.num)


class Line:

    def __init__(self, sem):
        self.sem, self.n = sem, 0

    def all(self):
        return (self.sem, self.n, self.sem.num)


class Ring:

    def __init__(self, bufs):
        self.bufs, self.free, self.i = bufs, [None] * len(bufs), -1

    def take(self):
        n = len(self.bufs)
        self.i = next((self.i + k) % n for k in range(1, n + 1) if self.free[(self.i + k) % n] != "in use")
        free, self.free[self.i] = self.free[self.i], "in use"
        return self.i, self.bufs[self.i], free


def program(nc, x, ln1_w, ln1_b, w_qkv, b_qkv, rpb, w_proj, b_proj, ln2_w, ln2_b, w_fc1, b_fc1, w_fc2, b_fc2,
            Wq, bq, Wk, bk, Wv, bv, sigma, phi, M_u, M_pp, M_pm, log_w, gumbel,
            c_id, c_fwd, c_vdft, c_tw, c_inv, c_ar, c_msk, c_rev, out):
    with ExitStack() as ctx:
        nsem = [0]

        def sem(tag="s"):
            nsem[0] += 1
            return ctx.enter_context(nc.semaphore(f"{tag}{nsem[0]}"))

        def line(tag="l"):
            return Line(sem(tag))

        pe, act, dve, pool, sp = (Queue(e) for e in (nc.tensor, nc.scalar, nc.vector, nc.gpsimd, nc.sync))
        for q, n in ((pe, "pe"), (act, "act"), (dve, "dve"), (pool, "pool")):
            q.on(sem(n))

        dr = lambda name, shape, dt=F32: nc.dram_tensor(name, shape, dt, kind="Internal").ap()
        Vd = dr("Vd", [NB, PW, PW, C])
        biasD = dr("biasD", [NH, 64, 196])
        T2 = dr("T2", [NB, SLOTS, 512])
        Un = dr("Un", [NB, SLOTS, 512])
        Ud = dr("Ud", [128, NB, SLOTS * 8])
        Yd = dr("Yd", [SLOTS, 32, 256])
        Mbf = dr("Mbf", [2, 3, 16, 16384], BF16)
        MUd = dr("MUd", [3, 3, 16384], BF16)

        VbD = dr("VbD", [2, KT, NCH, 112], BF16)
        banks = ctx.enter_context(nc.psum_tensor("banks", [128, 8 * 512], F32))
        psum = [banks[:, 512 * i:512 * i + 512] for i in range(8)]
        wsel = ctx.enter_context(nc.sbuf_tensor("wsel", [128, 24], F32))

        def settle(*lines):
            ends = [q.last() for q in (pe, act, dve, pool)] + [ln.all() for ln in lines]
            for q in (pe, act, dve, pool, sp):
                q.wait(*ends)

        P = dict(nc=nc, ctx=ctx, line=line, pe=pe, act=act, dve=dve, pool=pool, sp=sp, banks=banks, psum=psum,
                 wsel=wsel, Vd=Vd, biasD=biasD, T2=T2, Un=Un, Ud=Ud, Yd=Yd, Mbf=Mbf, MUd=MUd, VbD=VbD,
                 x=x, ln1_w=ln1_w, ln1_b=ln1_b, w_qkv=w_qkv, b_qkv=b_qkv, rpb=rpb, w_proj=w_proj, b_proj=b_proj,
                 ln2_w=ln2_w, ln2_b=ln2_b, w_fc1=w_fc1, b_fc1=b_fc1, w_fc2=w_fc2, b_fc2=b_fc2,
                 Wq=Wq, bq=bq, Wk=Wk, bk=bk, Wv=Wv, bv=bv, sigma=sigma, phi=phi, M_u=M_u, M_pp=M_pp, M_pm=M_pm,
                 log_w=log_w, gumbel=gumbel, c_id=c_id, c_fwd=c_fwd, c_vdft=c_vdft, c_tw=c_tw, c_inv=c_inv,
                 c_ar=c_ar, c_msk=c_msk, c_rev=c_rev, out=out)
        phase_ab(P)
        settle(*P["ends_ab"], *P["ends_prep"])
        phase_fwd(P)
        settle(*P["ends_fwd"])
        phase_freq(P)
        settle(*P["ends_freq"])
        phase_inv(P)


def phase_ab(P):
    nc, line = P["nc"], P["line"]
    pe, act, dve, pool, sp, psum = P["pe"], P["act"], P["dve"], P["pool"], P["sp"], P["psum"]
    Vd, biasD, T2, Un = P["Vd"], P["biasD"], P["T2"], P["Un"]
    with ExitStack() as c2:
        sb = lambda name, shape, dt=F32: c2.enter_context(nc.sbuf_tensor(name, shape, dt))
        XR_ = sb("XR", [G, 3 * NJ, 512])
        qT = [sb(f"qT{i}", [128, T]) for i in range(2)]
        kP = [sb(f"kP{i}", [128, PW, PW]) for i in range(2)]
        oT = sb("oT", [128, T])
        Qs = [sb(f"Qs{i}", [128, 7, NH, 64]) for i in range(2)]
        XN = Ring([sb(f"XN{i}", [G, 4, 132]) for i in range(5)])
        XT = Ring([sb(f"XT{i}", [128, 392]) for i in range(4)])
        VS = Ring([sb(f"VS{i}", [G, 512]) for i in range(2)])
        HT = Ring([sb(f"hT{i}", [128, 4, 392]) for i in range(2)])
        VC = Ring([sb(f"VC{i}", [G, 2, 128]) for i in range(4)])
        SB = Ring([sb(f"SB{i}", [128, 2, 196]) for i in range(2)])
        PB = Ring([sb(f"PB{i}", [128, 2, 196]) for i in range(3)])
        PN = Ring([sb(f"PN{i}", [128, 2, 196]) for i in range(3)])
        PT = Ring([sb(f"PT{i}", [G, 512]) for i in range(3)])
        mx = Ring([sb(f"mx{i}", [128, 6]) for i in range(4)])
        st = Ring([sb(f"st{i}", [G, 4, 6]) for i in range(2)])
        mv = sb("mv", [G, NB * NJ, 4, 2])
        rs = sb("rs", [G, 4, NB * NJ, 4])
        nw = Ring([sb(f"nw{i}", [G, 4, 4]) for i in range(2)])
        ident = sb("ident", [128, 128])
        wqkv = sb("wqkv", [128, 384])
        wpr = sb("wpr", [128, 128])
        wf1 = sb("wf1", [128, 512])
        wf2 = sb("wf2", [128, 4, 128])
        wl1 = sb("wl1", [128, 3, 128])
        biasN = sb("biasN", [128, 2, 196])
        col = sb("col", [128, 16])
        rowb = sb("rowb", [128, 6, 128])
        kv = sb("kv", [128, 5, 128])
        zero = SB.bufs[0]

        ld, ldx = line("ld"), [line("ldx") for _ in range(NB)]
        cw = lambda a: a.rearrange("(p o) -> p o", o=1)
        def row(g):
            return XR_[:, g % (3 * NJ), :]

        def load_x(b, *after):
            s0 = NJ * (b % 3)
            return sp.dma(ldx[b], lambda e: e.dma_start(XR_[:, s0:s0 + NJ, :], P["x"][b].rearrange(
                "(J r) w c -> (J r w c)", r=7).rearrange("(J j x) -> j J x", J=NJ, j=G)), *after)

        la = line("la0")
        t_x = {0: load_x(0)}
        sp.dma(la, lambda e: e.dma_start(ident[:, :], P["c_id"]))
        sp.dma(la, lambda e: e.dma_start(wqkv[:, :], P["w_qkv"]))
        for i, a in enumerate((P["ln1_w"], P["ln1_b"], P["b_qkv"][0:128], P["b_qkv"][128:256])):
            sp.dma(la, lambda e: e.dma_start(col[:, i:i + 1], cw(a)))
        t_la = la.all()
        row_in = lambda i, a: sp.dma(ld, lambda e: e.dma_start(
            rowb[:, i, :], a.rearrange("(o p) -> o p", o=1).broadcast_to([128, 128])))
        row_in(0, P["b_qkv"][256:384])
        t_bv = ld.all()
        ld = line("ld")
        t_z = pool(lambda e: e.memset(biasN[:, :, :], BIG))
        t_z0 = pool(lambda e: e.memset(zero[:, :, :], 0.0))
        lb = line("lb")
        sp.dma(lb, lambda e: e.dma_start(biasD.rearrange("(a h) q k -> (h q) a k", a=2), biasN[:, :, :]), t_z)
        lz = line("lz")
        for b in range(NB):
            for rr in ((0, 3), (PW - 3, 3)):
                sp.dma(lz, lambda e, b=b, rr=rr: e.dma_start(
                    Vd[b, rr[0]:rr[0] + 3].rearrange("r w c -> (r w c)").rearrange("(p n) -> p n", p=93),
                    zero.rearrange("p a b -> p (a b)")[0:93, 0:256]), t_z0)
            for cc in (0, PW - 3):
                sp.dma(lz, lambda e, b=b, cc=cc: e.dma_start(
                    Vd[b, 3:PW - 3, cc:cc + 3, :].rearrange("r w c -> r (w c)"),
                    zero.rearrange("p a b -> p (a b)")[0:56, 0:384]), t_z0)
        lr = line("lr")
        t_b0 = lb.all()
        for h in range(NH):
            for qi in range(8):
                def f(e, h=h, qi=qi):
                    dst = bass.AP(biasD.tensor, h * 12544 + qi * 1582, [[197, 8], [14, 7], [1, 7]])
                    src = bass.AP(P["rpb"].tensor, h * 49, [[0, 8], [7, 7], [1, 7]])
                    return e.dma_start(dst, src)
                sp.dma(lr, f, t_b0)
        t_raw = sp.dma(lb, lambda e: e.dma_start(
            biasN[:, :, :], biasD.rearrange("(a h) q k -> (h q) a k", a=2)), lr.all())
        for i, a in enumerate((P["ln2_w"], P["ln2_b"])):
            sp.dma(ld, lambda e: e.dma_start(col[:, 4 + i:5 + i], cw(a)))
        for i in range(4):
            sp.dma(ld, lambda e: e.dma_start(col[:, 6 + i:7 + i], cw(P["b_fc1"][128 * i:128 * i + 128])))
        for i, a in enumerate((P["b_proj"], P["b_fc2"], P["bq"], P["bk"], P["bv"])):
            row_in(1 + i, a)
        sp.dma(ld, lambda e: e.dma_start(wpr[:, :], P["w_proj"]))
        sp.dma(ld, lambda e: e.dma_start(wf1[:, :], P["w_fc1"]))
        sp.dma(ld, lambda e: e.dma_start(wf2[:, :, :], P["w_fc2"].rearrange("(i p) c -> p i c", p=128)))
        for i, a in enumerate((P["Wq"], P["Wk"], P["Wv"])):
            sp.dma(ld, lambda e: e.dma_start(wl1[:, i, :], a))
        t_ld = ld.all()
        for b in (1, 2):
            t_x[b] = load_x(b)
        t_q0 = [pool(lambda e, i=i: e.memset(Qs[i][:, :, :, :], 0.0)) for i in range(2)]
        t_k0 = [pool(lambda e, i=i: e.memset(kP[i][:, :, :], 0.0)) for i in range(2)]
        t_o0 = None
        for i in range(5):
            t_o0 = pool(lambda e, i=i: e.memset(XN.bufs[i][:, :, 128:129], 1.0))
        ones = sb("ones", [128, 128])
        t_one = pool(lambda e: e.memset(ones[:, :], 1.0))
        t_m = pool(lambda e: e.tensor_scalar(PB.bufs[0][:, :, :], biasN[:, :, :], 0.5 * BIG, None, ALU.is_lt), t_raw)
        t_m = pool(lambda e: e.tensor_scalar(PB.bufs[0][:, :, :], PB.bufs[0][:, :, :], -2.0, 1.0, ALU.mult, ALU.add), t_m)
        t_bias = pool(lambda e: e.tensor_tensor(biasN[:, :, :], biasN[:, :, :], PB.bufs[0][:, :, :], ALU.mult), t_m)
        PB.free[0] = t_bias
        SB.free[0] = lz.all()
        t_c = pool(lambda e: e.tensor_scalar(col[:, 10:11], col[:, 2:3], -SC, None, ALU.mult), t_la)
        gen = Ring([psum[0], psum[1], psum[5]])
        psS, psT = Ring(psum[2:4]), Ring(psum[4:5])
        po, pC = psum[6], psum[7]

        def rstd(k, g, t_mv):
            i, w, fr = nw.take()
            v, y = w[:, 0, :], rs[:, k, g, :]
            t = dve(lambda e: e.tensor_scalar(v, mv[:, g, :, 1], EPS, None, ALU.add), t_mv, fr)
            t = dve(lambda e: e.tensor_scalar(w[:, 1, :].bitcast(I32), v.bitcast(I32), 1, None,
                                              ALU.arith_shift_right), t)
            t = dve(lambda e: e.tensor_scalar(y.bitcast(I32), w[:, 1, :].bitcast(I32), -1, 0x5f3759df,
                                              ALU.mult, ALU.add), t)
            for _ in range(3):
                t = pool(lambda e: e.tensor_tensor(w[:, 2, :], y, y, ALU.mult), t)
                t = pool(lambda e: e.tensor_tensor(w[:, 2, :], w[:, 2, :], v, ALU.mult), t)
                t = pool(lambda e: e.tensor_scalar(w[:, 2, :], w[:, 2, :], -0.5, 1.5, ALU.mult, ALU.add), t)
                t = pool(lambda e: e.tensor_tensor(y, y, w[:, 2, :], ALU.mult), t)
            nw.free[i] = t
            return t

        def stats(g, t_src):
            i, s, fr = st.take()
            for m in range(4):
                t = dve(lambda e, m=m: e.bn_stats(s[:, m, :], row(g)[:, 128 * m:128 * m + 128]), t_src, fr, tick=m == 3)
            for m in range(4):
                t2 = dve(lambda e, m=m: e.bn_aggr(mv[:, g, m, :], s[:, m, :]), t, mv_free[g], tick=m == 3)
            st.free[i] = t2
            return t2

        mv_free = [None] * (NB * NJ)

        def norm(k, g, t_r):
            i, n, fr = XN.take()
            for m in range(4):
                t = dve(lambda e, m=m: e.tensor_scalar(n[:, m, 0:128], row(g)[:, 128 * m:128 * m + 128],
                                                        mv[:, g, m, 0:1], rs[:, k, g, m:m + 1],
                                                        ALU.subtract, ALU.mult), t_r, fr, t_o0)
            mv_free[g] = t
            return i, n, t

        def transposed(n, t_n):
            i, p, fr = gen.take()
            for m in range(4):
                t = pe(lambda e, m=m: e.transpose(p[:, G * m:G * m + G], n[:, m, 0:128], ident[0:G, 0:G]),
                       t_n, fr, t_la, tick=m == 3)
            return i, p, t

        q_free, k_free = [None, None], [None, None]
        q_done = {}
        v_done = {}
        lv = [line("lv") for _ in range(2)]
        t_x_cur = {}

        def qkv(b):
            while b >= 3 and (b - 3, NJ - 1) not in u_done:
                yield
            if b >= 3:
                t_x[b] = load_x(b, *[t for J in range(NJ) for t in (t2_done[b - 3, J], u_done[b - 3, J])])
            r = rstd(0, NJ * b, stats(NJ * b, t_x[b]))
            yield
            for J in range(NJ):
                g = NJ * b + J
                xi, n, t = norm(0, g, r)
                if J + 1 < NJ:
                    r = rstd(0, g + 1, stats(g + 1, t_x[b]))
                yield
                i, p, t = transposed(n, t)
                XN.free[xi] = t
                yield 0
                a, xt, fr = XT.take()
                t = act(lambda e: e.activation(xt.rearrange("c (j m) -> c m j", m=4),
                                               p[:, 0:392].rearrange("c (m j) -> c m j", m=4),
                                               ACT.Identity, bias=col[:, 1:2], scale=col[:, 0:1]), t, fr, t_la)
                gen.free[i] = t
                yield
                i, p, fr = gen.take()
                t1 = pe(lambda e: e.matmul(p[:, 0:392], wqkv[:, 0:128], xt[:, :], start=True, stop=True), t, fr)
                yield 0
                t2 = act(lambda e: e.activation(qT[b % 2][:, 392 * J:392 * J + 392], p[:, 0:392], ACT.Identity,
                                                bias=col[:, 10:11], scale=-SC), t1, t_c, q_free[b % 2])
                gen.free[i] = t2
                yield
                i, p2, fr = gen.take()
                t1 = pe(lambda e: e.matmul(p2[:, 0:392], wqkv[:, 128:256], xt[:, :], start=True, stop=True), fr)
                yield 0
                t3 = dve(lambda e: e.tensor_scalar(kP[b % 2][:, 3 + 7 * J:10 + 7 * J, 3:59],
                                                   p2[:, 0:392].rearrange("c (r w) -> c r w", w=56),
                                                   col[:, 3:4], None, ALU.add), t1, t_k0[b % 2], k_free[b % 2])
                gen.free[i] = t3
                q_done[b, J] = (t2, t3)
                yield
                i, p3, fr = gen.take()
                xm = xt.rearrange("c (j m) -> c m j", m=4)
                for m in range(4):
                    t1 = pe(lambda e, m=m: e.matmul(p3[0:G, 128 * m:128 * m + 128], xm[:, m, :], wqkv[:, 256:384],
                                                    start=True, stop=True), fr, tick=m == 3)
                XT.free[a] = t1
                yield 0
                vi, vs, vf = VS.take()
                t4 = dve(lambda e: e.tensor_tensor(vs.rearrange("j (m c) -> j m c", m=4),
                                                   p3[0:G, :].rearrange("j (m c) -> j m c", m=4),
                                                   rowb[0:G, 0:1, :].broadcast_to([G, 4, 128]), ALU.add), t1, vf, t_bv)
                gen.free[i] = t4
                ln = lv[vi]
                t5 = sp.dma(ln, lambda e: e.dma_start(
                    bass.AP(Vd.tensor, ((b * PW + 3 + 7 * J) * PW + 3) * C, [[PW * C, 7], [512, 14], [1, 512]]),
                    vs[:, :]), t4)
                VS.free[vi] = t5
                v_done[b, J] = t5
                yield

        lvc = [line("lvc") for _ in range(5)]
        o_free = [None] * NJ
        x2 = {}
        qs_free = [None, None]
        o_done = {}

        def spread(b, i):
            s = (7 * b + i) % 2
            src = qT[b % 2].rearrange("c (r w) -> c r w", w=56)[:, 8 * i:8 * i + 8, :].rearrange(
                "c r (x w) -> c x r w", w=8)
            for h in range(NH):
                hs = slice(32 * h, 32 * h + 32)
                t = pool(lambda e: e.tensor_copy(
                    Qs[s][hs, :, h, :].rearrange("c x (r w) -> c x r w", w=8), src[hs]),
                    pool.last(), t_q0[s], qs_free[s], *[q_done[b, min(7, (8 * i + d) // 7)][0] for d in (0, 7)])
            pool.wait(t)
            if i == 6:
                q_free[b % 2] = t
            return t

        tiles = [(b, i, jx) for b in range(NB) for i in range(7) for jx in range(7)]
        s_qs, s_po, ended = {}, [None], []
        h_s, h_m, h_e, h_p, h_t, h_o, h_v = {}, {}, {}, {}, {}, {}, {}

        def t_scores(n):
            b, i, jx = tiles[n]
            if (b, i, jx) == (0, 0, 0):
                s_qs[0, 0] = spread(0, 0)
            nxt = n + 4
            if jx == 3 and nxt < len(tiles) and tiles[nxt][0] == b:
                s_qs[b, i + 1] = spread(b, i + 1)
            if jx == 0 and (b, i) not in s_qs:
                s_qs[b, i] = spread(b, i)
            si, S, fr = psS.take()
            kr = [q_done[b, J][1] for J in range(NJ)] if (i, jx) == (0, 0) else []
            for pr in range(2):
                t = pe(lambda e: e.matmul(
                    S[:, 196 * pr:196 * pr + 196], Qs[(7 * b + i) % 2][:, jx, 2 * pr:2 * pr + 2, :],
                    kP[b % 2][:, 8 * i:8 * i + 14, 8 * jx:8 * jx + 14], start=True, stop=True),
                    fr, s_qs[b, i], *kr, tick=pr == 1)
            if jx == 6:
                qs_free[(7 * b + i) % 2] = t
            if (i, jx) == (6, 6):
                k_free[b % 2] = t
                ended.append(b)
            h_s[n] = (si, S, t)

        def t_max(n):
            si, S, t = h_s.pop(n)
            bi, sbf, f1 = SB.take()
            mi, m_, f2 = mx.take()
            for pr in range(2):
                td = dve(lambda e: e.tensor_tensor_reduce(
                    out=sbf[:, pr, :], in0=S[:, 196 * pr:196 * pr + 196], in1=biasN[:, pr, :], scale=1.0,
                    scalar=3.0e38, op0=ALU.add, op1=ALU.min, accum_out=m_[:, pr:pr + 1]),
                    t, f1, f2, t_bias)
            psS.free[si] = td
            pi, pb, f3 = PB.take()
            for pr in range(2):
                ta = act(lambda e: e.activation(
                    pb[:, pr, :], sbf[:, pr, :], ACT.Exp, bias=m_[:, pr:pr + 1], scale=-1.0,
                    accum_out=m_[:, 2 + pr:3 + pr]), td, f3)
            SB.free[bi] = ta
            h_m[n] = (pi, pb, mi, m_, ta)

        def t_norm(n):
            pi, pb, mi, m_, ta = h_m.pop(n)
            tr = dve(lambda e: e.reciprocal(m_[:, 4:6], m_[:, 2:4]), ta)
            ni, pn, f4 = PN.take()
            for pr in range(2):
                tp = dve(lambda e: e.tensor_scalar(
                    pn[:, pr, :], pb[:, pr, :], m_[:, 4 + pr:5 + pr], None, ALU.mult), tr, f4)
            PB.free[pi], mx.free[mi] = tp, tp
            h_e[n] = (ni, pn, tp)

        def t_turn(n):
            ni, pn, tp = h_e.pop(n)
            ti, pt, fr = psT.take()
            for c in range(2):
                for pr in range(2):
                    t = pe(lambda e: e.transpose(
                        pt[0:G, 256 * c + 128 * pr:256 * c + 128 * pr + 128],
                        pn[:, pr, G * c:G * c + G], ident[:, :]), tp, fr, tick=(c, pr) == (1, 1))
            PN.free[ni] = t
            h_t[n] = (ti, pt, t)

        def t_keep(n):
            ti, pt, t = h_t.pop(n)
            oi, ob, fo = PT.take()
            if n % 3:
                t = act(lambda e: e.activation(ob[:, :], pt[0:G, :], ACT.Copy), t, fo)
            else:
                t = dve(lambda e: e.tensor_copy(ob[:, :], pt[0:G, :]), t, fo)
            psT.free[ti] = t
            h_o[n] = (oi, ob, t)

        def t_values(n):
            b, i, jx = tiles[n]
            vi, vc, fr = VC.take()
            need = [v_done[b, J] for J in range(NJ)] if (i, jx) == (0, 0) else []
            for c in range(2):
                t = sp.dma(lvc[vi], lambda e: e.dma_start(
                    vc[:, c, :], Vd[b, 8 * i + 7 * c:8 * i + 7 * c + 7, 8 * jx:8 * jx + 14, :]),
                    fr, lz.all(), *need)
            h_v[n] = (vi, vc, t)

        def t_out(n):
            b, i, jx = tiles[n]
            oi, ob, t = h_o.pop(n)
            vi, vc, tv = h_v.pop(n)
            for c in range(2):
                for h in range(NH):
                    t1 = pe(lambda e: e.matmul(
                        po[32 * h:32 * h + 32, 64 * jx:64 * jx + 64], vc[:, c, 32 * h:32 * h + 32],
                        ob[:, 256 * c + 64 * h:256 * c + 64 * h + 64], start=c == 0, stop=c == 1,
                        tile_position=(0, 32 * h)),
                        t, tv, s_po[0], tick=(c, h) == (1, 3))
            PT.free[oi], VC.free[vi] = t1, t1
            if jx == 6:
                fr = [o_free[J] for J in range(NJ) if 7 * J < 8 * i + 8 and 7 * J + 7 > 8 * i]
                t = act(lambda e: e.activation(
                    oT.rearrange("c (r w) -> c r w", w=56)[:, 8 * i:8 * i + 8, :].rearrange(
                        "c r (x w) -> c x r w", w=8),
                    po[:, 0:448].rearrange("c (x r w) -> c x r w", r=8, w=8), ACT.Copy), t1, *fr)
                s_po[0] = t
                o_done[b, i] = t
                for J in [i] if i < 6 else [6, 7]:
                    back.append(("mlp", mlp(b, J)))
                if i == 6:
                    back.append(("attn", attn(b)))

        back, qk, live = [], [], []
        LANES = 3

        def pick(back):
            while back:
                kind = back[0][0]
                kinds = [k for k, _ in live]
                if len(live) >= LANES or kind == "attn" and "mlp" in kinds or kind in kinds and kind != "mlp":
                    break
                live.append(back.pop(0))
            todo = ([qk[0]] if qk else []) + live
            return todo[0:2], todo[2:4]

        def advance(item):
            try:
                return next(item[1])
            except StopIteration:
                (qk if item[0] == "qkv" else live).remove(item)
                return None

        def unit(tile_a=(), tile_b=()):
            g1, g2 = pick(back)
            mid = [item for item in g1 if advance(item) == 0]
            for f in tile_a:
                f()
            for item in mid:
                advance(item)
            mid = [item for item in g2 if advance(item) == 0]
            for f in tile_b:
                f()
            for item in mid:
                advance(item)
            return bool(g1)

        def add_rows(k, g, after):
            return pool(lambda e: e.tensor_tensor(
                row(g).rearrange("j (m c) -> j m c", m=4), row(g).rearrange("j (m c) -> j m c", m=4),
                rowb[0:G, k:k + 1, :].broadcast_to([G, 4, 128]), ALU.add), *after)

        def mlp(b, J):
            g = NJ * b + J
            ta = add_rows(1, g, [t_x[b], t_ld])
            i, p, fr = gen.take()
            om = oT[:, 392 * J:392 * J + 392].rearrange("c (j m) -> c m j", m=4)
            for m in range(4):
                t = pe(lambda e, m=m: e.matmul(p[0:G, 128 * m:128 * m + 128], om[:, m, :], wpr[:, :],
                                               start=True, stop=True), t_ld, fr, o_done[b, min(J, 6)], tick=m == 3)
            o_free[J] = t
            yield 0
            t = dve(lambda e: e.tensor_tensor(row(g), row(g), p[0:G, :], ALU.add), t, ta)
            gen.free[i] = t
            t = stats(g, t)
            t = rstd(1, g, t)
            yield
            yield
            yield
            xi, n, t = norm(1, g, t)
            ta = add_rows(2, g, [t])
            yield
            i, p, t = transposed(n, t)
            XN.free[xi] = t
            yield 0
            a, xt, fr = XT.take()
            t = act(lambda e: e.activation(xt[:, :], p[:, 0:392], ACT.Identity, bias=col[:, 5:6],
                                           scale=col[:, 4:5]), t, fr, t_ld)
            gen.free[i] = t
            yield
            th = []
            hi, hT, hf = HT.take()
            for f in range(4):
                i, p, fr = gen.take()
                t1 = pe(lambda e, f=f, p=p: e.matmul(p[:, 0:392], wf1[:, 128 * f:128 * f + 128], xt[:, :],
                                                     start=True, stop=True), t, fr)
                if f == 0:
                    yield 0
                t2 = act(lambda e, f=f, p=p: e.activation(hT[:, f, :], p[:, 0:392], ACT.Gelu,
                                                          bias=col[:, 6 + f:7 + f]), t1, hf)
                gen.free[i] = t2
                th.append(t2)
            XT.free[a] = t1
            yield
            i, p, fr = gen.take()
            for m in range(4):
                for f in range(4):
                    t = pe(lambda e, m=m, f=f: e.matmul(p[0:G, 128 * m:128 * m + 128], hT[:, f, G * m:G * m + G],
                                                        wf2[:, f, :], start=f == 0, stop=f == 3),
                           fr, th[f], tick=(m, f) == (3, 3))
            HT.free[hi] = t
            yield 0
            t = dve(lambda e: e.tensor_tensor(row(g), row(g), p[0:G, :], ALU.add), t, ta)
            gen.free[i] = t
            t = stats(g, t)
            t = rstd(2, g, t)
            yield
            yield
            yield
            xi, n, t = norm(2, g, t)
            yield
            for m in range(4):
                t = pe(lambda e, m=m: e.matmul(pC[:, 0:129], n[:, m, 0:128], n[:, m, 0:129],
                                               start=(J, m) == (0, 0), stop=(J, m) == (NJ - 1, 3)),
                       t, c_free[0], tick=m == 3)
            XN.free[xi] = t
            x2[g] = t
            yield

        c_free = [None]
        t2_done, u_done = {}, {}
        lt2 = [line("lt2") for _ in range(NJ)]
        kv_free = [None, None]
        lst = [line("lst") for _ in range(5)]

        def attn(b):
            tc = x2[NJ * b + NJ - 1]
            Cs, S1 = kv[:, 0, :], kv[:, 4, 0:1]
            t = act(lambda e: e.activation(Cs, pC[:, 0:128], ACT.Copy), tc, *kv_free)
            t = act(lambda e: e.activation(S1, pC[:, 128:129], ACT.Copy), tc, *kv_free)
            c_free[0] = t
            ts = pool(lambda e: e.tensor_scalar(kv[:, 1, :], ones[:, :], S1, None, ALU.mult), t, t_one)
            i, p, fr = gen.take()
            t1 = pe(lambda e: e.matmul(p[:, 0:128], Cs, wl1[:, 2, :], start=True, stop=True), t, fr)
            t1 = pe(lambda e: e.matmul(p[:, 128:256], kv[:, 1, :], wl1[:, 2, :], start=True, stop=True), ts)
            t2 = dve(lambda e: e.scalar_tensor_tensor(kv[:, 2, :], rowb[:, 5, :], S1, p[:, 0:128],
                                                      ALU.mult, ALU.add), t1, *kv_free)
            t2 = dve(lambda e: e.tensor_tensor(kv[:, 2, :], kv[:, 2, :], wl1[:, 1, :], ALU.mult), t2)
            t3 = dve(lambda e: e.scalar_tensor_tensor(kv[:, 3, :], rowb[:, 5, :], float(T), p[:, 128:256],
                                                      ALU.mult, ALU.add), t1)
            t3 = dve(lambda e: e.tensor_tensor(kv[:, 3, :], kv[:, 3, :], rowb[:, 4, :], ALU.mult), t3)
            gen.free[i] = t3
            yield
            i, p, fr = gen.take()
            t = pe(lambda e: e.matmul(p[:, 0:128], ones[:, :], kv[:, 2, :], start=True, stop=True), t2, fr)
            t = dve(lambda e: e.tensor_tensor(kv[:, 3, :], kv[:, 3, :], p[:, 0:128], ALU.add), t, t3)
            gen.free[i] = t
            tw = dve(lambda e: e.tensor_tensor(kv[:, 2, :], kv[:, 3, :], wl1[:, 0, :], ALU.mult), t)
            tb = dve(lambda e: e.tensor_tensor(kv[:, 4, :], kv[:, 3, :], rowb[:, 3, :], ALU.mult), t)
            yield
            for J in range(NJ):
                g = NJ * b + J
                xi, n, t = norm(2, g, x2[g])
                yield
                ta = pool(lambda e: e.tensor_tensor(
                    row(g).rearrange("j (m c) -> j m c", m=4), row(g).rearrange("j (m c) -> j m c", m=4),
                    kv[0:G, 4:5, :].broadcast_to([G, 4, 128]), ALU.add), t, tb)
                i, p, t = transposed(n, t)
                XN.free[xi] = t
                yield 0
                a, xt, fr = XT.take()
                t = act(lambda e: e.activation(xt[:, :], p[:, 0:392], ACT.Copy), t, fr)
                gen.free[i] = t
                yield
                i, p, fr = gen.take()
                for m in range(4):
                    t = pe(lambda e, m=m: e.matmul(p[0:G, 128 * m:128 * m + 128], xt[:, G * m:G * m + G], kv[:, 2, :],
                                                   start=True, stop=True), fr, t, tw, tick=m == 3)
                XT.free[a] = t
                kv_free[:] = t, ta
                yield 0
                t = dve(lambda e: e.tensor_tensor(row(g), row(g), p[0:G, :], ALU.add), t, ta)
                gen.free[i] = t
                t2_done[b, J] = sp.dma(lt2[J], lambda e: e.dma_start(T2[b, G * J:G * J + G, :], row(g)), t)
                t = stats(g, t)
                t = rstd(3, g, t)
                yield
                yield
                yield
                xi, n, t = norm(3, g, t)
                u_done[b, J] = t
                t = sp.dma(lst[xi], lambda e: e.dma_start(
                    Un[b, G * J:G * J + G, :].rearrange("j (m c) -> j m c", m=4), n[:, :, 0:128]), t)
                XN.free[xi] = t
                yield

        for _ in qkv(0):
            pass
        first = ((3, t_turn), (2, t_norm), (1, t_max), (0, t_scores))
        second = ((5, t_out), (4, t_keep), (3, t_values))
        for n in range(len(tiles) + 5):
            if n < len(tiles) and n % 49 == 0:
                while qk:
                    unit()
                if n // 49 + 1 < NB:
                    qk.append(("qkv", qkv(n // 49 + 1)))
                else:
                    for q in (sp, pe, act, dve, pool):
                        q.wait(q_free[0], k_free[0])
                    qk.append(("qkv", prepare(P, qT[0], kP[0].rearrange("p a b -> p (a b)"),
                                              kP[1].rearrange("p a b -> p (a b)"),
                                              lambda: [k_free[1]] if (NB - 1) in ended else [], gen)))
            now = [[(lambda s=s, k=n - lag: s(k)) for lag, s in part if 0 <= n - lag < len(tiles)]
                   for part in (second, first)]
            unit(*now)
        while unit():
            pass
        P["ends_ab"] = lt2 + lst + lv
        P["t_ab"] = [l.all() for l in lt2] + [l.all() for l in lst] + [l.all() for l in lv]


def prepare(P, A, K0, K1, k1_free, gen):
    line = P["line"]
    pe, act, dve, pool, sp = P["pe"], P["act"], P["dve"], P["pool"], P["sp"]
    w = P["wsel"]
    ML = Ring([A[:, 512 * i:512 * i + 512] for i in range(2)])
    mp, mm, dif = (A[:, 1024 + 512 * i:1536 + 512 * i] for i in range(3))
    mo = Ring([A[:, 2560 + 256 * i:2816 + 256 * i].bitcast(BF16) for i in range(2)])
    vd = K0[0:G, 0:1792].rearrange("p (a x) -> p a x", a=8)
    ph = K0[0:G, 1792:2816].rearrange("p (a m k) -> p a m k", a=8, m=4)
    vf = K0[:, 2816:3040]
    lg, tm, sg = K0[:, 3040:3048], K0[:, 3080:3104], K0[:, 3104:3108]
    mk = K0[:, 3048:3080].rearrange("p (i j) -> p i j", i=4)
    la, lp = line("la"), line("lp")
    bc = lambda a: a.rearrange("(o p) -> o p", o=1).broadcast_to([128, 4])
    sp.dma(la, lambda e: e.dma_start(lg[:, 0:4], bc(P["log_w"])))
    sp.dma(la, lambda e: e.dma_start(lg[:, 4:8], bc(P["gumbel"])))
    t = sp.dma(la, lambda e: e.dma_start(mk, P["c_msk"].rearrange("(o i) j -> o i j", o=1).broadcast_to([128, 4, 8])))
    t_s1 = pool(lambda e: e.memset(sg, 1.0))
    t_p0 = pool(lambda e: e.memset(ph, 0.0))
    for q in range(4):
        sp.dma(lp, lambda e: e.dma_start(sg[32 * q:32 * q + 16, 0:1],
                                         P["sigma"].rearrange("(p o) -> p o", o=1)), t_s1)
    phv = P["phi"][0:3136].rearrange("(a j m) k -> j a m k", j=G, m=4)
    for a in range(8):
        sp.dma(lp, lambda e: e.dma_start(ph[:, a, :, 0:16], phv[:, a]), t_p0)
    t_ph = lp.all()
    yield
    z, y, eq, h = tm[:, 0:4], tm[:, 4:8], tm[:, 8:12], tm[:, 12:16]
    t = dve(lambda e: e.tensor_tensor(z, lg[:, 0:4], lg[:, 4:8], ALU.add), t)
    t = dve(lambda e: e.reduce_max(tm[:, 16:17], z, mybir.AxisListType.X), t)
    t = dve(lambda e: e.tensor_scalar(z, z, tm[:, 16:17], None, ALU.subtract), t)
    t = act(lambda e: e.activation(y, z, ACT.Exp, accum_out=tm[:, 17:18]), t)
    yield
    t = dve(lambda e: e.reciprocal(tm[:, 18:19], tm[:, 17:18]), t)
    t = dve(lambda e: e.tensor_scalar(y, y, tm[:, 18:19], None, ALU.mult), t)
    t = dve(lambda e: e.reduce_max(tm[:, 16:17], y, mybir.AxisListType.X), t)
    t = dve(lambda e: e.tensor_scalar(eq, y, tm[:, 16:17], None, ALU.is_ge), t)
    t = dve(lambda e: e.memset(tm[:, 20:21], 1.0), t)
    for i in range(4):
        t = dve(lambda e: e.tensor_tensor(h[:, i:i + 1], eq[:, i:i + 1], tm[:, 20:21], ALU.mult), t)
        t = dve(lambda e: e.tensor_tensor(tm[:, 20:21], tm[:, 20:21], h[:, i:i + 1], ALU.subtract), t)
    t = dve(lambda e: e.tensor_tensor(w[:, 0:4], h, y, ALU.subtract), t)
    t_w = dve(lambda e: e.tensor_tensor(w[:, 0:4], w[:, 0:4], y, ALU.add), t)
    t = dve(lambda e: e.tensor_scalar(w[:, 8:16], mk[:, 0, :], h[:, 0:1], None, ALU.mult), t_w)
    for i in range(1, 4):
        t = dve(lambda e: e.scalar_tensor_tensor(w[:, 8:16], mk[:, i, :], h[:, i:i + 1], w[:, 8:16],
                                                 ALU.mult, ALU.add), t)
    yield

    lm = [line("lm") for _ in range(2)]
    lo = [line("lo") for _ in range(2)]

    def split(src, n, t, dst):
        for i in range(3):
            oi, o, fr = mo.take()
            t1 = act(lambda e: e.activation(o[:, 0:n], src[:, 0:n], ACT.Copy), t, fr)
            mo.free[oi] = sp.dma(lo[oi], lambda e: e.dma_start(dst(i), o[:, 0:n]), t1)
            yield
            if i < 2:
                t = dve(lambda e: e.tensor_tensor(src[:, 0:n], src[:, 0:n], o[:, 0:n], ALU.subtract), t1)
        last[0] = t1

    last = [None]

    def mixed(dst, n, view, *t_free):
        t = None
        for i in range(4):
            li, m, fr = ML.take()
            t1 = sp.dma(lm[li], lambda e: e.dma_start(m[:, 0:n], view(i)), fr)
            if i % 2:
                yield
            if i == 0:
                t = dve(lambda e: e.tensor_scalar(dst[:, 0:n], m[:, 0:n], w[:, 0:1], None, ALU.mult), t1, t_w, *t_free)
            else:
                t = dve(lambda e: e.scalar_tensor_tensor(dst[:, 0:n], m[:, 0:n], w[:, i:i + 1], dst[:, 0:n],
                                                         ALU.mult, ALU.add), t1, t)
            ML.free[li] = t
        last[0] = t

    flat = lambda a: a.rearrange("k d e -> (k d e)").rearrange("(p x) -> p x", p=128)
    f0 = f1 = None
    for c in range(4):
        cs = slice(512 * c, 512 * c + 512)
        yield from mixed(mp, 512, lambda i: flat(P["M_pp"][i])[:, cs], f0)
        yield from mixed(mm, 512, lambda i: flat(P["M_pm"][i])[:, cs], f1)
        t = last[0]
        t1 = dve(lambda e: e.tensor_tensor(dif, mp, mm, ALU.subtract), t, f0, f1)
        t2 = dve(lambda e: e.tensor_tensor(mp, mp, mm, ALU.add), t1)
        for par, (s, t) in enumerate(((mp, t2), (dif, t1))):
            yield from split(s, 512, t, lambda i: P["Mbf"][par, i].rearrange("k x -> (k x)").rearrange(
                "(p x) -> p x", p=128)[:, cs])
            f0, f1 = (last[0], f1) if par == 0 else (f0, last[0])
    yield from mixed(mm, 384, lambda i: flat(P["M_u"][i]), f1)
    yield from split(mm, 384, last[0], lambda i: P["MUd"][i].rearrange("k x -> (k x)").rearrange("(p x) -> p x", p=128))

    for i in range(2):
        s, r = sg[:, i:i + 1], sg[:, i + 1:i + 2]
        t = act(lambda e: e.activation(r, s, ACT.Sqrt), t_ph, t if i else None)
        t = dve(lambda e: e.tensor_scalar(sg[:, 3:4], r, 1e-30, None, ALU.max), t)
        t = dve(lambda e: e.reciprocal(sg[:, 3:4], sg[:, 3:4]), t)
        t = dve(lambda e: e.tensor_tensor(sg[:, 3:4], sg[:, 3:4], s, ALU.mult), t)
        t = dve(lambda e: e.tensor_tensor(r, r, sg[:, 3:4], ALU.add), t)
        t = dve(lambda e: e.tensor_scalar(r, r, 0.5, None, ALU.mult), t)
        yield
    t_sig = t
    while not k1_free():
        yield
    vp = [K1[:, 784 * i:784 * i + 784].bitcast(BF16) for i in range(3)]
    lvd, tf, t_vd = line("lvd"), None, None
    lst = line("lst")
    for c in range(7):
        cs = slice(224 * c, 224 * c + 224)
        t = sp.dma(lvd, lambda e: e.dma_start(vd, P["c_vdft"][:, :, cs]), t_vd)
        yield
        i, p, fr = gen.take()
        for a in range(8):
            t_vd = pe(lambda e: e.matmul(p[:, 0:224], ph[:, a, :, :], vd[:, a, :], start=a == 0, stop=a == 7),
                      t, t_ph, fr, tick=a == 7)
        yield 0
        t = act(lambda e: e.activation(vf, p[:, 0:224], ACT.Copy, scale=sg[:, 2:3]), t_vd, t_sig, tf)
        gen.free[i] = t
        t = dve(lambda e: e.tensor_copy(vp[0][:, cs], vf), t, *k1_free())
        for i in (1, 2):
            t = dve(lambda e: e.tensor_tensor(vf, vf, vp[i - 1][:, cs], ALU.subtract), t)
            t = dve(lambda e: e.tensor_copy(vp[i][:, cs], vf), t)
        tf = t
        yield
    for k, (_, v) in enumerate(TERMS):
        for q in range(4):
            sp.dma(lst, lambda e: e.dma_start(
                P["VbD"][q % 2, 16 * k:16 * k + 16, :, 56 * (q // 2):56 * (q // 2) + 56],
                vp[v][32 * q:32 * q + 16, :].rearrange("k (c x) -> k c x", c=NCH)), tf)
    lc = line("lc")
    for p in range(2):
        pool.dma(lc, lambda e: e.dma_start(P["VbD"][p, 112:118], P["c_ar"][p]))
    P["ends_prep"] = [lst, lc] + lo


def phase_fwd(P):
    nc, line = P["nc"], P["line"]
    pe, act, dve, pool, sp, psum = P["pe"], P["act"], P["dve"], P["pool"], P["sp"], P["psum"]
    Un = P["Un"]
    with ExitStack() as c2:
        sb = lambda name, shape, dt=F32: c2.enter_context(nc.sbuf_tensor(name, shape, dt))
        U = Ring([sb(f"U{i}", [128, SLOTS, 4, 2]) for i in range(2)])
        F = sb("F", [G, 2, 4, 784])
        UA = Ring([sb(f"UA{i}", [G, 4, 512]) for i in range(2)])
        UR = Ring([sb(f"UR{i}", [G, 4, 512]) for i in range(2)])
        EO = [Ring([sb(f"E{c}{i}", [G, 4, 512]) for i in range(2)]) for c in range(2)]
        lf, lu = line("lf"), [line("lu") for _ in range(2)]
        rev = sb("rev", [G, G])
        sp.dma(lf, lambda e: e.dma_start(rev[:, :], P["c_rev"]))
        tf = sp.dma(lf, lambda e: e.dma_start(F[:, :, :, :], P["c_fwd"]))
        bank = Ring(psum)
        lo_ = [line("lou") for _ in range(2)]
        n = 0
        for b in range(NB):
            i, ua, fr = UA.take()
            i, ur, fr2 = UR.take()
            sp.dma(lu[i], lambda e: e.dma_start(ua[:, :, :], Un[b, 0:392].rearrange("(a p) x -> p a x", p=G)), fr, fr2)
            t = sp.dma(lu[i], lambda e: e.dma_start(ur[:, :, :], Un[b, 392:784].rearrange(
                "(a p) x -> p a x", p=G)))
            ei, ev, fr = EO[0].take()
            oi, od, fr2 = EO[1].take()
            for a in range(4):
                pi, p, fp = bank.take()
                tp = pe(lambda e: e.matmul(p[0:G, :], rev[:, :], ur[:, 3 - a, :], start=True, stop=True), t, fp, tf)
                t0 = dve(lambda e: e.tensor_tensor(ev[:, a, :], ua[:, a, :], p[0:G, :], ALU.add), tp, t, fr)
                t1 = dve(lambda e: e.tensor_tensor(od[:, a, :], ua[:, a, :], p[0:G, :], ALU.subtract), fr2)
                bank.free[pi] = t1
            UA.free[i], UR.free[i] = t1, tp
            ui, u, fu = U.take()
            for m in range(4):
                for c, (src, ts) in enumerate(((ev, t0), (od, t1))):
                    for half in range(2):
                        pi, p, fr = bank.take()
                        for a in range(4):
                            tp = pe(lambda e, a=a: e.matmul(p[:, 0:392], src[:, a, 128 * m:128 * m + 128],
                                                            F[:, c, a, 392 * half:392 * half + 392],
                                                            start=a == 0, stop=a == 3), ts, fr, tf, tick=a == 3)
                        lo = 392 * (c ^ half)
                        dst = u[:, lo:lo + 392, m, half]
                        n += 1
                        if n % 2:
                            bank.free[pi] = act(lambda e: e.activation(dst, p[:, 0:392], ACT.Copy), tp, fu)
                        else:
                            bank.free[pi] = dve(lambda e: e.tensor_copy(dst, p[:, 0:392]), tp, fu)
            EO[0].free[ei], EO[1].free[oi] = tp, tp
            U.free[ui] = sp.dma(lo_[ui], lambda e: e.dma_start(P["Ud"][:, b], u.rearrange("d s m r -> d (s m r)")),
                                act.last(), dve.last())
        P["ends_fwd"] = lo_


def phase_freq(P):
    nc, line = P["nc"], P["line"]
    pe, act, dve, pool, sp = P["pe"], P["act"], P["dve"], P["pool"], P["sp"]
    banks, psum, Yd = P["banks"], P["psum"], P["Yd"]
    with ExitStack() as c2:
        sb = lambda name, shape, dt=F32: c2.enter_context(nc.sbuf_tensor(name, shape, dt))
        M = sb("M", [KT, 2, 16384], BF16)
        Gm = sb("Gm", [128, 2, 112, 128])
        VS = Ring([sb(f"V{i}", [KT, 2, 112], BF16) for i in range(2)])
        TW = Ring([sb(f"TW{i}", [128, 3, FC]) for i in range(2)])
        UL = Ring([sb(f"UL{i}", [128, NB, FC, 8]) for i in range(1)])
        U7 = Ring([sb(f"U7{i}", [128, FC, 56]) for i in range(2)])
        tmp = sb("tmp", [128, FC, 3, 4])
        YS = Ring([sb(f"YS{i}", [128, 7, 256]) for i in range(1)])
        zb = sb("zb", [1, 512], BF16)
        t_zb = pool(lambda e: e.memset(zb[:, :], 0.0))
        lm = line("lm2")
        for par in range(2):
            for k, (m, _) in enumerate(TERMS):
                sp.dma(lm, lambda e: e.dma_start(M[16 * k:16 * k + 16, par, :], P["Mbf"][par, m]))
            for r, tap in ((112, par), (115, 2)):
                sp.dma(lm, lambda e: e.dma_start(M[r:r + 3, par, :], P["MUd"][:, tap, :]))
        t_m = lm.all()
        lv, lw, ll = [line("lvq") for _ in range(2)], [line("ltw") for _ in range(2)], line("lul")
        ly = line("ly")
        tiles = Ring(psum[0:4])
        ready = {}

        def load(ch):
            vi, v, fv = VS.take()
            tv = sp.dma(lv[vi], lambda e: e.dma_start(v[:, :, :], P["VbD"][:, :, ch, :].rearrange("a k x -> k a x")), fv)
            wi, w, fw = TW.take()
            tw = sp.dma(lw[wi], lambda e: e.dma_start(
                w[:, :, :], P["c_tw"][:, FC * ch:FC * ch + FC].rearrange("(o a) s -> o a s", o=1).broadcast_to([128, 3, FC])), fw)
            li, u, fl = UL.take()
            tu = sp.dma(ll, lambda e: e.dma_start(u.rearrange("d b s x -> d b (s x)"),
                                                  P["Ud"][:, :, FC * 8 * ch:FC * 8 * ch + FC * 8]), fl)
            ui, u7, fu = U7.take()
            a = u7.rearrange("d s (m r b) -> d s m r b", m=7, r=2)
            s4 = u.rearrange("d b s (m r) -> d s m r b", m=4, r=2)
            t = pool(lambda e: e.tensor_copy(u7[:, :, 24:56].rearrange("d s (x b) -> d s x b", b=4),
                                             u.rearrange("d b s x -> d s x b")), tu, fu)
            cc = [w[:, k, :].rearrange("d (s o) -> d s o", o=1).broadcast_to([128, FC, 4]) for k in range(3)]
            for m in range(3):
                R, I = s4[:, :, m + 1, 0, :], s4[:, :, m + 1, 1, :]
                x = tmp[:, :, m, :]
                t = pool(lambda e: e.tensor_tensor(x, I, cc[1], ALU.mult), tw, pool.last())
                t = pool(lambda e: e.tensor_tensor(a[:, :, m, 0, :], R, cc[0], ALU.mult))
                t = pool(lambda e: e.tensor_tensor(a[:, :, m, 0, :], a[:, :, m, 0, :], x, ALU.add), t)
                t = pool(lambda e: e.tensor_tensor(x, R, cc[1], ALU.mult), t)
                t = pool(lambda e: e.tensor_tensor(a[:, :, m, 1, :], I, cc[2], ALU.mult))
                t = pool(lambda e: e.tensor_tensor(a[:, :, m, 1, :], a[:, :, m, 1, :], x, ALU.subtract), t)
            UL.free[li], TW.free[wi] = t, t
            ready[ch] = (vi, v, tv, ui, u7, t)

        used = [None, None]
        full = [None, None]
        ybank = [None] * 4
        count = [0]

        def filters(ch, par):
            vi, v, tv = ready[ch][0:3]
            ends = [None, None]
            for eg in range(32):
                ti, pt, fr = tiles.take()
                for k in range(4):
                    ec = 4 * eg + k
                    tp = pe(lambda e: e.matmul(pt[:, 128 * k:128 * k + 112],
                                               M.rearrange("r a (d e) -> r a e d", e=128)[:, par, ec, :],
                                               v[:, par, :], start=True, stop=True), fr, t_m, tv, tick=k == 3)
                src = pt.rearrange("d (e x) -> d x e", x=128)[:, 0:112, :]
                dst = Gm[:, par, :, 4 * eg:4 * eg + 4]
                count[0] += 1
                if count[0] % 2:
                    t = act(lambda e: e.activation(dst, src, ACT.Copy), tp, used[par])
                else:
                    t = dve(lambda e: e.tensor_copy(dst, src), tp, used[par])
                ends[count[0] % 2] = t
                tiles.free[ti] = t
                yield
            full[par] = ends
            if par == 1:
                VS.free[vi] = tp

        def sums(ch, par):
            ui, u7, tu = ready[ch][3:6]
            if par == 1:
                yi, ys, fy = YS.take()
            for gp in range(7):
                bk, cl = gp // 2, 256 * (gp % 2)
                pb = psum[4 + bk]
                wd = 512 if bk < 3 else 256
                if par == 0 and gp % 2 == 0:
                    pe(lambda e: e.matmul(pb[:, 0:wd], zb[:, 0:128], zb[:, 0:wd], start=True, stop=False),
                       ybank[bk], t_zb, tick=False)
                for q in (par, 2 + par):
                    for s in range(4):
                        sl = 4 * gp + s
                        r = ((q // 2) * FC + sl) * 2
                        tp = pe(lambda e: e.matmul(pb[32 * s:32 * s + 32, cl:cl + 256],
                                                   u7[:, sl, 8 * (3 - q):8 * (3 - q) + 32],
                                                   Gm[:, par, r:r + 2, :], start=False, stop=q == 3 and (gp % 2 == 1 or gp == 6),
                                                   tile_position=(0, 32 * s)),
                                tu, *full[par],
                                tick=s == 3)
                    yield
                if par == 1 and (gp % 2 or gp == 6):
                    g0 = gp - gp % 2
                    src = pb[:, 0:256 * (gp - g0 + 1)].rearrange("p (a x) -> p a x", x=256)
                    if bk % 2:
                        ybank[bk] = act(lambda e: e.activation(ys[:, g0:gp + 1, :], src, ACT.Copy), tp, fy)
                    else:
                        ybank[bk] = dve(lambda e: e.tensor_copy(ys[:, g0:gp + 1, :], src), tp, fy)
            used[par] = tp
            if par == 1:
                U7.free[ui] = tp
                for s in range(4):
                    dst = Yd[FC * ch:FC * ch + FC].rearrange("(g s) r x -> s r g x", s=4)[s]
                    t = sp.dma(ly, lambda e: e.dma_start(dst, ys[32 * s:32 * s + 32, :, :]), *ybank)
                YS.free[yi] = t

        def together(gen, mul):
            for i in range(32):
                if gen is not None:
                    next(gen)
                if i % 2 and 2 < i:
                    next(mul, None)
            for g in (gen, mul):
                if g is not None:
                    for _ in g:
                        pass

        load(0)
        for _ in filters(0, 0):
            pass
        for ch in range(NCH):
            together(filters(ch, 1), sums(ch, 0))
            if ch + 1 < NCH:
                load(ch + 1)
            together(filters(ch + 1, 0) if ch + 1 < NCH else None, sums(ch, 1))
        P["ends_freq"] = [ly]


def phase_inv(P):
    nc, line = P["nc"], P["line"]
    pe, act, dve, pool, sp, psum = P["pe"], P["act"], P["dve"], P["pool"], P["sp"], P["psum"]
    Yd, T2, w = P["Yd"], P["T2"], P["wsel"]
    out = P["out"].rearrange("b h w c -> b (h w c)").rearrange("b (j x) -> b j x", x=512)
    with ExitStack() as c2:
        sb = lambda name, shape, dt=F32: c2.enter_context(nc.sbuf_tensor(name, shape, dt))
        IV = sb("IV", [G, 2, 8, 392])
        YL = Ring([sb(f"YL{i}", [G, 8, 2, 2, 256]) for i in range(2)])
        YC = Ring([sb(f"YC{i}", [G, 2, 8, 2, 128]) for i in range(2)])
        RN = Ring([sb(f"RN{i}", [G, 2, 4, 256]) for i in range(2)])
        S2 = Ring([sb(f"S2{i}", [G, 256]) for i in range(2)])
        TT = Ring([sb(f"TT{i}", [G, 2, 256]) for i in range(2)])
        lf = line("lf3")
        rev = sb("rev3", [G, G])
        sp.dma(lf, lambda e: e.dma_start(rev[:, :], P["c_rev"]))
        tf = sp.dma(lf, lambda e: e.dma_start(IV[:, :, :, :], P["c_inv"]))
        ll, lr, lo = [line("ll") for _ in range(2)], [line("lr") for _ in range(2)], [line("lo3") for _ in range(2)]
        bank = Ring(psum)
        work = [(b, pp) for b in range(NB) for pp in range(2)]
        got = {}
        rows = lambda b, k, pp, A: A[b, 392 * k:392 * k + 392, 256 * pp:256 * pp + 256].rearrange("(a p) x -> p a x", p=G)

        def load(n):
            if n >= len(work):
                return
            b, pp = work[n]
            i, yl, fr = YL.take()
            for a in range(8):
                src = Yd[G * a:G * a + G].rearrange("s (p r b) x -> s b p r x", r=2, b=4)[:, b, 2 * pp:2 * pp + 2]
                t = sp.dma(ll[i], lambda e: e.dma_start(yl[:, a], src), fr)
            j, rn, fr = RN.take()
            for k in range(2):
                t2 = sp.dma(lr[j], lambda e: e.dma_start(rn[:, k], rows(b, k, pp, T2)), fr)
            got[n] = (i, yl, t, j, rn, t2)

        load(0)
        for n, (b, pp) in enumerate(work):
            load(n + 1)
            i, yl, t, j, rn, t2 = got.pop(n)
            ci, yc, fr = YC.take()
            ta = dve(lambda e: e.tensor_tensor(yc[:, 0], yl[:, :, :, 0, 0:128], yl[:, :, :, 1, 128:256], ALU.subtract), t, fr)
            tb = pool(lambda e: e.tensor_tensor(yc[:, 1], yl[:, :, :, 0, 128:256], yl[:, :, :, 1, 0:128], ALU.add), t, fr)
            ta = dve(lambda e: e.tensor_copy(yc[0:1, 0, 0], yl[0:1, 0, :, 0, 0:128]), ta, tb)
            tb = dve(lambda e: e.tensor_copy(yc[0:1, 1, 0], yl[0:1, 0, :, 1, 128:256]), tb)
            YL.free[i] = tb
            for jt in range(4):
                pi, p, fr = bank.take()
                for c in range(2):
                    for a in range(8):
                        k = (a >= 4) ^ c
                        tp = pe(lambda e: e.matmul(p[0:G, 256 * c:256 * c + 256], IV[:, c, a, G * jt:G * jt + G],
                                                   yc[:, int(k), a], start=a == 0, stop=a == 7),
                                fr, ta, tb, tf, tick=a == 7)
                si, s2, fr = S2.take()
                t = act(lambda e: e.activation(s2[:, :], p[0:G, 256:512], ACT.Copy), tp, fr)
                xi, tt, fr = TT.take()
                t1 = dve(lambda e: e.tensor_tensor(tt[:, 0], p[0:G, 0:256], s2[:, :], ALU.add), t, fr)
                t3 = dve(lambda e: e.tensor_tensor(tt[:, 1], p[0:G, 0:256], s2[:, :], ALU.subtract), t)
                bank.free[pi], S2.free[si] = t3, t3
                dve(lambda e: e.scalar_tensor_tensor(rn[:, 0, jt], tt[:, 0], w[0:G, 8 + jt:9 + jt], rn[:, 0, jt],
                                                     ALU.mult, ALU.add), t1, t2)
                pi, p, fr = bank.take()
                t = pe(lambda e: e.matmul(p[0:G, 0:256], rev[:, :], tt[:, 1], start=True, stop=True), t3, fr)
                TT.free[xi] = t
                t = dve(lambda e: e.scalar_tensor_tensor(rn[:, 1, 3 - jt], p[0:G, 0:256], w[0:G, 15 - jt:16 - jt],
                                                         rn[:, 1, 3 - jt], ALU.mult, ALU.add), t)
                bank.free[pi] = t
            YC.free[ci] = tp
            for k in range(2):
                to = sp.dma(lo[j], lambda e: e.dma_start(rows(b, k, pp, out), rn[:, k]), t)
            RN.free[j] = to
        sp.wait(*[l.all() for l in lo])


def tables():
    NP_, J = 1568, 784
    even = np.arange(0, 784, 2)
    odd = np.arange(1, 784, 2)
    slots = np.concatenate([even, odd])
    j = np.arange(392)[:, None] + 0.5
    th = lambda a, f: 2 * np.pi * a * f / NP_
    fe, fo = even[None, :].astype(float), odd[None, :].astype(float)
    fi = fe.copy()
    fi[0, 0] = 784.0
    Fe = np.concatenate([np.cos(th(j, fe)), -np.sin(th(j, fo))], 1)
    Fo = np.concatenate([np.cos(th(j, fo)), -np.sin(th(j, fi))], 1)
    fwd = np.stack([Fe, Fo], 0).reshape(2, 4, 98, 784).transpose(2, 0, 1, 3)
    jj = np.arange(784)[:, None].astype(float)
    fs = slots[None, :].astype(float)
    V = np.empty((784, 784, 2))
    V[:, :, 0] = np.cos(th(jj, fs))
    V[:, :, 1] = -np.sin(th(jj, fs))
    V[:, 0, 1] = np.cos(th(jj[:, 0], 784.0))
    vdft = V.reshape(8, 98, 1568).transpose(1, 0, 2)
    tc, ts = np.cos(th(1.0, slots)), np.sin(th(1.0, slots))
    tci = tc.copy()
    tci[0] = -1.0
    tw = np.stack([tc, ts, tci])
    w = np.full(784, 2.0)
    w[0] = 1.0
    jr = np.arange(392)[None, :] + 0.5
    ev, od = slots[:392, None].astype(float), slots[392:, None].astype(float)
    wc = w[:392, None] / NP_
    evi = ev.copy()
    evi[0, 0] = 784.0
    C1 = np.concatenate([wc * np.cos(th(jr, ev)), -2.0 / NP_ * np.sin(th(jr, od))])
    C2 = np.concatenate([-wc * np.sin(th(jr, evi)), 2.0 / NP_ * np.cos(th(jr, od))])
    inv = np.stack([C1, C2], 0).reshape(2, 8, 98, 392).transpose(2, 0, 1, 3)
    f = lambda a: np.ascontiguousarray(a, dtype=np.float32)
    return f(fwd), f(vdft), f(tw), f(inv)


def shape_constants():
    fwd, vdft, tw, inv = tables()
    ar = np.zeros((2, 6, NCH, 2, FC, 2), np.float32)
    ar[:, 0:3, :, 0, :, 0] = 1
    ar[:, 0:3, 0, 0, 0, 1] = 1
    ar[0, 3:6, :, 1, :, 0] = 1
    ar[0, 3:6, 0, 1, 0, 1] = 1
    msk = np.array([[1.0 if J < 8 >> i else 0.0 for J in range(8)] for i in range(4)], np.float32)
    return {"c_id": np.eye(128, dtype=np.float32), "c_fwd": fwd, "c_vdft": vdft, "c_tw": tw, "c_inv": inv,
            "c_ar": ar.reshape(2, 6, NCH, 112), "c_msk": msk, "c_rev": np.eye(G, dtype=np.float32)[::-1]}


_INS = ['x', 'L0_conv_ln1_w', 'L0_conv_ln1_b', 'L0_conv_w_qkv', 'L0_conv_b_qkv', 'L0_conv_rpb', 'L0_conv_w_proj', 'L0_conv_b_proj', 'L0_conv_ln2_w', 'L0_conv_ln2_b', 'L0_conv_w_fc1', 'L0_conv_b_fc1', 'L0_conv_w_fc2', 'L0_conv_b_fc2', 'L1_attn_Wq', 'L1_attn_bq', 'L1_attn_Wk', 'L1_attn_bk', 'L1_attn_Wv', 'L1_attn_bv', 'L1_ffn_sigma', 'L1_ffn_phi', 'L1_ffn_M_u', 'L1_ffn_M_phi_plus', 'L1_ffn_M_phi_minus', 'L1_ffn_log_weights', 'L1_ffn_gumbel']


def kernel(**inputs):
    import numpy as _np
    import concourse.bacc as _bacc
    from concourse import mybir as _mybir
    from concourse.bass_utils import run_bass_kernel_spmd as _run

    nc = _bacc.Bacc("TRN2", target_bir_lowering=False, num_devices=1)
    arrays, args = {}, []
    consts = shape_constants()
    for name, a in [(n, inputs[n]) for n in _INS] + list(consts.items()):
        a = _np.ascontiguousarray(a)
        arrays[f"in_{name}_dram"] = a
        args.append(nc.dram_tensor(f"in_{name}_dram", a.shape, _mybir.dt.from_np(a.dtype), kind="ExternalInput").ap())
    args.append(nc.dram_tensor("out_0_dram", (4, 56, 56, 128), _mybir.dt.float32, kind="ExternalOutput").ap())
    program(nc, *args)
    r = _run(nc, [arrays], core_ids=[0])
    return r.results[0]["out_0_dram"]
```

```python
import concourse.bass as bass
from concourse import mybir
from concourse.alu_op_type import AluOpType as ALU
from contextlib import ExitStack
import numpy as np

F32 = mybir.dt.float32
BF16 = mybir.dt.bfloat16
I32 = mybir.dt.int32
ACT = mybir.ActivationFunctionType
NB, T, C, NH, HD = 4, 3136, 128, 4, 32
G = 98
NJ = 8
PW = 62
EPS = 1e-5
SC = HD ** -0.5
BIG = 1.0e30
L, FC, NCH, SLOTS = 4, 28, 28, 784
TERMS = [(0, 0), (0, 1), (1, 0), (0, 2), (1, 1), (2, 0), (1, 2)]
KT = 16 * len(TERMS) + 6


class Queue:

    def __init__(self, eng):
        self.eng, self.seen, self.sem, self.n = eng, {}, None, 0

    def on(self, sem):
        self.sem, self.n = sem, 0

    def wait(self, *tokens):
        for t in tokens:
            if t is not None and self.seen.get(t[2], 0) < t[1]:
                self.seen[t[2]] = t[1]
                self.eng.wait_ge(t[0], t[1])

    def __call__(self, fn, *after, tick=True):
        self.wait(*after)
        ins = fn(self.eng)
        if tick:
            self.n += 1
            ins.then_inc(self.sem, 1)
            return (self.sem, self.n, self.sem.num)
        return None

    def last(self):
        return (self.sem, self.n, self.sem.num)

    def dma(self, line, fn, *after):
        self.wait(*after)
        line.n += 16
        fn(self.eng).then_inc(line.sem, 16)
        return (line.sem, line.n, line.sem.num)


class Line:

    def __init__(self, sem):
        self.sem, self.n = sem, 0

    def all(self):
        return (self.sem, self.n, self.sem.num)


class Ring:

    def __init__(self, bufs):
        self.bufs, self.free, self.i = bufs, [None] * len(bufs), -1

    def take(self):
        n = len(self.bufs)
        self.i = next((self.i + k) % n for k in range(1, n + 1) if self.free[(self.i + k) % n] != "in use")
        free, self.free[self.i] = self.free[self.i], "in use"
        return self.i, self.bufs[self.i], free

    def none(self):
        return all(f == "in use" for f in self.free)


def program(nc, x, ln1_w, ln1_b, w_qkv, b_qkv, rpb, w_proj, b_proj, ln2_w, ln2_b, w_fc1, b_fc1, w_fc2, b_fc2,
            Wq, bq, Wk, bk, Wv, bv, sigma, phi, M_u, M_pp, M_pm, log_w, gumbel,
            c_id, c_fwd, c_vdft, c_tw, c_inv, c_ar, c_msk, c_rev, out):
    with ExitStack() as ctx:
        nsem = [0]

        def sem(tag="s"):
            nsem[0] += 1
            return ctx.enter_context(nc.semaphore(f"{tag}{nsem[0]}"))

        def line(tag="l"):
            return Line(sem(tag))

        pe, act, dve, pool, sp = (Queue(e) for e in (nc.tensor, nc.scalar, nc.vector, nc.gpsimd, nc.sync))
        for q, n in ((pe, "pe"), (act, "act"), (dve, "dve"), (pool, "pool")):
            q.on(sem(n))

        dr = lambda name, shape, dt=F32: nc.dram_tensor(name, shape, dt, kind="Internal").ap()
        Vd = dr("Vd", [NB, PW, PW, C])
        biasD = dr("biasD", [NH, 64, 196])
        T2 = dr("T2", [NB, SLOTS, 512])
        Un = dr("Un", [NB, SLOTS, 512])
        Ud = dr("Ud", [128, NB, SLOTS * 8])
        Yd = dr("Yd", [SLOTS, 32, 256])
        Mbf = dr("Mbf", [2, 3, 16, 16384], BF16)
        MUd = dr("MUd", [3, 3, 16384], BF16)

        VbD = dr("VbD", [2, KT, NCH, 112], BF16)
        banks = ctx.enter_context(nc.psum_tensor("banks", [128, 8 * 512], F32))
        psum = [banks[:, 512 * i:512 * i + 512] for i in range(8)]
        wsel = ctx.enter_context(nc.sbuf_tensor("wsel", [128, 24], F32))
        rev = ctx.enter_context(nc.sbuf_tensor("rev", [G, G], F32))
        zone = ctx.enter_context(nc.sbuf_tensor("zone", [128, 16384], F32))

        def settle(*lines):
            ends = [q.last() for q in (pe, act, dve, pool)] + [ln.all() for ln in lines]
            for q in (pe, act, dve, pool, sp):
                q.wait(*ends)

        P = dict(nc=nc, ctx=ctx, line=line, pe=pe, act=act, dve=dve, pool=pool, sp=sp, banks=banks, psum=psum,
                 wsel=wsel, rev=rev, zone=zone, Vd=Vd, biasD=biasD, T2=T2, Un=Un, Ud=Ud, Yd=Yd, Mbf=Mbf, MUd=MUd, VbD=VbD,
                 x=x, ln1_w=ln1_w, ln1_b=ln1_b, w_qkv=w_qkv, b_qkv=b_qkv, rpb=rpb, w_proj=w_proj, b_proj=b_proj,
                 ln2_w=ln2_w, ln2_b=ln2_b, w_fc1=w_fc1, b_fc1=b_fc1, w_fc2=w_fc2, b_fc2=b_fc2,
                 Wq=Wq, bq=bq, Wk=Wk, bk=bk, Wv=Wv, bv=bv, sigma=sigma, phi=phi, M_u=M_u, M_pp=M_pp, M_pm=M_pm,
                 log_w=log_w, gumbel=gumbel, c_id=c_id, c_fwd=c_fwd, c_vdft=c_vdft, c_tw=c_tw, c_inv=c_inv,
                 c_ar=c_ar, c_msk=c_msk, c_rev=c_rev, out=out)
        phase_ab(P)
        settle(*P["ends_ab"])
        phase_freq(P)
        settle(*P["ends_freq"])
        phase_inv(P)


def phase_ab(P):
    nc, line = P["nc"], P["line"]
    pe, act, dve, pool, sp, psum = P["pe"], P["act"], P["dve"], P["pool"], P["sp"], P["psum"]
    Vd, biasD, T2, Un = P["Vd"], P["biasD"], P["T2"], P["Un"]
    with ExitStack() as c2:
        sb = lambda name, shape, dt=F32: c2.enter_context(nc.sbuf_tensor(name, shape, dt))
        XR_ = sb("XR", [G, 3 * NJ, 512])
        qT = [sb(f"qT{i}", [128, T]) for i in range(2)]
        kP = [sb(f"kP{i}", [128, PW, PW]) for i in range(2)]
        mx = Ring([sb(f"mx{i}", [128, 6]) for i in range(4)])
        st = Ring([sb(f"st{i}", [G, 4, 6]) for i in range(2)])
        col = sb("col", [128, 16])
        ident = sb("ident", [128, 128])

        def carve(buf):
            at = [0]

            def part(dims, parts=128):
                n = int(np.prod(dims))
                v = buf[0:parts, at[0]:at[0] + n]
                at[0] += n
                if len(dims) == 2:
                    return v.rearrange("p (a b) -> p a b", a=dims[0])
                if len(dims) == 3:
                    return v.rearrange("p (a b c) -> p a b c", a=dims[0], b=dims[1])
                return v
            return part

        part = carve(P["zone"])
        oT = part([T])
        XN = Ring([part([4, 132], G) for i in range(5)])
        XT = Ring([part([392]) for i in range(4)])
        VS = Ring([part([512], G) for i in range(2)])
        HT = Ring([part([4, 392]) for i in range(2)])
        mv = part([NB * NJ, 4, 2], G)
        rs = part([4, NB * NJ, 4], G)
        nw = Ring([part([4, 4], G) for i in range(2)])
        wqkv, wpr, wf1, wf2, wl1 = part([384]), part([128]), part([512]), part([4, 128]), part([3, 128])
        biasN = part([2, 196])
        rowb = part([6, 128])
        kv = part([5, 128])
        ones = part([128])
        W = sb("W", [128, 9280])
        part = carve(W)
        Qs = [part([7, NH, 64]) for i in range(2)]
        SB = Ring([part([2, 196]) for i in range(2)])
        PB = Ring([part([2, 196]) for i in range(3)])
        PN = Ring([part([2, 196]) for i in range(3)])
        PT = Ring([part([512], G) for i in range(3)])
        VC = Ring([part([2, 128], G) for i in range(4)])
        zero = SB.bufs[0]

        ld, ldx = line("ld"), [line("ldx") for _ in range(NB)]
        cw = lambda a: a.rearrange("(p o) -> p o", o=1)
        def row(g):
            return XR_[:, g % (3 * NJ), :]

        def load_x(b, *after):
            s0 = NJ * (b % 3)
            return sp.dma(ldx[b], lambda e: e.dma_start(XR_[:, s0:s0 + NJ, :], P["x"][b].rearrange(
                "(J r) w c -> (J r w c)", r=7).rearrange("(J j x) -> j J x", J=NJ, j=G)), *after)

        la = line("la0")
        t_x = {0: load_x(0)}
        sp.dma(la, lambda e: e.dma_start(ident[:, :], P["c_id"]))
        sp.dma(la, lambda e: e.dma_start(wqkv[:, :], P["w_qkv"]))
        for i, a in enumerate((P["ln1_w"], P["ln1_b"], P["b_qkv"][0:128], P["b_qkv"][128:256])):
            sp.dma(la, lambda e: e.dma_start(col[:, i:i + 1], cw(a)))
        t_la = la.all()
        row_in = lambda i, a: sp.dma(ld, lambda e: e.dma_start(
            rowb[:, i, :], a.rearrange("(o p) -> o p", o=1).broadcast_to([128, 128])))
        row_in(0, P["b_qkv"][256:384])
        t_bv = ld.all()
        ld = line("ld")
        t_o0 = None
        for i in range(5):
            t_o0 = pool(lambda e, i=i: e.memset(XN.bufs[i][:, :, 128:129], 1.0))
        t_z = pool(lambda e: e.memset(biasN[:, :, :], BIG))
        t_z0 = pool(lambda e: e.memset(zero[:, :, :], 0.0))
        lb = line("lb")
        sp.dma(lb, lambda e: e.dma_start(biasD.rearrange("(a h) q k -> (h q) a k", a=2), biasN[:, :, :]), t_z)
        lz, lr = line("lz"), line("lr")
        t_raw = t_ld = None

        def setup():
            nonlocal t_raw, t_ld
            t_b0 = lb.all()
            for h in range(NH):
                for qi in range(8):
                    def f(e, h=h, qi=qi):
                        dst = bass.AP(biasD.tensor, h * 12544 + qi * 1582, [[197, 8], [14, 7], [1, 7]])
                        src = bass.AP(P["rpb"].tensor, h * 49, [[0, 8], [7, 7], [1, 7]])
                        return e.dma_start(dst, src)
                    sp.dma(lr, f, t_b0)
                    yield
            for b in range(NB):
                for rr in ((0, 3), (PW - 3, 3)):
                    sp.dma(lz, lambda e: e.dma_start(
                        Vd[b, rr[0]:rr[0] + 3].rearrange("r w c -> (r w c)").rearrange("(p n) -> p n", p=93),
                        zero.rearrange("p a b -> p (a b)")[0:93, 0:256]), t_z0)
                    yield
                for cc in (0, PW - 3):
                    sp.dma(lz, lambda e: e.dma_start(
                        Vd[b, 3:PW - 3, cc:cc + 3, :].rearrange("r w c -> r (w c)"),
                        zero.rearrange("p a b -> p (a b)")[0:56, 0:384]), t_z0)
                    yield
            t_raw = sp.dma(lb, lambda e: e.dma_start(
                biasN[:, :, :], biasD.rearrange("(a h) q k -> (h q) a k", a=2)), lr.all())
            t_x[1] = load_x(1)
            for i, a in enumerate((P["ln2_w"], P["ln2_b"])):
                sp.dma(ld, lambda e: e.dma_start(col[:, 4 + i:5 + i], cw(a)))
                yield
            for i in range(4):
                sp.dma(ld, lambda e: e.dma_start(col[:, 6 + i:7 + i], cw(P["b_fc1"][128 * i:128 * i + 128])))
                yield
            for i, a in enumerate((P["b_proj"], P["b_fc2"], P["bq"], P["bk"], P["bv"])):
                row_in(1 + i, a)
                yield
            sp.dma(ld, lambda e: e.dma_start(wpr, P["w_proj"]))
            sp.dma(ld, lambda e: e.dma_start(wf1, P["w_fc1"]))
            sp.dma(ld, lambda e: e.dma_start(wf2, P["w_fc2"].rearrange("(i p) c -> p i c", p=128)))
            yield
            for i, a in enumerate((P["Wq"], P["Wk"], P["Wv"])):
                sp.dma(ld, lambda e: e.dma_start(wl1[:, i, :], a))
                yield
            t_ld = ld.all()
            t_x[2] = load_x(2)

        t_k0 = [pool(lambda e: e.memset(kP[0][:, :, :], 0.0)), None]
        t_q0 = [None, None]
        t_one = pool(lambda e: e.memset(ones[:, :], 1.0))
        t_c = pool(lambda e: e.tensor_scalar(col[:, 10:11], col[:, 2:3], -SC, None, ALU.mult), t_la)
        gen = Ring([psum[0], psum[1], psum[5]])
        psS, psT = Ring(psum[2:4]), Ring(psum[4:5])
        po, pC = psum[6], psum[7]

        quick = []

        def rstd(k, g, t_mv):
            i, w, fr = nw.take()
            v, y = w[:, 0, :], rs[:, k, g, :]
            t = dve(lambda e: e.tensor_scalar(v, mv[:, g, :, 1], EPS, None, ALU.add), t_mv, fr)
            t = dve(lambda e: e.tensor_scalar(w[:, 1, :].bitcast(I32), v.bitcast(I32), 1, None,
                                              ALU.arith_shift_right), t)
            t = dve(lambda e: e.tensor_scalar(y.bitcast(I32), w[:, 1, :].bitcast(I32), -1, 0x5f3759df,
                                              ALU.mult, ALU.add), t)
            q = dve if quick else pool
            for _ in range(3):
                t = q(lambda e: e.tensor_tensor(w[:, 2, :], y, y, ALU.mult), t)
                t = q(lambda e: e.tensor_tensor(w[:, 2, :], w[:, 2, :], v, ALU.mult), t)
                t = q(lambda e: e.tensor_scalar(w[:, 2, :], w[:, 2, :], -0.5, 1.5, ALU.mult, ALU.add), t)
                t = q(lambda e: e.tensor_tensor(y, y, w[:, 2, :], ALU.mult), t)
            nw.free[i] = t
            if k in ON_ACT:
                m_ = mv[:, g, :, 0]
                t = q(lambda e: e.tensor_tensor(m_, m_, y, ALU.mult), t, t_mv)
                t = q(lambda e: e.tensor_scalar(m_, m_, -1.0, None, ALU.mult), t)
            return t

        def stats(g, t_src):
            i, s, fr = st.take()
            for m in range(4):
                t = dve(lambda e, m=m: e.bn_stats(s[:, m, :], row(g)[:, 128 * m:128 * m + 128]), t_src, fr, tick=m == 3)
            for m in range(4):
                t2 = dve(lambda e, m=m: e.bn_aggr(mv[:, g, m, :], s[:, m, :]), t, mv_free[g], tick=m == 3)
            st.free[i] = t2
            return t2

        ON_ACT = (0,)
        mv_free = [None] * (NB * NJ)

        def norm(k, g, t_r):
            i, n, fr = XN.take()
            for m in range(4 if k in ON_ACT else 0):
                t = act(lambda e, m=m: e.activation(n[:, m, 0:128], row(g)[:, 128 * m:128 * m + 128], ACT.Identity,
                                                    bias=mv[:, g, m, 0:1], scale=rs[:, k, g, m:m + 1]), t_r, fr, t_o0)
            for m in range(0 if k in ON_ACT else 4):
                t = dve(lambda e, m=m: e.tensor_scalar(n[:, m, 0:128], row(g)[:, 128 * m:128 * m + 128],
                                                        mv[:, g, m, 0:1], rs[:, k, g, m:m + 1],
                                                        ALU.subtract, ALU.mult), t_r, fr, t_o0)
            mv_free[g] = t
            return i, n, t

        def transposed(n, t_n):
            i, p, fr = gen.take()
            for m in range(4):
                t = pe(lambda e, m=m: e.transpose(p[:, G * m:G * m + G], n[:, m, 0:128], ident[0:G, 0:G]),
                       t_n, fr, t_la, tick=m == 3)
            return i, p, t

        q_free, k_free = [None, None], [None, None]
        q_done = {}
        v_done = {}
        lv = [line("lv") for _ in range(2)]
        t_x_cur = {}

        def qkv(b):
            while b >= 3 and (b - 3, NJ - 1) not in u_done:
                yield
            if b >= 3:
                t_x[b] = load_x(b, *[t for J in range(NJ) for t in (t2_done[b - 3, J], u_done[b - 3, J])])
            r = rstd(0, NJ * b, stats(NJ * b, t_x[b]))
            yield
            for J in range(NJ):
                g = NJ * b + J
                xi, n, t = norm(0, g, r)
                if J + 1 < NJ:
                    r = rstd(0, g + 1, stats(g + 1, t_x[b]))
                yield
                i, p, t = transposed(n, t)
                XN.free[xi] = t
                yield 0
                a, xt, fr = XT.take()
                t = act(lambda e: e.activation(xt.rearrange("c (j m) -> c m j", m=4),
                                               p[:, 0:392].rearrange("c (m j) -> c m j", m=4),
                                               ACT.Identity, bias=col[:, 1:2], scale=col[:, 0:1]), t, fr, t_la)
                gen.free[i] = t
                yield
                i, p, fr = gen.take()
                t1 = pe(lambda e: e.matmul(p[:, 0:392], wqkv[:, 0:128], xt[:, :], start=True, stop=True), t, fr)
                yield 0
                t2 = act(lambda e: e.activation(qT[b % 2][:, 392 * J:392 * J + 392], p[:, 0:392], ACT.Identity,
                                                bias=col[:, 10:11], scale=-SC), t1, t_c, q_free[b % 2])
                gen.free[i] = t2
                yield
                i, p2, fr = gen.take()
                t1 = pe(lambda e: e.matmul(p2[:, 0:392], wqkv[:, 128:256], xt[:, :], start=True, stop=True), fr)
                yield 0
                t3 = act(lambda e: e.activation(kP[b % 2][:, 3 + 7 * J:10 + 7 * J, 3:59],
                                                   p2[:, 0:392].rearrange("c (r w) -> c r w", w=56),
                                                   ACT.Identity, bias=col[:, 3:4]), t1, t_k0[b % 2], k_free[b % 2])
                gen.free[i] = t3
                q_done[b, J] = (t2, t3)
                yield
                i, p3, fr = gen.take()
                xm = xt.rearrange("c (j m) -> c m j", m=4)
                for m in range(4):
                    t1 = pe(lambda e, m=m: e.matmul(p3[0:G, 128 * m:128 * m + 128], xm[:, m, :], wqkv[:, 256:384],
                                                    start=True, stop=True), fr, tick=m == 3)
                XT.free[a] = t1
                yield 0
                vi, vs, vf = VS.take()
                t4 = dve(lambda e: e.tensor_tensor(vs.rearrange("j (m c) -> j m c", m=4),
                                                   p3[0:G, :].rearrange("j (m c) -> j m c", m=4),
                                                   rowb[0:G, 0:1, :].broadcast_to([G, 4, 128]), ALU.add), t1, vf, t_bv)
                gen.free[i] = t4
                ln = lv[vi]
                t5 = sp.dma(ln, lambda e: e.dma_start(
                    bass.AP(Vd.tensor, ((b * PW + 3 + 7 * J) * PW + 3) * C, [[PW * C, 7], [512, 14], [1, 512]]),
                    vs[:, :]), t4)
                VS.free[vi] = t5
                v_done[b, J] = t5
                yield

        lvc = [line("lvc") for _ in range(5)]
        o_free = [None] * NJ
        x2 = {}
        qs_free = [None, None]
        o_done = {}

        def spread(b, i):
            s = (7 * b + i) % 2
            src = qT[b % 2].rearrange("c (r w) -> c r w", w=56)[:, 8 * i:8 * i + 8, :].rearrange(
                "c r (x w) -> c x r w", w=8)
            for h in range(NH):
                hs = slice(32 * h, 32 * h + 32)
                t = pool(lambda e: e.tensor_copy(
                    Qs[s][hs, :, h, :].rearrange("c x (r w) -> c x r w", w=8), src[hs]),
                    pool.last(), t_q0[s], qs_free[s], *[q_done[b, min(7, (8 * i + d) // 7)][0] for d in (0, 7)])
            pool.wait(t)
            if i == 6:
                q_free[b % 2] = t
            return t

        tiles = [(b, i, jx) for b in range(NB) for i in range(7) for jx in range(7)]
        s_qs, s_po, ended = {}, [None], []
        h_s, h_m, h_e, h_p, h_t, h_o, h_v = {}, {}, {}, {}, {}, {}, {}

        def t_scores(n):
            b, i, jx = tiles[n]
            nxt = n + 4
            if jx == 3 and nxt < len(tiles) and tiles[nxt][0] == b:
                s_qs[b, i + 1] = spread(b, i + 1)
            if jx == 3 and i == 6 and (b + 1, 1) in q_done:
                s_qs[b + 1, 0] = spread(b + 1, 0)
            if jx == 0 and (b, i) not in s_qs:
                s_qs[b, i] = spread(b, i)
            si, S, fr = psS.take()
            kr = [q_done[b, J][1] for J in range(NJ)] if (i, jx) == (0, 0) else []
            for pr in range(2):
                t = pe(lambda e: e.matmul(
                    S[:, 196 * pr:196 * pr + 196], Qs[(7 * b + i) % 2][:, jx, 2 * pr:2 * pr + 2, :],
                    kP[b % 2][:, 8 * i:8 * i + 14, 8 * jx:8 * jx + 14], start=True, stop=True),
                    fr, s_qs[b, i], *kr, tick=pr == 1)
            if jx == 6:
                qs_free[(7 * b + i) % 2] = t
            if (i, jx) == (6, 6):
                k_free[b % 2] = t
                ended.append(b)
            h_s[n] = (si, S, t)

        def t_max(n):
            si, S, t = h_s.pop(n)
            bi, sbf, f1 = SB.take()
            mi, m_, f2 = mx.take()
            for pr in range(2):
                td = dve(lambda e: e.tensor_tensor_reduce(
                    out=sbf[:, pr, :], in0=S[:, 196 * pr:196 * pr + 196], in1=biasN[:, pr, :], scale=1.0,
                    scalar=3.0e38, op0=ALU.add, op1=ALU.min, accum_out=m_[:, pr:pr + 1]),
                    t, f1, f2, t_bias)
            psS.free[si] = td
            pi, pb, f3 = PB.take()
            for pr in range(2):
                ta = act(lambda e: e.activation(
                    pb[:, pr, :], sbf[:, pr, :], ACT.Exp, bias=m_[:, pr:pr + 1], scale=-1.0,
                    accum_out=m_[:, 2 + pr:3 + pr]), td, f3)
            SB.free[bi] = ta
            h_m[n] = (pi, pb, mi, m_, ta)

        def t_norm(n):
            pi, pb, mi, m_, ta = h_m.pop(n)
            tr = dve(lambda e: e.reciprocal(m_[:, 4:6], m_[:, 2:4]), ta)
            ni, pn, f4 = PN.take()
            for pr in range(2):
                tp = dve(lambda e: e.tensor_scalar(
                    pn[:, pr, :], pb[:, pr, :], m_[:, 4 + pr:5 + pr], None, ALU.mult), tr, f4)
            PB.free[pi], mx.free[mi] = tp, tp
            h_e[n] = (ni, pn, tp)

        def t_turn(n):
            ni, pn, tp = h_e.pop(n)
            ti, pt, fr = psT.take()
            for c in range(2):
                for pr in range(2):
                    t = pe(lambda e: e.transpose(
                        pt[0:G, 256 * c + 128 * pr:256 * c + 128 * pr + 128],
                        pn[:, pr, G * c:G * c + G], ident[:, :]), tp, fr, tick=(c, pr) == (1, 1))
            PN.free[ni] = t
            h_t[n] = (ti, pt, t)

        def t_keep(n):
            ti, pt, t = h_t.pop(n)
            oi, ob, fo = PT.take()
            t = act(lambda e: e.activation(ob[:, :], pt[0:G, :], ACT.Copy), t, fo)
            psT.free[ti] = t
            h_o[n] = (oi, ob, t)

        def t_values(n):
            b, i, jx = tiles[n]
            vi, vc, fr = VC.take()
            need = [v_done[b, J] for J in range(NJ)] if (i, jx) == (0, 0) else []
            for c in range(2):
                t = sp.dma(lvc[vi], lambda e: e.dma_start(
                    vc[:, c, :], Vd[b, 8 * i + 7 * c:8 * i + 7 * c + 7, 8 * jx:8 * jx + 14, :]),
                    fr, lz.all(), *need)
            h_v[n] = (vi, vc, t)

        def t_out(n):
            b, i, jx = tiles[n]
            oi, ob, t = h_o.pop(n)
            vi, vc, tv = h_v.pop(n)
            for c in range(2):
                for h in range(NH):
                    t1 = pe(lambda e: e.matmul(
                        po[32 * h:32 * h + 32, 64 * jx:64 * jx + 64], vc[:, c, 32 * h:32 * h + 32],
                        ob[:, 256 * c + 64 * h:256 * c + 64 * h + 64], start=c == 0, stop=c == 1,
                        tile_position=(0, 32 * h)),
                        t, tv, s_po[0], tick=(c, h) == (1, 3))
            PT.free[oi], VC.free[vi] = t1, t1
            if jx == 6:
                fr = [o_free[J] for J in range(NJ) if 7 * J < 8 * i + 8 and 7 * J + 7 > 8 * i]
                t = act(lambda e: e.activation(
                    oT.rearrange("c (r w) -> c r w", w=56)[:, 8 * i:8 * i + 8, :].rearrange(
                        "c r (x w) -> c x r w", w=8),
                    po[:, 0:448].rearrange("c (x r w) -> c x r w", r=8, w=8), ACT.Copy), t1, *fr)
                s_po[0] = t
                o_done[b, i] = t
                for J in [i] if i < 6 else [6, 7]:
                    back.append(("mlp", mlp(b, J)))
                if i == 6:
                    back.append(("attn", attn(b)))

        back, qk, live = [], [], []
        LANES = 4

        def pick(back):
            while back:
                kind = back[0][0]
                kinds = [k for k, _ in live]
                if len(live) >= LANES or kind == "attn" and "mlp" in kinds or kinds.count("mlp") == 2 and kind == "mlp" or kind in kinds and kind != "mlp":
                    break
                live.append(back.pop(0))
            todo = ([qk[0]] if qk else []) + live
            k = max(1, len(todo) - 3)
            return todo[0:k], todo[k:]

        LATER = 2
        later = []

        def advance(item):
            if item in later:
                later.remove(item)
                return 0
            try:
                r = next(item[1])
                if r == LATER:
                    later.append(item)
                return r
            except StopIteration:
                (qk if item[0] == "qkv" else live).remove(item)
                return None

        def unit(tile_a=(), tile_b=()):
            g1, g2 = pick(back)
            mid = [item for item in g1 if advance(item) == 0]
            for f in tile_a:
                f()
            for item in mid:
                advance(item)
            mid = [item for item in g2 if advance(item) == 0]
            for f in tile_b:
                f()
            for item in mid:
                advance(item)
            return bool(g1)

        def add_rows(k, g, after):
            return pool(lambda e: e.tensor_tensor(
                row(g).rearrange("j (m c) -> j m c", m=4), row(g).rearrange("j (m c) -> j m c", m=4),
                rowb[0:G, k:k + 1, :].broadcast_to([G, 4, 128]), ALU.add), *after)

        def mlp(b, J):
            g = NJ * b + J
            ta = add_rows(1, g, [t_x[b], t_ld])
            i, p, fr = gen.take()
            om = oT[:, 392 * J:392 * J + 392].rearrange("c (j m) -> c m j", m=4)
            for m in range(4):
                t = pe(lambda e, m=m: e.matmul(p[0:G, 128 * m:128 * m + 128], om[:, m, :], wpr[:, :],
                                               start=True, stop=True), t_ld, fr, o_done[b, min(J, 6)], tick=m == 3)
            o_free[J] = t
            yield 0
            t = dve(lambda e: e.tensor_tensor(row(g), row(g), p[0:G, :], ALU.add), t, ta)
            gen.free[i] = t
            t = stats(g, t)
            t = rstd(1, g, t)
            if not quick:
                yield
                yield
            yield LATER
            xi, n, t = norm(1, g, t)
            ta = add_rows(2, g, [t])
            yield
            i, p, t = transposed(n, t)
            XN.free[xi] = t
            yield 0
            while XT.none():
                yield 0
            a, xt, fr = XT.take()
            t = act(lambda e: e.activation(xt[:, :], p[:, 0:392], ACT.Identity, bias=col[:, 5:6],
                                           scale=col[:, 4:5]), t, fr, t_ld)
            gen.free[i] = t
            yield
            th = []
            while HT.none():
                yield
            hi, hT, hf = HT.take()
            for f in range(4):
                i, p, fr = gen.take()
                t1 = pe(lambda e, f=f, p=p: e.matmul(p[:, 0:392], wf1[:, 128 * f:128 * f + 128], xt[:, :],
                                                     start=True, stop=True), t, fr)
                if f == 0:
                    yield 0
                t2 = act(lambda e, f=f, p=p: e.activation(hT[:, f, :], p[:, 0:392], ACT.Gelu,
                                                          bias=col[:, 6 + f:7 + f]), t1, hf)
                gen.free[i] = t2
                th.append(t2)
            XT.free[a] = t1
            yield
            i, p, fr = gen.take()
            for m in range(4):
                for f in range(4):
                    t = pe(lambda e, m=m, f=f: e.matmul(p[0:G, 128 * m:128 * m + 128], hT[:, f, G * m:G * m + G],
                                                        wf2[:, f, :], start=f == 0, stop=f == 3),
                           fr, th[f], tick=(m, f) == (3, 3))
            HT.free[hi] = t
            yield 0
            t = dve(lambda e: e.tensor_tensor(row(g), row(g), p[0:G, :], ALU.add), t, ta)
            gen.free[i] = t
            t = stats(g, t)
            t = rstd(2, g, t)
            if not quick:
                yield
                yield
            yield LATER
            xi, n, t = norm(2, g, t)
            yield
            for m in range(4):
                t = pe(lambda e, m=m: e.matmul(pC[:, 0:129], n[:, m, 0:128], n[:, m, 0:129],
                                               start=(J, m) == (0, 0), stop=(J, m) == (NJ - 1, 3)),
                       t, c_free[0], tick=m == 3)
            XN.free[xi] = t
            x2[g] = t
            yield

        c_free = [None]
        t2_done, u_done = {}, {}
        lt2 = [line("lt2") for _ in range(NJ)]
        kv_free = [None, None]
        lst = [line("lst") for _ in range(5)]

        def attn(b):
            tc = x2[NJ * b + NJ - 1]
            Cs, S1 = kv[:, 0, :], kv[:, 4, 0:1]
            t = act(lambda e: e.activation(Cs, pC[:, 0:128], ACT.Copy), tc, *kv_free)
            t = act(lambda e: e.activation(S1, pC[:, 128:129], ACT.Copy), tc, *kv_free)
            c_free[0] = t
            ts = pool(lambda e: e.tensor_scalar(kv[:, 1, :], ones[:, :], S1, None, ALU.mult), t, t_one)
            i, p, fr = gen.take()
            t1 = pe(lambda e: e.matmul(p[:, 0:128], Cs, wl1[:, 2, :], start=True, stop=True), t, fr)
            t1 = pe(lambda e: e.matmul(p[:, 128:256], kv[:, 1, :], wl1[:, 2, :], start=True, stop=True), ts)
            t2 = dve(lambda e: e.scalar_tensor_tensor(kv[:, 2, :], rowb[:, 5, :], S1, p[:, 0:128],
                                                      ALU.mult, ALU.add), t1, *kv_free)
            t2 = dve(lambda e: e.tensor_tensor(kv[:, 2, :], kv[:, 2, :], wl1[:, 1, :], ALU.mult), t2)
            t3 = dve(lambda e: e.scalar_tensor_tensor(kv[:, 3, :], rowb[:, 5, :], float(T), p[:, 128:256],
                                                      ALU.mult, ALU.add), t1)
            t3 = dve(lambda e: e.tensor_tensor(kv[:, 3, :], kv[:, 3, :], rowb[:, 4, :], ALU.mult), t3)
            gen.free[i] = t3
            yield
            i, p, fr = gen.take()
            t = pe(lambda e: e.matmul(p[:, 0:128], ones[:, :], kv[:, 2, :], start=True, stop=True), t2, fr)
            t = dve(lambda e: e.tensor_tensor(kv[:, 3, :], kv[:, 3, :], p[:, 0:128], ALU.add), t, t3)
            gen.free[i] = t
            tw = dve(lambda e: e.tensor_tensor(kv[:, 2, :], kv[:, 3, :], wl1[:, 0, :], ALU.mult), t)
            tb = dve(lambda e: e.tensor_tensor(kv[:, 4, :], kv[:, 3, :], rowb[:, 3, :], ALU.mult), t)
            yield
            for J in range(NJ):
                g = NJ * b + J
                xi, n, t = norm(2, g, x2[g])
                yield
                ta = pool(lambda e: e.tensor_tensor(
                    row(g).rearrange("j (m c) -> j m c", m=4), row(g).rearrange("j (m c) -> j m c", m=4),
                    kv[0:G, 4:5, :].broadcast_to([G, 4, 128]), ALU.add), t, tb)
                i, p, t = transposed(n, t)
                XN.free[xi] = t
                yield 0
                a, xt, fr = XT.take()
                t = act(lambda e: e.activation(xt[:, :], p[:, 0:392], ACT.Copy), t, fr)
                gen.free[i] = t
                yield
                i, p, fr = gen.take()
                for m in range(4):
                    t = pe(lambda e, m=m: e.matmul(p[0:G, 128 * m:128 * m + 128], xt[:, G * m:G * m + G], kv[:, 2, :],
                                                   start=True, stop=True), fr, t, tw, tick=m == 3)
                XT.free[a] = t
                kv_free[:] = t, ta
                yield 0
                t = dve(lambda e: e.tensor_tensor(row(g), row(g), p[0:G, :], ALU.add), t, ta)
                gen.free[i] = t
                t2_done[b, J] = sp.dma(lt2[J], lambda e: e.dma_start(T2[b, G * J:G * J + G, :], row(g)), t)
                t = stats(g, t)
                t = rstd(3, g, t)
                if not quick:
                    yield
                    yield
                yield LATER
                xi, n, t = norm(3, g, t)
                u_done[b, J] = t
                t = sp.dma(lst[xi], lambda e: e.dma_start(
                    Un[b, G * J:G * J + G, :].rearrange("j (m c) -> j m c", m=4), n[:, :, 0:128]), t)
                XN.free[xi] = t
                yield

        lf, lu, lou = line("lf"), [line("lu") for _ in range(2)], [line("lou") for _ in range(2)]
        fwd_state = {}

        def forward(images):
            F = XR_[:, 8:24, :].rearrange("p a b -> p (a b)")[:, 0:6272].rearrange("p (c a x) -> p c a x", c=2, a=4)
            U = [v.rearrange("d (s m r) -> d s m r", m=4, r=2)
                 for v in (kP[1].rearrange("p a b -> p (a b)")[:, 0:3136], qT[1][:, :])]
            first = not fwd_state
            if first:
                sp.dma(lf, lambda e: e.dma_start(P["rev"][:, :], P["c_rev"]))
                fwd_state["F"] = sp.dma(lf, lambda e: e.dma_start(F, P["c_fwd"]),
                                        *[t[2, J] for t in (t2_done, u_done) for J in range(NJ)])
                part = carve(W)
                for k in ("A", "R", "E", "O"):
                    fwd_state[k] = Ring([part([4, 256], G) for _ in range(2)])
                    fwd_state[k].free = [None, None]
                fwd_state["bank"] = Ring([psum[2], psum[3], psum[4], psum[6]])
                fwd_state["U"] = [None, None]
                for q in (sp, pe, act, dve):
                    q.wait(act.last(), dve.last(), pe.last(), pool.last(), *[l.all() for l in lvc])
            tf, bank, u_free = fwd_state["F"], fwd_state["bank"], fwd_state["U"]
            UA, UR, EV, OD = (fwd_state[k] for k in ("A", "R", "E", "O"))
            jobs, got = [(b, mp) for b in images for mp in range(2)], {}
            stored = [l.all() for l in lst]

            def load(n):
                if n >= len(jobs):
                    return
                b, mp = jobs[n]
                i, ua, fr = UA.take()
                i, ur, fr2 = UR.take()
                cs = slice(256 * mp, 256 * mp + 256)
                rows = lambda k: Un[b, 392 * k:392 * k + 392, cs].rearrange("(a p) x -> p a x", p=G)
                sp.dma(lu[i], lambda e: e.dma_start(ua, rows(0)), fr, fr2, *stored)
                t = sp.dma(lu[i], lambda e: e.dma_start(ur, rows(1)))
                got[n] = i, ua, ur, t

            load(0)
            load(1)
            for _ in range(8 if first else 1):
                yield
            for n, (b, mp) in enumerate(jobs):
                if n:
                    load(n + 1)
                i, ua, ur, t = got.pop(n)
                ei, ev, fr = EV.take()
                oi, od, fr2 = OD.take()
                for a in range(0, 4, 2):
                    pi, p, fp = bank.take()
                    for k in range(2):
                        tp = pe(lambda e: e.matmul(p[0:G, 256 * k:256 * k + 256], P["rev"][:, :], ur[:, 3 - a - k, :],
                                                   start=True, stop=True), t, fp, tf, tick=k == 1)
                    pv = p[0:G, :].rearrange("p (a x) -> p a x", a=2)
                    t0 = dve(lambda e: e.tensor_tensor(ev[:, a:a + 2, :], ua[:, a:a + 2, :], pv, ALU.add), tp, t, fr)
                    t1 = dve(lambda e: e.tensor_tensor(od[:, a:a + 2, :], ua[:, a:a + 2, :], pv, ALU.subtract), fr2)
                    bank.free[pi] = t1
                    yield
                UA.free[i], UR.free[i] = t1, tp
                for blk in range(2):
                    for m in range(2):
                        for c, (src, ts) in enumerate(((ev, t0), (od, t1))):
                            half = c ^ blk
                            pi, p, fr = bank.take()
                            for a in range(4):
                                tp = pe(lambda e: e.matmul(p[:, 0:392], src[:, a, 128 * m:128 * m + 128],
                                                           F[:, c, a, 392 * half:392 * half + 392],
                                                           start=a == 0, stop=a == 3), ts, fr, tf, tick=a == 3)
                            dst = U[blk][:, :, 2 * mp + m, half]
                            bank.free[pi] = act(lambda e: e.activation(dst, p[:, 0:392], ACT.Copy), tp, u_free[blk])
                            yield
                    if mp == 1:
                        u_free[blk] = sp.dma(lou[blk], lambda e: e.dma_start(
                            P["Ud"][:, b, 3136 * blk:3136 * blk + 3136], U[blk].rearrange("d s m r -> d (s m r)")),
                            bank.free[pi])
                EV.free[ei], OD.free[oi] = tp, tp

        def load_m(ends):
            lm = line("lm2")
            M = P["zone"][:, :].bitcast(BF16).rearrange("p (a x) -> p a x", a=2)
            sp.wait(*ends, *[l.all() for l in lst + lt2 + lv + P["ends_prep"]])
            for par in range(2):
                for k, (m, _) in enumerate(TERMS):
                    sp.dma(lm, lambda e: e.dma_start(M[16 * k:16 * k + 16, par, :], P["Mbf"][par, m]))
                for r, tap in ((112, par), (115, 2)):
                    sp.dma(lm, lambda e: e.dma_start(M[r:r + 3, par, :], P["MUd"][:, tap, :]))
            P["t_m"] = lm.all()

        small = setup()
        for n, _ in enumerate(qkv(0)):
            if n == 6:
                t_q0[:] = [pool(lambda e: e.memset(Qs[i], 0.0)) for i in range(2)]
            if n == 24:
                t_k0[1] = pool(lambda e: e.memset(kP[1][:, :, :], 0.0))
            if (0, 1) in q_done and not s_qs:
                s_qs[0, 0] = spread(0, 0)
            if n > 1:
                next(small, None)
                next(small, None)
        for _ in small:
            pass
        SB.free[0] = lz.all()
        t_m = pool(lambda e: e.tensor_scalar(PB.bufs[0][:, :, :], biasN[:, :, :], 0.5 * BIG, None, ALU.is_lt), t_raw)
        t_m = pool(lambda e: e.tensor_scalar(PB.bufs[0][:, :, :], PB.bufs[0][:, :, :], -2.0, 1.0, ALU.mult, ALU.add), t_m)
        t_bias = pool(lambda e: e.tensor_tensor(biasN[:, :, :], biasN[:, :, :], PB.bufs[0][:, :, :], ALU.mult), t_m)
        PB.free[0] = t_bias
        first = ((0, t_scores), (3, t_turn), (1, t_max), (2, t_norm))
        second = ((5, t_out), (4, t_keep), (3, t_values))
        for n in range(len(tiles) + 5):
            if n < len(tiles) and n % 49 == 0:
                while qk:
                    unit()
                if n // 49 + 1 < NB:
                    qk.append(("qkv", qkv(n // 49 + 1)))
                else:
                    for q in (sp, pe, act, dve, pool):
                        q.wait(q_free[0], k_free[0])
                    qk.append(("qkv", prepare(P, qT[0], kP[0].rearrange("p a b -> p (a b)"),
                                              gen)))
            now = [[(lambda s=s, k=n - lag: s(k)) for lag, s in part if 0 <= n - lag < len(tiles)]
                   for part in (second, first)]
            unit(*now)
        quick.append(True)
        fw = forward([0, 1, 2])
        while unit([lambda: next(fw, None)] if (2, NJ - 1) in u_done else ()):
            pass
        for _ in fw:
            pass
        ends = [q.last() for q in (pe, act, dve, pool)]
        fw = forward([3])
        next(fw)
        load_m(ends)
        for _ in fw:
            pass
        P["ends_ab"] = lt2 + lst + lv + lu + P["ends_prep"]
        P["t_u"] = [l.all() for l in lou]
        P["t_ab"] = [l.all() for l in P["ends_ab"]]


def prepare(P, A, K0, gen):
    line = P["line"]
    pe, act, dve, pool, sp = P["pe"], P["act"], P["dve"], P["pool"], P["sp"]
    w = P["wsel"]
    ML = Ring([A[:, 512 * i:512 * i + 512] for i in range(2)])
    mp, mm, dif = (A[:, 1024 + 512 * i:1536 + 512 * i] for i in range(3))
    mo = Ring([A[:, 2560 + 256 * i:2816 + 256 * i].bitcast(BF16) for i in range(2)])
    vd = K0[0:G, 0:1792].rearrange("p (a x) -> p a x", a=8)
    ph = K0[0:G, 1792:2816].rearrange("p (a m k) -> p a m k", a=8, m=4)
    vf = K0[:, 2816:3040]
    lg, tm, sg = K0[:, 3040:3048], K0[:, 3080:3104], K0[:, 3104:3108]
    mk = K0[:, 3048:3080].rearrange("p (i j) -> p i j", i=4)
    la, lp = line("la"), line("lp")
    bc = lambda a: a.rearrange("(o p) -> o p", o=1).broadcast_to([128, 4])
    sp.dma(la, lambda e: e.dma_start(lg[:, 0:4], bc(P["log_w"])))
    sp.dma(la, lambda e: e.dma_start(lg[:, 4:8], bc(P["gumbel"])))
    t = sp.dma(la, lambda e: e.dma_start(mk, P["c_msk"].rearrange("(o i) j -> o i j", o=1).broadcast_to([128, 4, 8])))
    t_s1 = pool(lambda e: e.memset(sg, 1.0))
    t_p0 = pool(lambda e: e.memset(ph, 0.0))
    for q in range(4):
        sp.dma(lp, lambda e: e.dma_start(sg[32 * q:32 * q + 16, 0:1],
                                         P["sigma"].rearrange("(p o) -> p o", o=1)), t_s1)
    phv = P["phi"][0:3136].rearrange("(a j m) k -> j a m k", j=G, m=4)
    for a in range(8):
        sp.dma(lp, lambda e: e.dma_start(ph[:, a, :, 0:16], phv[:, a]), t_p0)
    t_ph = lp.all()
    yield
    z, y, eq, h = tm[:, 0:4], tm[:, 4:8], tm[:, 8:12], tm[:, 12:16]
    t = dve(lambda e: e.tensor_tensor(z, lg[:, 0:4], lg[:, 4:8], ALU.add), t)
    t = dve(lambda e: e.reduce_max(tm[:, 16:17], z, mybir.AxisListType.X), t)
    t = dve(lambda e: e.tensor_scalar(z, z, tm[:, 16:17], None, ALU.subtract), t)
    t = act(lambda e: e.activation(y, z, ACT.Exp, accum_out=tm[:, 17:18]), t)
    yield
    t = dve(lambda e: e.reciprocal(tm[:, 18:19], tm[:, 17:18]), t)
    t = dve(lambda e: e.tensor_scalar(y, y, tm[:, 18:19], None, ALU.mult), t)
    t = dve(lambda e: e.reduce_max(tm[:, 16:17], y, mybir.AxisListType.X), t)
    t = dve(lambda e: e.tensor_scalar(eq, y, tm[:, 16:17], None, ALU.is_ge), t)
    t = dve(lambda e: e.memset(tm[:, 20:21], 1.0), t)
    for i in range(4):
        t = dve(lambda e: e.tensor_tensor(h[:, i:i + 1], eq[:, i:i + 1], tm[:, 20:21], ALU.mult), t)
        t = dve(lambda e: e.tensor_tensor(tm[:, 20:21], tm[:, 20:21], h[:, i:i + 1], ALU.subtract), t)
    t = dve(lambda e: e.tensor_tensor(w[:, 0:4], h, y, ALU.subtract), t)
    t_w = dve(lambda e: e.tensor_tensor(w[:, 0:4], w[:, 0:4], y, ALU.add), t)
    t = dve(lambda e: e.tensor_scalar(w[:, 8:16], mk[:, 0, :], h[:, 0:1], None, ALU.mult), t_w)
    for i in range(1, 4):
        t = dve(lambda e: e.scalar_tensor_tensor(w[:, 8:16], mk[:, i, :], h[:, i:i + 1], w[:, 8:16],
                                                 ALU.mult, ALU.add), t)
    yield

    lm = [line("lm") for _ in range(2)]
    lo = [line("lo") for _ in range(2)]

    def split(src, n, t, dst):
        for i in range(3):
            oi, o, fr = mo.take()
            t1 = act(lambda e: e.activation(o[:, 0:n], src[:, 0:n], ACT.Copy), t, fr)
            mo.free[oi] = sp.dma(lo[oi], lambda e: e.dma_start(dst(i), o[:, 0:n]), t1)
            yield
            if i < 2:
                t = dve(lambda e: e.tensor_tensor(src[:, 0:n], src[:, 0:n], o[:, 0:n], ALU.subtract), t1)
        last[0] = t1

    last = [None]

    def mixed(dst, n, view, *t_free):
        t = None
        for i in range(4):
            li, m, fr = ML.take()
            t1 = sp.dma(lm[li], lambda e: e.dma_start(m[:, 0:n], view(i)), fr)
            if i % 2:
                yield
            if i == 0:
                t = dve(lambda e: e.tensor_scalar(dst[:, 0:n], m[:, 0:n], w[:, 0:1], None, ALU.mult), t1, t_w, *t_free)
            else:
                t = dve(lambda e: e.scalar_tensor_tensor(dst[:, 0:n], m[:, 0:n], w[:, i:i + 1], dst[:, 0:n],
                                                         ALU.mult, ALU.add), t1, t)
            ML.free[li] = t
        last[0] = t

    flat = lambda a: a.rearrange("k d e -> (k d e)").rearrange("(p x) -> p x", p=128)
    f0 = f1 = None
    for c in range(4):
        cs = slice(512 * c, 512 * c + 512)
        yield from mixed(mp, 512, lambda i: flat(P["M_pp"][i])[:, cs], f0)
        yield from mixed(mm, 512, lambda i: flat(P["M_pm"][i])[:, cs], f1)
        t = last[0]
        t1 = dve(lambda e: e.tensor_tensor(dif, mp, mm, ALU.subtract), t, f0, f1)
        t2 = dve(lambda e: e.tensor_tensor(mp, mp, mm, ALU.add), t1)
        for par, (s, t) in enumerate(((mp, t2), (dif, t1))):
            yield from split(s, 512, t, lambda i: P["Mbf"][par, i].rearrange("k x -> (k x)").rearrange(
                "(p x) -> p x", p=128)[:, cs])
            f0, f1 = (last[0], f1) if par == 0 else (f0, last[0])
    yield from mixed(mm, 384, lambda i: flat(P["M_u"][i]), f1)
    yield from split(mm, 384, last[0], lambda i: P["MUd"][i].rearrange("k x -> (k x)").rearrange("(p x) -> p x", p=128))

    for i in range(2):
        s, r = sg[:, i:i + 1], sg[:, i + 1:i + 2]
        t = act(lambda e: e.activation(r, s, ACT.Sqrt), t_ph, t if i else None)
        t = dve(lambda e: e.tensor_scalar(sg[:, 3:4], r, 1e-30, None, ALU.max), t)
        t = dve(lambda e: e.reciprocal(sg[:, 3:4], sg[:, 3:4]), t)
        t = dve(lambda e: e.tensor_tensor(sg[:, 3:4], sg[:, 3:4], s, ALU.mult), t)
        t = dve(lambda e: e.tensor_tensor(r, r, sg[:, 3:4], ALU.add), t)
        t = dve(lambda e: e.tensor_scalar(r, r, 0.5, None, ALU.mult), t)
        yield
    t_sig = t
    t_a = [last[0], f0, f1] + mo.free
    vp = [A[:, 784 * i:784 * i + 784].bitcast(BF16) for i in range(3)]
    lvd, tf, t_vd = line("lvd"), None, None
    lst = line("lst")
    for c in range(7):
        cs = slice(224 * c, 224 * c + 224)
        t = sp.dma(lvd, lambda e: e.dma_start(vd, P["c_vdft"][:, :, cs]), t_vd)
        yield
        i, p, fr = gen.take()
        for a in range(8):
            t_vd = pe(lambda e: e.matmul(p[:, 0:224], ph[:, a, :, :], vd[:, a, :], start=a == 0, stop=a == 7),
                      t, t_ph, fr, tick=a == 7)
        yield 0
        t = act(lambda e: e.activation(vf, p[:, 0:224], ACT.Copy, scale=sg[:, 2:3]), t_vd, t_sig, tf)
        gen.free[i] = t
        t = dve(lambda e: e.tensor_copy(vp[0][:, cs], vf), t, *t_a)
        for i in (1, 2):
            t = dve(lambda e: e.tensor_tensor(vf, vf, vp[i - 1][:, cs], ALU.subtract), t)
            t = dve(lambda e: e.tensor_copy(vp[i][:, cs], vf), t)
        tf = t
        yield
    for k, (_, v) in enumerate(TERMS):
        for q in range(4):
            sp.dma(lst, lambda e: e.dma_start(
                P["VbD"][q % 2, 16 * k:16 * k + 16, :, 56 * (q // 2):56 * (q // 2) + 56],
                vp[v][32 * q:32 * q + 16, :].rearrange("k (c x) -> k c x", c=NCH)), tf)
    lc = line("lc")
    for p in range(2):
        pool.dma(lc, lambda e: e.dma_start(P["VbD"][p, 112:118], P["c_ar"][p]))
    P["ends_prep"] = [lst, lc] + lo


def phase_freq(P):
    nc, line = P["nc"], P["line"]
    pe, act, dve, pool, sp = P["pe"], P["act"], P["dve"], P["pool"], P["sp"]
    banks, psum, Yd = P["banks"], P["psum"], P["Yd"]
    with ExitStack() as c2:
        sb = lambda name, shape, dt=F32: c2.enter_context(nc.sbuf_tensor(name, shape, dt))
        M = P["zone"][:, :].bitcast(BF16)[0:KT].rearrange("p (a d e) -> p a e d", a=2, e=128)
        Gm = sb("Gm", [128, 2, 112, 128])
        VS = Ring([sb(f"V{i}", [KT, 2, 112], BF16) for i in range(2)])
        TW = Ring([sb(f"TW{i}", [128, 3, FC]) for i in range(2)])
        UL = Ring([sb(f"UL{i}", [128, NB, FC, 8]) for i in range(1)])
        U7 = Ring([sb(f"U7{i}", [128, FC, 56]) for i in range(2)])
        tmp = sb("tmp", [128, FC, 3, 4])
        YS = Ring([sb(f"YS{i}", [128, 7, 256]) for i in range(1)])
        zb = sb("zb", [1, 512], BF16)
        t_zb = pool(lambda e: e.memset(zb[:, :], 0.0))
        t_m = P["t_m"]
        lv, lw, ll = [line("lvq") for _ in range(2)], [line("ltw") for _ in range(2)], line("lul")
        ly = line("ly")
        tiles = Ring(psum[0:4])
        ready = {}

        def load(ch):
            vi, v, fv = VS.take()
            tv = sp.dma(lv[vi], lambda e: e.dma_start(v[:, :, :], P["VbD"][:, :, ch, :].rearrange("a k x -> k a x")), fv)
            wi, w, fw = TW.take()
            tw = sp.dma(lw[wi], lambda e: e.dma_start(
                w[:, :, :], P["c_tw"][:, FC * ch:FC * ch + FC].rearrange("(o a) s -> o a s", o=1).broadcast_to([128, 3, FC])), fw)
            li, u, fl = UL.take()
            tu = sp.dma(ll, lambda e: e.dma_start(u.rearrange("d b s x -> d b (s x)"),
                                                  P["Ud"][:, :, FC * 8 * ch:FC * 8 * ch + FC * 8]),
                        fl, P["t_u"][min(ch, 1)])
            ui, u7, fu = U7.take()
            a = u7.rearrange("d s (m r b) -> d s m r b", m=7, r=2)
            s4 = u.rearrange("d b s (m r) -> d s m r b", m=4, r=2)
            t = pool(lambda e: e.tensor_copy(u7[:, :, 24:56].rearrange("d s (x b) -> d s x b", b=4),
                                             u.rearrange("d b s x -> d s x b")), tu, fu)
            cc = [w[:, k, :].rearrange("d (s o) -> d s o", o=1).broadcast_to([128, FC, 4]) for k in range(3)]
            for m in range(3):
                R, I = s4[:, :, m + 1, 0, :], s4[:, :, m + 1, 1, :]
                x = tmp[:, :, m, :]
                t = pool(lambda e: e.tensor_tensor(x, I, cc[1], ALU.mult), tw, pool.last())
                t = pool(lambda e: e.tensor_tensor(a[:, :, m, 0, :], R, cc[0], ALU.mult))
                t = pool(lambda e: e.tensor_tensor(a[:, :, m, 0, :], a[:, :, m, 0, :], x, ALU.add), t)
                t = pool(lambda e: e.tensor_tensor(x, R, cc[1], ALU.mult), t)
                t = pool(lambda e: e.tensor_tensor(a[:, :, m, 1, :], I, cc[2], ALU.mult))
                t = pool(lambda e: e.tensor_tensor(a[:, :, m, 1, :], a[:, :, m, 1, :], x, ALU.subtract), t)
            UL.free[li], TW.free[wi] = t, t
            ready[ch] = (vi, v, tv, ui, u7, t)

        used = [None, None]
        full = [None, None]
        ybank = [None] * 4
        count = [0]

        def filters(ch, par):
            vi, v, tv = ready[ch][0:3]
            ends = [None, None]
            for eg in range(32):
                ti, pt, fr = tiles.take()
                for k in range(4):
                    ec = 4 * eg + k
                    tp = pe(lambda e: e.matmul(pt[:, 128 * k:128 * k + 112],
                                               M[:, par, ec, :],
                                               v[:, par, :], start=True, stop=True), fr, t_m, tv, tick=k == 3)
                src = pt.rearrange("d (e x) -> d x e", x=128)[:, 0:112, :]
                dst = Gm[:, par, :, 4 * eg:4 * eg + 4]
                count[0] += 1
                if count[0] % 2:
                    t = act(lambda e: e.activation(dst, src, ACT.Copy), tp, used[par])
                else:
                    t = dve(lambda e: e.tensor_copy(dst, src), tp, used[par])
                ends[count[0] % 2] = t
                tiles.free[ti] = t
                yield
            full[par] = ends
            if par == 1:
                VS.free[vi] = tp

        def sums(ch, par):
            ui, u7, tu = ready[ch][3:6]
            if par == 1:
                yi, ys, fy = YS.take()
            for gp in range(7):
                bk, cl = gp // 2, 256 * (gp % 2)
                pb = psum[4 + bk]
                wd = 512 if bk < 3 else 256
                if par == 0 and gp % 2 == 0:
                    pe(lambda e: e.matmul(pb[:, 0:wd], zb[:, 0:128], zb[:, 0:wd], start=True, stop=False),
                       ybank[bk], t_zb, tick=False)
                for q in (par, 2 + par):
                    for s in range(4):
                        sl = 4 * gp + s
                        r = ((q // 2) * FC + sl) * 2
                        tp = pe(lambda e: e.matmul(pb[32 * s:32 * s + 32, cl:cl + 256],
                                                   u7[:, sl, 8 * (3 - q):8 * (3 - q) + 32],
                                                   Gm[:, par, r:r + 2, :], start=False, stop=q == 3 and (gp % 2 == 1 or gp == 6),
                                                   tile_position=(0, 32 * s)),
                                tu, *full[par],
                                tick=s == 3)
                    yield
                if par == 1 and (gp % 2 or gp == 6):
                    g0 = gp - gp % 2
                    src = pb[:, 0:256 * (gp - g0 + 1)].rearrange("p (a x) -> p a x", x=256)
                    if bk % 2:
                        ybank[bk] = act(lambda e: e.activation(ys[:, g0:gp + 1, :], src, ACT.Copy), tp, fy)
                    else:
                        ybank[bk] = dve(lambda e: e.tensor_copy(ys[:, g0:gp + 1, :], src), tp, fy)
            used[par] = tp
            if par == 1:
                U7.free[ui] = tp
                for s in range(4):
                    dst = Yd[FC * ch:FC * ch + FC].rearrange("(g s) r x -> s r g x", s=4)[s]
                    t = sp.dma(ly, lambda e: e.dma_start(dst, ys[32 * s:32 * s + 32, :, :]), *ybank)
                YS.free[yi] = t

        def together(gen, mul):
            for i in range(32):
                if gen is not None:
                    next(gen)
                if i % 2 and 2 < i:
                    next(mul, None)
            for g in (gen, mul):
                if g is not None:
                    for _ in g:
                        pass

        load(0)
        for _ in filters(0, 0):
            pass
        for q in (act, dve):
            q.wait(*P["t_u"])
        z = P["zone"]
        IV = z[0:G, 8192:14464].rearrange("p (c a x) -> p c a x", c=2, a=8)
        YL0 = z[0:G, 0:8192].rearrange("p (a q r x) -> p a q r x", a=8, q=2, r=2)
        lf, ll0 = line("lf3"), line("ll")
        for ch in range(NCH):
            if ch == NCH - 1:
                sp.wait(pe.last(), ly.all())
                for a in range(7):
                    load_y(sp, ll0, YL0, Yd, a, 0, 0)
            together(filters(ch, 1), sums(ch, 0))
            if ch == NCH - 1:
                sp.dma(lf, lambda e: e.dma_start(IV, P["c_inv"]), pe.last())
            if ch + 1 < NCH:
                load(ch + 1)
            together(filters(ch + 1, 0) if ch + 1 < NCH else None, sums(ch, 1))
        sp.wait(ly.all())
        load_y(sp, ll0, YL0, Yd, 7, 0, 0)
        P["IV"], P["YL0"], P["ll0"], P["t_iv"] = IV, YL0, ll0, lf.all()
        P["ends_freq"] = [ly]


def load_y(sp, ln, yl, Yd, a, b, pp, *after):
    src = Yd[G * a:G * a + G].rearrange("s (p r b) x -> s b p r x", r=2, b=4)[:, b, 2 * pp:2 * pp + 2]
    return sp.dma(ln, lambda e: e.dma_start(yl[:, a], src), *after)


def phase_inv(P):
    nc, line = P["nc"], P["line"]
    pe, act, dve, pool, sp, psum = P["pe"], P["act"], P["dve"], P["pool"], P["sp"], P["psum"]
    Yd, T2, w = P["Yd"], P["T2"], P["wsel"]
    out = P["out"].rearrange("b h w c -> b (h w c)").rearrange("b (j x) -> b j x", x=512)
    with ExitStack() as c2:
        sb = lambda name, shape, dt=F32: c2.enter_context(nc.sbuf_tensor(name, shape, dt))
        IV, rev = P["IV"], P["rev"]
        YL = Ring([P["YL0"], sb("YL1", [G, 8, 2, 2, 256])])
        YC = Ring([sb(f"YC{i}", [G, 2, 8, 2, 128]) for i in range(2)])
        RN = Ring([sb(f"RN{i}", [G, 2, 4, 256]) for i in range(2)])
        S2 = Ring([sb(f"S2{i}", [G, 256]) for i in range(2)])
        TT = Ring([sb(f"TT{i}", [G, 2, 256]) for i in range(2)])
        tf = P["t_iv"]
        ll, lr, lo = [P["ll0"], line("ll")], [line("lr") for _ in range(2)], [line("lo3") for _ in range(2)]
        bank = Ring(psum)
        work = [(b, pp) for b in range(NB) for pp in range(2)]
        got = {}
        rows = lambda b, k, pp, A: A[b, 392 * k:392 * k + 392, 256 * pp:256 * pp + 256].rearrange("(a p) x -> p a x", p=G)

        def load(n):
            if n >= len(work):
                return
            b, pp = work[n]
            i, yl, fr = YL.take()
            for a in range(8 if n else 0):
                load_y(sp, ll[i], yl, Yd, a, b, pp, fr)
            got[n] = (i, yl, ll[i].all())

        def load_rows(n):
            b, pp = work[n]
            j, rn, fr = RN.take()
            for k in range(2):
                t = sp.dma(lr[j], lambda e: e.dma_start(rn[:, k], rows(b, k, pp, T2)), fr)
            return j, rn, t

        def combine(n):
            i, yl, t = got.pop(n)
            ci, yc, fr = YC.take()
            done = []
            for h in range(2):
                hs = slice(4 * h, 4 * h + 4)
                for k, (op, q) in enumerate(((ALU.subtract, 0), (ALU.add, 128))):
                    ta = dve(lambda e: e.tensor_tensor(yc[:, k, hs], yl[:, hs, :, 0, q:q + 128],
                                                       yl[:, hs, :, 1, 128 - q:256 - q], op), t, fr)
                    if h == 0:
                        ta = dve(lambda e: e.tensor_copy(yc[0:1, k, 0], yl[0:1, 0, :, k, q:q + 128]), ta)
                    if n:
                        yield
                done.append(ta)
            YL.free[i] = ta
            ready[n] = (ci, yc, done)

        ready, held = {}, []

        def turned():
            rn, jt, tt, xi, t3, back = held.pop(0)
            pi, p, fr = bank.take()
            t = pe(lambda e: e.matmul(p[0:G, 0:256], rev[:, :], tt[:, 1], start=True, stop=True), t3, fr)
            TT.free[xi] = t
            t = dve(lambda e: e.scalar_tensor_tensor(rn[:, 1, 3 - jt], p[0:G, 0:256], w[0:G, 15 - jt:16 - jt],
                                                     rn[:, 1, 3 - jt], ALU.mult, ALU.add), t)
            bank.free[pi] = t
            back(t)

        def store(n, j, rn):
            b, pp = work[n]

            def go(t):
                for k in range(2):
                    to = sp.dma(lo[j], lambda e: e.dma_start(rows(b, k, pp, out), rn[:, k]), t)
                RN.free[j] = to
            return go

        load(0)
        load(1)
        got_rows = {0: load_rows(0)}
        for _ in combine(0):
            pass
        for n, (b, pp) in enumerate(work):
            load(n + 2)
            j, rn, t2 = got_rows.pop(n)
            ci, yc, ts = ready.pop(n)
            nxt = combine(n + 1) if n + 1 < len(work) else iter(())
            for jt in range(4):
                pi, p, fr = bank.take()
                for c in range(2):
                    for a in range(8):
                        k = (a >= 4) ^ c
                        tp = pe(lambda e: e.matmul(p[0:G, 256 * c:256 * c + 256], IV[:, c, a, G * jt:G * jt + G],
                                                   yc[:, int(k), a], start=a == 0, stop=a == 7),
                                fr, ts[a // 4], tf, tick=a == 7)
                si, s2, fr = S2.take()
                t = act(lambda e: e.activation(s2[:, :], p[0:G, 256:512], ACT.Copy), tp, fr)
                xi, tt, fr = TT.take()
                t3 = dve(lambda e: e.tensor_tensor(tt[:, 1], p[0:G, 0:256], s2[:, :], ALU.subtract), t, fr)
                t1 = dve(lambda e: e.tensor_tensor(tt[:, 0], p[0:G, 0:256], s2[:, :], ALU.add))
                bank.free[pi], S2.free[si] = t1, t1
                if held:
                    turned()
                dve(lambda e: e.scalar_tensor_tensor(rn[:, 0, jt], tt[:, 0], w[0:G, 8 + jt:9 + jt], rn[:, 0, jt],
                                                     ALU.mult, ALU.add), t1, t2)
                held.append((rn, jt, tt, xi, t3, store(n, j, rn) if jt == 3 else lambda t: None))
                if jt == 0 and n + 1 < len(work):
                    got_rows[n + 1] = load_rows(n + 1)
                next(nxt, None)
            for _ in nxt:
                pass
            YC.free[ci] = tp
        turned()
        sp.wait(*[l.all() for l in lo])


def tables():
    NP_, J = 1568, 784
    even = np.arange(0, 784, 2)
    odd = np.arange(1, 784, 2)
    slots = np.concatenate([even, odd])
    j = np.arange(392)[:, None] + 0.5
    th = lambda a, f: 2 * np.pi * a * f / NP_
    fe, fo = even[None, :].astype(float), odd[None, :].astype(float)
    fi = fe.copy()
    fi[0, 0] = 784.0
    Fe = np.concatenate([np.cos(th(j, fe)), -np.sin(th(j, fo))], 1)
    Fo = np.concatenate([np.cos(th(j, fo)), -np.sin(th(j, fi))], 1)
    fwd = np.stack([Fe, Fo], 0).reshape(2, 4, 98, 784).transpose(2, 0, 1, 3)
    jj = np.arange(784)[:, None].astype(float)
    fs = slots[None, :].astype(float)
    V = np.empty((784, 784, 2))
    V[:, :, 0] = np.cos(th(jj, fs))
    V[:, :, 1] = -np.sin(th(jj, fs))
    V[:, 0, 1] = np.cos(th(jj[:, 0], 784.0))
    vdft = V.reshape(8, 98, 1568).transpose(1, 0, 2)
    tc, ts = np.cos(th(1.0, slots)), np.sin(th(1.0, slots))
    tci = tc.copy()
    tci[0] = -1.0
    tw = np.stack([tc, ts, tci])
    w = np.full(784, 2.0)
    w[0] = 1.0
    jr = np.arange(392)[None, :] + 0.5
    ev, od = slots[:392, None].astype(float), slots[392:, None].astype(float)
    wc = w[:392, None] / NP_
    evi = ev.copy()
    evi[0, 0] = 784.0
    C1 = np.concatenate([wc * np.cos(th(jr, ev)), -2.0 / NP_ * np.sin(th(jr, od))])
    C2 = np.concatenate([-wc * np.sin(th(jr, evi)), 2.0 / NP_ * np.cos(th(jr, od))])
    inv = np.stack([C1, C2], 0).reshape(2, 8, 98, 392).transpose(2, 0, 1, 3)
    f = lambda a: np.ascontiguousarray(a, dtype=np.float32)
    return f(fwd), f(vdft), f(tw), f(inv)


def shape_constants():
    fwd, vdft, tw, inv = tables()
    ar = np.zeros((2, 6, NCH, 2, FC, 2), np.float32)
    ar[:, 0:3, :, 0, :, 0] = 1
    ar[:, 0:3, 0, 0, 0, 1] = 1
    ar[0, 3:6, :, 1, :, 0] = 1
    ar[0, 3:6, 0, 1, 0, 1] = 1
    msk = np.array([[1.0 if J < 8 >> i else 0.0 for J in range(8)] for i in range(4)], np.float32)
    return {"c_id": np.eye(128, dtype=np.float32), "c_fwd": fwd, "c_vdft": vdft, "c_tw": tw, "c_inv": inv,
            "c_ar": ar.reshape(2, 6, NCH, 112), "c_msk": msk, "c_rev": np.eye(G, dtype=np.float32)[::-1]}


_INS = ['x', 'L0_conv_ln1_w', 'L0_conv_ln1_b', 'L0_conv_w_qkv', 'L0_conv_b_qkv', 'L0_conv_rpb', 'L0_conv_w_proj', 'L0_conv_b_proj', 'L0_conv_ln2_w', 'L0_conv_ln2_b', 'L0_conv_w_fc1', 'L0_conv_b_fc1', 'L0_conv_w_fc2', 'L0_conv_b_fc2', 'L1_attn_Wq', 'L1_attn_bq', 'L1_attn_Wk', 'L1_attn_bk', 'L1_attn_Wv', 'L1_attn_bv', 'L1_ffn_sigma', 'L1_ffn_phi', 'L1_ffn_M_u', 'L1_ffn_M_phi_plus', 'L1_ffn_M_phi_minus', 'L1_ffn_log_weights', 'L1_ffn_gumbel']


def kernel(**inputs):
    import numpy as _np
    import concourse.bacc as _bacc
    from concourse import mybir as _mybir
    from concourse.bass_utils import run_bass_kernel_spmd as _run

    nc = _bacc.Bacc("TRN2", target_bir_lowering=False, num_devices=1)
    arrays, args = {}, []
    consts = shape_constants()
    for name, a in [(n, inputs[n]) for n in _INS] + list(consts.items()):
        a = _np.ascontiguousarray(a)
        arrays[f"in_{name}_dram"] = a
        args.append(nc.dram_tensor(f"in_{name}_dram", a.shape, _mybir.dt.from_np(a.dtype), kind="ExternalInput").ap())
    args.append(nc.dram_tensor("out_0_dram", (4, 56, 56, 128), _mybir.dt.float32, kind="ExternalOutput").ap())
    program(nc, *args)
    r = _run(nc, [arrays], core_ids=[0])
    return r.results[0]["out_0_dram"]
```
